# Optimizing a Trainium2 kernel written in Bass

```python
import numpy as np
import jax
import jax.numpy as jnp

def _softmax(x, axis=-1):
    return jax.nn.softmax(x, axis=axis)

def _gelu(x):
    return jax.nn.gelu(x, approximate=True)

def _silu(x):
    return jax.nn.silu(x)

def _sigmoid(x):
    return jax.nn.sigmoid(x)

def _layernorm(x, axis=-1, eps=1e-05):
    m = jnp.mean(x, axis=axis, keepdims=True)
    v = jnp.var(x, axis=axis, keepdims=True)
    return (x - m) / jnp.sqrt(v + eps)

def _scatter_add(tgt, idx, src, axis=0):
    return tgt.at[idx].add(src)

def _segment_sum(src, seg, n):
    return jax.ops.segment_sum(src, seg, n)
kernel_name = 'mk_adaln_d2_jaxref_r8_933be4'

def setup_inputs(seed: int=0):
    np.random.seed(seed)
    _w = jnp.asarray

    def _L0_attn_setup():
        import jax, jax.numpy as jnp
        import numpy as np
        H = 16

        def _split_heads(t):
            B, N, D = t.shape
            return t.reshape(B, N, H, D // H).transpose(0, 2, 1, 3)
        key = jax.random.key(seed)
        ks = jax.random.split(key, 9)
        B, N, D = (4, 512, 128)
        mk = lambda k, shape: jax.random.normal(k, shape, dtype=jnp.float32) * 0.02
        return {'x': jax.random.normal(ks[0], (B, N, D), dtype=jnp.float32), 'Wq': mk(ks[1], (D, D)), 'bq': mk(ks[2], (D,)), 'Wk': mk(ks[3], (D, D)), 'bk': mk(ks[4], (D,)), 'Wv': mk(ks[5], (D, D)), 'bv': mk(ks[6], (D,)), 'Wo': mk(ks[7], (D, D)), 'bo': mk(ks[8], (D,))}
    _L0_attn_in = _L0_attn_setup()

    def _L0_ffn_setup():
        import jax, jax.numpy as jnp
        import numpy as np
        DIM = 128
        INTER = 64
        E = 16
        TOPK = 4
        N_GROUPS = 4
        TOPK_GROUPS = 2
        ROUTE_SCALE = 1.0
        INIT_STD = 0.02
        B, S = (2, 128)
        key = jax.random.key(seed)
        ks = jax.random.split(key, 8)
        return {'x': jax.random.normal(ks[0], (B, S, DIM), jnp.float32), 'gate_w': jax.random.normal(ks[1], (E, DIM), jnp.float32) * INIT_STD, 'gate_bias': jnp.zeros((E,), jnp.float32), 'w1': jax.random.normal(ks[2], (E, INTER, DIM), jnp.float32) * INIT_STD, 'w2': jax.random.normal(ks[3], (E, DIM, INTER), jnp.float32) * INIT_STD, 'w3': jax.random.normal(ks[4], (E, INTER, DIM), jnp.float32) * INIT_STD, 'ws1': jax.random.normal(ks[5], (INTER, DIM), jnp.float32) * INIT_STD, 'ws2': jax.random.normal(ks[6], (DIM, INTER), jnp.float32) * INIT_STD, 'ws3': jax.random.normal(ks[7], (INTER, DIM), jnp.float32) * INIT_STD}
    _L0_ffn_in = _L0_ffn_setup()
    _L0_c = _w((lambda *s: np.random.randn(*s).astype(np.float32) * 0.05)(4, 128))
    _L0_wmod = _w((lambda *s: np.random.randn(*s).astype(np.float32) * 0.05)(128, 6 * 128) * 128 ** (-0.5))

    def _L1_attn_setup():
        import jax, jax.numpy as jnp
        import numpy as np
        D_MODEL = 128
        N_HEADS = 16
        HEAD_DIM = D_MODEL // N_HEADS
        WINDOW = 64
        PREFIX = 16
        B = 2
        S = 512

        def _windowed_global_attention(q, k, v):
            Bb, H, S_, Dh = q.shape
            W, P = (WINDOW, PREFIX)
            C = S_ // W
            scale = 1.0 / np.sqrt(Dh).astype(np.float32)
            qc = q.reshape(Bb, H, C, W, Dh)
            kp = jnp.pad(k, ((0, 0), (0, 0), (W, 0), (0, 0)))
            vp = jnp.pad(v, ((0, 0), (0, 0), (W, 0), (0, 0)))
            tail_idx = jnp.arange(C)[:, None] * W + jnp.arange(2 * W)[None, :]
            kt = kp[:, :, tail_idx, :]
            vt = vp[:, :, tail_idx, :]
            kg = k[:, :, :P, :]
            vg = v[:, :, :P, :]
            sg = jnp.einsum('bhcqd,bhkd->bhcqk', qc, kg) * scale
            st = jnp.einsum('bhcqd,bhckd->bhcqk', qc, kt) * scale
            q_pos = jnp.arange(C)[:, None] * W + jnp.arange(W)[None, :]
            kt_pos = jnp.arange(C)[:, None] * W - W + jnp.arange(2 * W)[None, :]
            mg = jnp.arange(P)[None, None, :] <= q_pos[:, :, None]
            diff = q_pos[:, :, None] - kt_pos[:, None, :]
            mt = (diff >= 0) & (diff < W) & (kt_pos[:, None, :] >= P)
            neg = jnp.asarray(-1000000000.0, sg.dtype)
            scores = jnp.concatenate([jnp.where(mg[None, None], sg, neg), jnp.where(mt[None, None], st, neg)], axis=-1)
            attn = jax.nn.softmax(scores, axis=-1)
            vcat = jnp.concatenate([jnp.broadcast_to(vg[:, :, None], (Bb, H, C, P, Dh)), vt], axis=3)
            out = jnp.einsum('bhcqk,bhckd->bhcqd', attn, vcat)
            return out.reshape(Bb, H, S_, Dh)
        key = jax.random.key(seed)
        k1, k2, k3 = jax.random.split(key, 3)
        x = jax.random.normal(k1, (B, S, D_MODEL), dtype=jnp.float32)
        w_qkv = jax.random.normal(k2, (3 * D_MODEL, D_MODEL), dtype=jnp.float32) * 0.02
        w_out = jax.random.normal(k3, (D_MODEL, D_MODEL), dtype=jnp.float32) * 0.02
        return {'x': x, 'w_qkv': w_qkv, 'w_out': w_out}
    _L1_attn_in = _L1_attn_setup()

    def _L1_ffn_setup():
        import jax, jax.numpy as jnp
        import numpy as np
        DIM = 128
        DEPTH = 2
        HEADS = 8
        DIM_HEAD = 64
        WINDOW = 64
        INNER = HEADS * DIM_HEAD
        HID = int(DIM * 4 * 2 / 3)
        B, N = (2, 1024)
        QK_SCALE = 8.0

        def shift_token(t):
            t1, t2 = jnp.split(t, 2, axis=-1)
            t2 = jnp.pad(t2, ((0, 0), (1, 0), (0, 0)))[:, :-1]
            return jnp.concatenate([t1, t2], axis=-1)

        def l2norm(t):
            return t / jnp.clip(jnp.linalg.norm(t, axis=-1, keepdims=True), 1e-12)

        def rotate_half(x):
            x1, x2 = jnp.split(x, 2, axis=-1)
            return jnp.concatenate([-x2, x1], axis=-1)

        def rotary_xpos(q, k):
            n = q.shape[-2]
            half_idx = jnp.arange(0, DIM_HEAD, 2, dtype=jnp.float32)
            inv_freq = 1.0 / 10000.0 ** (half_idx / DIM_HEAD)
            t = jnp.arange(n, dtype=jnp.float32)
            freqs = t[:, None] * inv_freq[None, :]
            freqs = jnp.concatenate([freqs, freqs], axis=-1)
            base = (half_idx + 0.4 * DIM_HEAD) / (1.4 * DIM_HEAD)
            power = (t - n // 2) / float(WINDOW // 2)
            scale = base[None, :] ** power[:, None]
            scale = jnp.concatenate([scale, scale], axis=-1)
            cos, sin = (jnp.cos(freqs), jnp.sin(freqs))
            q = q * cos * scale + rotate_half(q) * sin * scale
            k = k * cos / scale + rotate_half(k) * sin / scale
            return (q, k)

        def local_attention(q, k, v):
            b, h, n, d = q.shape
            w = n // WINDOW
            bq = q.reshape(b, h, w, WINDOW, d) * QK_SCALE
            bk = k.reshape(b, h, w, WINDOW, d)
            bv = v.reshape(b, h, w, WINDOW, d)

            def look_around(t):
                p = jnp.pad(t, ((0, 0), (0, 0), (1, 0), (0, 0), (0, 0)))
                return jnp.concatenate([p[:, :, :w], p[:, :, 1:]], axis=3)
            bk, bv = (look_around(bk), look_around(bv))
            bt = jnp.arange(n).reshape(w, WINDOW)
            btp = jnp.pad(bt, ((1, 0), (0, 0)), constant_values=-1)
            btk = jnp.concatenate([btp[:w], btp[1:]], axis=1)
            sim = jnp.einsum('bhwid,bhwjd->bhwij', bq, bk)
            i = bt[:, :, None]
            j = btk[:, None, :]
            mask = (i < j) | (i > j + WINDOW) | (j == -1)
            sim = jnp.where(mask, -jnp.finfo(sim.dtype).max, sim)
            attn = jax.nn.softmax(sim, axis=-1)
            out = jnp.einsum('bhwij,bhwjd->bhwid', attn, bv)
            return out.reshape(b, h, n, d)

        def _layer(x, wqkv, qs, ksc, wo, lg, lb, w1, b1, w2, b2):
            b, n, _ = x.shape
            h = shift_token(x)
            qkv = h @ wqkv
            q, k, v = jnp.split(qkv, 3, axis=-1)
            to_heads = lambda t: t.reshape(b, n, HEADS, DIM_HEAD).transpose(0, 2, 1, 3)
            q, k, v = (to_heads(q), to_heads(k), to_heads(v))
            q = l2norm(q) * qs
            k = l2norm(k) * ksc
            q, k = rotary_xpos(q, k)
            o = local_attention(q, k, v)
            o = o.transpose(0, 2, 1, 3).reshape(b, n, INNER)
            x = x + o @ wo
            h = shift_token(x)
            mu = h.mean(-1, keepdims=True)
            var = h.var(-1, keepdims=True)
            h = (h - mu) / jnp.sqrt(var + 1e-05) * lg + lb
            h = h @ w1 + b1
            a, g = jnp.split(h, 2, axis=-1)
            h = a * jax.nn.gelu(g, approximate=False)
            x = x + h @ w2 + b2
            return x
        key = jax.random.key(seed)
        ks = jax.random.split(key, 6)
        return {'x': jax.random.normal(ks[0], (B, N, DIM), jnp.float32), 'wqkv': jax.random.normal(ks[1], (DEPTH, DIM, 3 * INNER), jnp.float32) * 0.02, 'q_scale': jnp.ones((DEPTH, DIM_HEAD), jnp.float32), 'k_scale': jnp.ones((DEPTH, DIM_HEAD), jnp.float32), 'wo': jax.random.normal(ks[2], (DEPTH, INNER, DIM), jnp.float32) * 0.02, 'ln_g': jnp.ones((DEPTH, DIM), jnp.float32), 'ln_b': jnp.zeros((DEPTH, DIM), jnp.float32), 'w1': jax.random.normal(ks[3], (DEPTH, DIM, 2 * HID), jnp.float32) * 0.02, 'b1': jnp.zeros((DEPTH, 2 * HID), jnp.float32), 'w2': jax.random.normal(ks[4], (DEPTH, HID, DIM), jnp.float32) * 0.02, 'b2': jnp.zeros((DEPTH, DIM), jnp.float32)}
    _L1_ffn_in = _L1_ffn_setup()
    _L1_c = _w((lambda *s: np.random.randn(*s).astype(np.float32) * 0.05)(4, 128))
    _L1_wmod = _w((lambda *s: np.random.randn(*s).astype(np.float32) * 0.05)(128, 6 * 128) * 128 ** (-0.5))
    _d = {'L0_attn_x': _L0_attn_in['x'], 'L0_attn_Wq': _L0_attn_in['Wq'], 'L0_attn_bq': _L0_attn_in['bq'], 'L0_attn_Wk': _L0_attn_in['Wk'], 'L0_attn_bk': _L0_attn_in['bk'], 'L0_attn_Wv': _L0_attn_in['Wv'], 'L0_attn_bv': _L0_attn_in['bv'], 'L0_attn_Wo': _L0_attn_in['Wo'], 'L0_attn_bo': _L0_attn_in['bo'], 'L0_ffn_gate_w': _L0_ffn_in['gate_w'], 'L0_ffn_gate_bias': _L0_ffn_in['gate_bias'], 'L0_ffn_w1': _L0_ffn_in['w1'], 'L0_ffn_w2': _L0_ffn_in['w2'], 'L0_ffn_w3': _L0_ffn_in['w3'], 'L0_ffn_ws1': _L0_ffn_in['ws1'], 'L0_ffn_ws2': _L0_ffn_in['ws2'], 'L0_ffn_ws3': _L0_ffn_in['ws3'], 'L0_c': _L0_c, 'L0_wmod': _L0_wmod, 'L1_attn_w_qkv': _L1_attn_in['w_qkv'], 'L1_attn_w_out': _L1_attn_in['w_out'], 'L1_ffn_wqkv': _L1_ffn_in['wqkv'], 'L1_ffn_q_scale': _L1_ffn_in['q_scale'], 'L1_ffn_k_scale': _L1_ffn_in['k_scale'], 'L1_ffn_wo': _L1_ffn_in['wo'], 'L1_ffn_ln_g': _L1_ffn_in['ln_g'], 'L1_ffn_ln_b': _L1_ffn_in['ln_b'], 'L1_ffn_w1': _L1_ffn_in['w1'], 'L1_ffn_b1': _L1_ffn_in['b1'], 'L1_ffn_w2': _L1_ffn_in['w2'], 'L1_ffn_b2': _L1_ffn_in['b2'], 'L1_c': _L1_c, 'L1_wmod': _L1_wmod}
    _x0 = _d['L0_attn_x']
    _d['L0_attn_x'] = jax.random.normal(jax.random.fold_in(jax.random.key(seed), 1), (4, 1024, 128), dtype=_x0.dtype)
    del _x0
    return _d

def reference(L0_attn_x, L0_attn_Wq, L0_attn_bq, L0_attn_Wk, L0_attn_bk, L0_attn_Wv, L0_attn_bv, L0_attn_Wo, L0_attn_bo, L0_ffn_gate_w, L0_ffn_gate_bias, L0_ffn_w1, L0_ffn_w2, L0_ffn_w3, L0_ffn_ws1, L0_ffn_ws2, L0_ffn_ws3, L0_c, L0_wmod, L1_attn_w_qkv, L1_attn_w_out, L1_ffn_wqkv, L1_ffn_q_scale, L1_ffn_k_scale, L1_ffn_wo, L1_ffn_ln_g, L1_ffn_ln_b, L1_ffn_w1, L1_ffn_b1, L1_ffn_w2, L1_ffn_b2, L1_c, L1_wmod):

    def _L0_attn_ref(x, Wq, bq, Wk, bk, Wv, bv, Wo, bo):
        import jax, jax.numpy as jnp
        import numpy as np
        H = 16

        def _split_heads(t):
            B, N, D = t.shape
            return t.reshape(B, N, H, D // H).transpose(0, 2, 1, 3)
        B, N, D = x.shape
        d_head = D // H
        s = (d_head ** 0.5) ** (-0.25)
        q = _split_heads(x @ Wq + bq)
        _ = x @ Wk + bk
        v = _split_heads(x @ Wv + bv)
        q = jax.nn.softmax(q, axis=-1) * s
        k = jax.nn.softmax(q, axis=-2) * s
        ctx = jnp.einsum('bhnd,bhne->bhde', k, v)
        attn = jnp.einsum('bhnd,bhde->bhne', q, ctx)
        attn = attn.transpose(0, 2, 1, 3).reshape(B, N, D)
        return attn @ Wo + bo

    def _L0_ffn_ref(x, gate_w, gate_bias, w1, w2, w3, ws1, ws2, ws3):
        import jax, jax.numpy as jnp
        import numpy as np
        DIM = 128
        INTER = 64
        E = 16
        TOPK = 4
        N_GROUPS = 4
        TOPK_GROUPS = 2
        ROUTE_SCALE = 1.0
        INIT_STD = 0.02
        B, S = (2, 128)
        Bx, Sx, D = x.shape
        T = Bx * Sx
        xf = x.reshape(T, D)
        scores = jax.nn.sigmoid(xf @ gate_w.T)
        original_scores = scores
        s = scores + gate_bias
        sg = s.reshape(T, N_GROUPS, E // N_GROUPS)
        group_scores = sg.max(axis=-1)
        _, gidx = jax.lax.top_k(group_scores, TOPK_GROUPS)
        keep = jnp.zeros((T, N_GROUPS), bool).at[jnp.arange(T)[:, None], gidx].set(True)
        s_masked = jnp.where(keep[:, :, None], sg, -jnp.inf).reshape(T, E)
        _, idx = jax.lax.top_k(s_masked, TOPK)
        weights = jnp.take_along_axis(original_scores, idx, axis=1) * ROUTE_SCALE
        comb = jnp.zeros((T, E), x.dtype).at[jnp.arange(T)[:, None], idx].add(weights)
        h1 = jnp.einsum('td,eid->tei', xf, w1)
        h3 = jnp.einsum('td,eid->tei', xf, w3)
        h = jax.nn.silu(h1) * h3
        y = jnp.einsum('tei,edi,te->td', h, w2, comb)
        z = jax.nn.silu(xf @ ws1.T) * (xf @ ws3.T) @ ws2.T
        return (y + z).reshape(Bx, Sx, D)

    def _L1_attn_ref(x, w_qkv, w_out):
        import jax, jax.numpy as jnp
        import numpy as np
        D_MODEL = 128
        N_HEADS = 16
        HEAD_DIM = D_MODEL // N_HEADS
        WINDOW = 64
        PREFIX = 16
        B = 2
        S = 512

        def _windowed_global_attention(q, k, v):
            Bb, H, S_, Dh = q.shape
            W, P = (WINDOW, PREFIX)
            C = S_ // W
            scale = 1.0 / np.sqrt(Dh).astype(np.float32)
            qc = q.reshape(Bb, H, C, W, Dh)
            kp = jnp.pad(k, ((0, 0), (0, 0), (W, 0), (0, 0)))
            vp = jnp.pad(v, ((0, 0), (0, 0), (W, 0), (0, 0)))
            tail_idx = jnp.arange(C)[:, None] * W + jnp.arange(2 * W)[None, :]
            kt = kp[:, :, tail_idx, :]
            vt = vp[:, :, tail_idx, :]
            kg = k[:, :, :P, :]
            vg = v[:, :, :P, :]
            sg = jnp.einsum('bhcqd,bhkd->bhcqk', qc, kg) * scale
            st = jnp.einsum('bhcqd,bhckd->bhcqk', qc, kt) * scale
            q_pos = jnp.arange(C)[:, None] * W + jnp.arange(W)[None, :]
            kt_pos = jnp.arange(C)[:, None] * W - W + jnp.arange(2 * W)[None, :]
            mg = jnp.arange(P)[None, None, :] <= q_pos[:, :, None]
            diff = q_pos[:, :, None] - kt_pos[:, None, :]
            mt = (diff >= 0) & (diff < W) & (kt_pos[:, None, :] >= P)
            neg = jnp.asarray(-1000000000.0, sg.dtype)
            scores = jnp.concatenate([jnp.where(mg[None, None], sg, neg), jnp.where(mt[None, None], st, neg)], axis=-1)
            attn = jax.nn.softmax(scores, axis=-1)
            vcat = jnp.concatenate([jnp.broadcast_to(vg[:, :, None], (Bb, H, C, P, Dh)), vt], axis=3)
            out = jnp.einsum('bhcqk,bhckd->bhcqd', attn, vcat)
            return out.reshape(Bb, H, S_, Dh)
        Bb, S_, Dm = x.shape
        qkv = x @ w_qkv.T
        q, k, v = jnp.split(qkv, 3, axis=-1)

        def heads(t):
            return t.reshape(Bb, S_, N_HEADS, HEAD_DIM).transpose(0, 2, 1, 3)
        q, k, v = (heads(q), heads(k), heads(v))
        o = _windowed_global_attention(q, k, v)
        o = o.transpose(0, 2, 1, 3).reshape(Bb, S_, Dm)
        return o @ w_out.T

    def _L1_ffn_ref(x, wqkv, q_scale, k_scale, wo, ln_g, ln_b, w1, b1, w2, b2):
        import jax, jax.numpy as jnp
        import numpy as np
        DIM = 128
        DEPTH = 2
        HEADS = 8
        DIM_HEAD = 64
        WINDOW = 64
        INNER = HEADS * DIM_HEAD
        HID = int(DIM * 4 * 2 / 3)
        B, N = (2, 1024)
        QK_SCALE = 8.0

        def shift_token(t):
            t1, t2 = jnp.split(t, 2, axis=-1)
            t2 = jnp.pad(t2, ((0, 0), (1, 0), (0, 0)))[:, :-1]
            return jnp.concatenate([t1, t2], axis=-1)

        def l2norm(t):
            return t / jnp.clip(jnp.linalg.norm(t, axis=-1, keepdims=True), 1e-12)

        def rotate_half(x):
            x1, x2 = jnp.split(x, 2, axis=-1)
            return jnp.concatenate([-x2, x1], axis=-1)

        def rotary_xpos(q, k):
            n = q.shape[-2]
            half_idx = jnp.arange(0, DIM_HEAD, 2, dtype=jnp.float32)
            inv_freq = 1.0 / 10000.0 ** (half_idx / DIM_HEAD)
            t = jnp.arange(n, dtype=jnp.float32)
            freqs = t[:, None] * inv_freq[None, :]
            freqs = jnp.concatenate([freqs, freqs], axis=-1)
            base = (half_idx + 0.4 * DIM_HEAD) / (1.4 * DIM_HEAD)
            power = (t - n // 2) / float(WINDOW // 2)
            scale = base[None, :] ** power[:, None]
            scale = jnp.concatenate([scale, scale], axis=-1)
            cos, sin = (jnp.cos(freqs), jnp.sin(freqs))
            q = q * cos * scale + rotate_half(q) * sin * scale
            k = k * cos / scale + rotate_half(k) * sin / scale
            return (q, k)

        def local_attention(q, k, v):
            b, h, n, d = q.shape
            w = n // WINDOW
            bq = q.reshape(b, h, w, WINDOW, d) * QK_SCALE
            bk = k.reshape(b, h, w, WINDOW, d)
            bv = v.reshape(b, h, w, WINDOW, d)

            def look_around(t):
                p = jnp.pad(t, ((0, 0), (0, 0), (1, 0), (0, 0), (0, 0)))
                return jnp.concatenate([p[:, :, :w], p[:, :, 1:]], axis=3)
            bk, bv = (look_around(bk), look_around(bv))
            bt = jnp.arange(n).reshape(w, WINDOW)
            btp = jnp.pad(bt, ((1, 0), (0, 0)), constant_values=-1)
            btk = jnp.concatenate([btp[:w], btp[1:]], axis=1)
            sim = jnp.einsum('bhwid,bhwjd->bhwij', bq, bk)
            i = bt[:, :, None]
            j = btk[:, None, :]
            mask = (i < j) | (i > j + WINDOW) | (j == -1)
            sim = jnp.where(mask, -jnp.finfo(sim.dtype).max, sim)
            attn = jax.nn.softmax(sim, axis=-1)
            out = jnp.einsum('bhwij,bhwjd->bhwid', attn, bv)
            return out.reshape(b, h, n, d)

        def _layer(x, wqkv, qs, ksc, wo, lg, lb, w1, b1, w2, b2):
            b, n, _ = x.shape
            h = shift_token(x)
            qkv = h @ wqkv
            q, k, v = jnp.split(qkv, 3, axis=-1)
            to_heads = lambda t: t.reshape(b, n, HEADS, DIM_HEAD).transpose(0, 2, 1, 3)
            q, k, v = (to_heads(q), to_heads(k), to_heads(v))
            q = l2norm(q) * qs
            k = l2norm(k) * ksc
            q, k = rotary_xpos(q, k)
            o = local_attention(q, k, v)
            o = o.transpose(0, 2, 1, 3).reshape(b, n, INNER)
            x = x + o @ wo
            h = shift_token(x)
            mu = h.mean(-1, keepdims=True)
            var = h.var(-1, keepdims=True)
            h = (h - mu) / jnp.sqrt(var + 1e-05) * lg + lb
            h = h @ w1 + b1
            a, g = jnp.split(h, 2, axis=-1)
            h = a * jax.nn.gelu(g, approximate=False)
            x = x + h @ w2 + b2
            return x
        for l in range(DEPTH):
            x = _layer(x, wqkv[l], q_scale[l], k_scale[l], wo[l], ln_g[l], ln_b[l], w1[l], b1[l], w2[l], b2[l])
        return x
    x = L0_attn_x
    mod = (_silu(L0_c) @ L0_wmod).reshape(L0_c.shape[0], 6, 1, -1)
    sa, ca, ga, sb, cb, gb = (mod[:, 0], mod[:, 1], mod[:, 2], mod[:, 3], mod[:, 4], mod[:, 5])
    ga = (2 * (ga >= 0) - 1) * jnp.maximum(jnp.abs(ga), 0.25)
    gb = (2 * (gb >= 0) - 1) * jnp.maximum(jnp.abs(gb), 0.25)
    h = _layernorm(x, axis=-1) * (1 + ca) + sa
    x = x + ga * _L0_attn_ref(h, L0_attn_Wq, L0_attn_bq, L0_attn_Wk, L0_attn_bk, L0_attn_Wv, L0_attn_bv, L0_attn_Wo, L0_attn_bo)
    h = _layernorm(x, axis=-1) * (1 + cb) + sb
    x = x + gb * _L0_ffn_ref(h, L0_ffn_gate_w, L0_ffn_gate_bias, L0_ffn_w1, L0_ffn_w2, L0_ffn_w3, L0_ffn_ws1, L0_ffn_ws2, L0_ffn_ws3)
    mod = (_silu(L1_c) @ L1_wmod).reshape(L1_c.shape[0], 6, 1, -1)
    sa, ca, ga, sb, cb, gb = (mod[:, 0], mod[:, 1], mod[:, 2], mod[:, 3], mod[:, 4], mod[:, 5])
    ga = (2 * (ga >= 0) - 1) * jnp.maximum(jnp.abs(ga), 0.25)
    gb = (2 * (gb >= 0) - 1) * jnp.maximum(jnp.abs(gb), 0.25)
    h = _layernorm(x, axis=-1) * (1 + ca) + sa
    x = x + ga * _L1_attn_ref(h, L1_attn_w_qkv, L1_attn_w_out)
    h = _layernorm(x, axis=-1) * (1 + cb) + sb
    x = x + gb * _L1_ffn_ref(h, L1_ffn_wqkv, L1_ffn_q_scale, L1_ffn_k_scale, L1_ffn_wo, L1_ffn_ln_g, L1_ffn_ln_b, L1_ffn_w1, L1_ffn_b1, L1_ffn_w2, L1_ffn_b2)
    return x

_drawn_inputs = setup_inputs


def setup_inputs(seed=0):
    import zlib

    import numpy as np

    out = dict(_drawn_inputs(seed))
    spreads = {'L0_ffn_gate_bias': (0.0, 0.8),
     'L1_ffn_q_scale': (1.0, 0.6),
     'L1_ffn_k_scale': (1.0, 0.6),
     'L1_ffn_ln_g': (1.0, 0.6),
     'L1_ffn_ln_b': (0.0, 0.8),
     'L1_ffn_b1': (0.0, 0.8),
     'L1_ffn_b2': (0.0, 0.8)}
    factors = {'L0_attn_Wq': 8.0,
     'L0_attn_bq': 8.0,
     'L0_attn_Wv': 8.0,
     'L0_attn_bv': 8.0,
     'L0_attn_Wo': 8.0,
     'L0_attn_bo': 8.0,
     'L0_ffn_gate_w': 8.0,
     'L0_ffn_w1': 8.0,
     'L0_ffn_w2': 8.0,
     'L0_ffn_w3': 8.0,
     'L0_ffn_ws1': 8.0,
     'L0_ffn_ws2': 8.0,
     'L0_ffn_ws3': 8.0,
     'L0_c': 8.0,
     'L0_wmod': 8.0,
     'L1_attn_w_qkv': 8.0,
     'L1_attn_w_out': 8.0,
     'L1_ffn_wqkv': 7.954,
     'L1_ffn_wo': 7.962,
     'L1_ffn_w1': 8.0,
     'L1_ffn_w2': 8.0}
    for name, (base, spread) in spreads.items():
        noise = np.random.default_rng([zlib.crc32(name.encode()), seed]).standard_normal(out[name].shape)
        drawn = base * np.exp(spread * noise) if base else spread * noise
        out[name] = jnp.asarray(drawn.astype(out[name].dtype))
    for name, factor in factors.items():
        out[name] = (out[name] * factor).astype(out[name].dtype)
    return out
```

```python
from contextlib import ExitStack

import numpy as np
import concourse.bass as bass
from concourse import mybir

F32 = mybir.dt.float32
BF16 = mybir.dt.bfloat16
ALU = mybir.AluOpType
ACT = mybir.ActivationFunctionType
AX = mybir.AxisListType

P = 128
B, S, D = 4, 1024, 128
TB = S // P
NT = B * TB
G4 = 4
GT = G4 * P
EPS = 1e-5
STREAMS = (0, 1)
NEG = -1e30

H0, DH0 = 16, 8
S0 = float((DH0 ** 0.5) ** -0.25)
E, INTER, TOPK, NG, TOPG = 16, 64, 4, 4, 2
EG = E // NG
NJ = E * INTER // P
H1, DH1, W1, PRE = 16, 8, 64, 16
KEYS1 = W1 + PRE + P
KB1 = W1 + PRE
DEPTH, H2, DH2, W2 = 2, 8, 64, 64
INNER = H2 * DH2
KEYS2 = W2 + P
HID = int(D * 4 * 2 / 3)
HC = -(-HID // P)


class Signal:

    def __init__(self, sem, base=0):
        self.sem, self.base = sem, base

    def at(self, n):
        return self.base + n


class Chain:

    def __init__(self, eng, signal, start):
        self.eng, self.counter, self.start, self.k = eng, signal, start, 0

    def __call__(self, ins):
        self.k += 1
        ins.then_inc(self.counter.sem, 1)
        self.eng.wait_ge(self.counter.sem, self.counter.base + self.start + self.k)


def bc(ap, axis, n):
    a = ap.unsqueeze(axis)
    shape = list(a.shape)
    shape[axis] = n
    return a.broadcast_to(shape)


class Core:

    L0GA, L0GB, L1GA, L1SB, L1CB, L1GB = range(6)

    def __init__(self, nc, ctx):
        self.nc, self.ctx = nc, ctx
        sb = self.sb
        self.X = sb("X", [P, NT, D])
        self.ident = sb("ident", [P, P])
        self.identb = sb("identb", [P, P], BF16)
        self.neghalf = sb("neghalf", [P, 2 * H2])
        self.epsv = sb("epsv", [P, G4])
        self.carrier = sb("carrier", [P, 1])
        self.modc = sb("modc", [P, 2, 2])
        self.modT = sb("modT", [P, 2, 6, B])
        self.gbT = sb("gbT", [P, B])
        self.rowB = sb("rowB", [P, 6, B, D])
        self.PS = ctx.enter_context(nc.psum_tensor("PS", [P, 8, 512], F32))
        self.z_attn = nc.dram_tensor("z_attn", [B, S + 1, D], F32, kind="Internal").ap()
        self.z_ffn = nc.dram_tensor("z_ffn", [B, S + 1, D], F32, kind="Internal").ap()

        signal = self.counter
        self.dve_step, self.act_step, self.pool_step = signal("dve_step"), signal("act_step"), signal("pool_step")
        self.stats_ready, self.rstd_ready = signal("stats_ready"), signal("rstd_ready")
        self.xn_ready, self.xnT_ready, self.hT_ready = signal("xn_ready"), signal("xnT_ready"), signal("hT_ready")
        self.resid_done = signal("resid_done")

        self.stat6 = sb("stat6", [P, 2, G4, 6])
        self.meanvar = sb("meanvar", [P, 2, G4, 2])
        self.vareps = sb("vareps", [P, 2, G4])
        self.rstd = sb("rstd", [P, 2, G4])
        self.xn = sb("xn", [P, 2, G4, D])
        self.hT = sb("hT", [P, 2, GT])

    def sb(self, name, shape, dt=F32, ctx=None):
        return (ctx or self.ctx).enter_context(self.nc.sbuf_tensor(name, shape, dt))

    def counter(self, name, base=0):
        return Signal(self.ctx.enter_context(self.nc.semaphore(name)), base)

    def bank(self, st, k, n=1):
        if n == 1:
            return self.PS[:, 4 * st + k, :]
        return self.PS[:, 4 * st + k:4 * st + k + n, :]

    def ln_stats(self, dve, chain, tiles):
        for st in STREAMS:
            for i, tile in enumerate(tiles[st]):
                last = dve.bn_stats(self.stat6[:, st, i, :], tile)
        chain(last)
        dve.memset(self.carrier[:, :], 0.0)
        for st in STREAMS:
            for i, tile in enumerate(tiles[st]):
                last = dve.bn_aggr(self.meanvar[:, st, i, :], self.stat6[:, st, i, :])
            last.then_inc(self.stats_ready.sem, 1)

    def ln_rstd(self, pool, chain, u, n):
        for st in STREAMS:
            pool.wait_ge(self.stats_ready.sem, self.stats_ready.at(u + st + 1))
            chain(pool.tensor_tensor(self.vareps[:, st, 0:n], self.meanvar[:, st, 0:n, 1], self.epsv[:, 0:n], ALU.add))
            pool.tensor_tensor(self.rstd[:, st, 0:n], self.vareps[:, st, 0:n], self.neghalf[:, 0:n],
                               ALU.pow).then_inc(self.rstd_ready.sem, 1)

    def ln_apply(self, dve, u, tiles):
        for st in STREAMS:
            dve.wait_ge(self.rstd_ready.sem, self.rstd_ready.at(u + st + 1))
            for i, tile in enumerate(tiles[st]):
                last = dve.tensor_scalar(self.xn[:, st, i, :], tile, self.meanvar[:, st, i, 0:1],
                                         self.rstd[:, st, i:i + 1], ALU.subtract, ALU.mult)
            last.then_inc(self.xn_ready.sem, 1)

    def ln_transpose(self, pe, u, n, resid=None):
        for st in STREAMS:
            if resid is not None:
                pe.wait_ge(self.resid_done.sem, self.resid_done.at(resid + st))
            pe.wait_ge(self.xn_ready.sem, self.xn_ready.at(u + st + 1))
            for i in range(n):
                last = pe.transpose(self.bank(st, 0)[:, i * P:(i + 1) * P], self.xn[:, st, i, :], self.ident[:, :])
            last.then_inc(self.xnT_ready.sem, 1)

    def mod_of_batch(self, act, turn, l, k, batches, units=None):
        if units is not None:
            act.wait_ge(self.hT_ready.sem, self.hT_ready.at(units))
        for st in STREAMS:
            last = act.activation(self.modc[:, st, :], self.modT[:, l, k:k + 2, batches[st]], ACT.Copy)
        last.then_inc(self.act_step.sem, 1)
        act.wait_ge(self.act_step.sem, self.act_step.at(turn + 1))

    def ln_advance(self, units):
        for s in (self.stats_ready, self.rstd_ready, self.xn_ready, self.xnT_ready, self.hT_ready):
            s.base += units


def setup(c, A):
    nc, X, PS, bank, ident, identb, signal = c.nc, c.X, c.PS, c.bank, c.ident, c.identb, c.counter
    with ExitStack() as sc:
        def ssb(name, shape, dt=F32):
            return sc.enter_context(nc.sbuf_tensor(name, shape, dt))

        cT = ssb("cT", [P, 2, B])
        cs = ssb("cs", [P, 2, B])
        csB = ssb("csB", [P, 2, B, P])
        wmod = ssb("wmod", [P, 2, 6 * D])
        sgn = ssb("sgn", [P, 4, B, D])
        zrow = ssb("zrow", [B, D])
        gb_abs = ssb("gb_abs", [P, B])
        mod_done = signal("mod_done")
        zero_stored = signal("zero_stored")
        loaded = signal("loaded")
        with nc.Block() as block:

            @block.sync
            def _(sp):
                n = 0
                for dst, src in ((ident[:, :], A["c_ident"]), (cT[:, 0, :], A["L0_cT"]), (cT[:, 1, :], A["L1_cT"]),
                                 (wmod[:, 0, :], A["L0_wmod"]), (wmod[:, 1, :], A["L1_wmod"])):
                    sp.dma_start(dst, src).then_inc(loaded.sem, 16)
                    n += 16
                for b in range(B):
                    sp.dma_start(X[:, TB * b:TB * (b + 1), :],
                                 A["L0_attn_x"][b].rearrange("(t p) d -> p t d", p=P)).then_inc(loaded.sem, 16)
                    n += 16
                sp.wait_ge(c.dve_step.sem, 1)
                for z in (c.z_attn, c.z_ffn):
                    sp.dma_start(z[:, 0, :], zrow[:, :]).then_inc(zero_stored.sem, 16)
                sp.wait_ge(zero_stored.sem, 32)

            @block.scalar
            def _(act):
                act.wait_ge(loaded.sem, 16 * 9)
                act.activation(cs[:, :, :], cT[:, :, :], ACT.Silu).then_inc(c.act_step.sem, 1)
                act.wait_ge(mod_done.sem, 1)
                act.wait_ge(c.dve_step.sem, 3)
                for l in range(2):
                    for k in range(6):
                        c0 = 256 + (6 * l + k) * B
                        last = act.activation(c.modT[:, l, k, :], PS[:, 4, c0:c0 + B], ACT.Copy,
                                              bias=float(k in (1, 4)))
                last.then_inc(c.act_step.sem, 1)

            @block.vector
            def _(dve):
                dve.memset(zrow[:, :], 0.0).then_inc(c.dve_step.sem, 1)
                dve.memset(c.neghalf[:, :], -0.5)
                dve.memset(c.epsv[:, :], EPS)
                dve.wait_ge(c.act_step.sem, 1)
                dve.tensor_copy(csB[:, :, :, :].rearrange("p a b c -> p (a b) c"),
                                bc(cs[:, :, :].rearrange("p a b -> p (a b)"), 2, P)).then_inc(c.dve_step.sem, 1)
                dve.tensor_copy(identb[:, :], ident[:, :])
                dve.wait_ge(mod_done.sem, 1)
                for b in range(B):
                    dve.tensor_copy(c.rowB[:, 2:6, b, :],
                                    PS[:, b, :].rearrange("p (k d) -> p k d", d=D))
                    last = dve.tensor_copy(c.rowB[:, 0:2, b, :],
                                           PS[:, 4 + b, 0:256].rearrange("p (k d) -> p k d", d=D))
                chain = Chain(dve, c.dve_step, 2)
                chain(last)
                gates = (0, 1, 2, 5)
                for i, k in enumerate(gates):
                    last = dve.tensor_scalar(sgn[:, i, :, :], c.rowB[:, k, :, :], 0.0, 2.0, ALU.is_ge, ALU.mult)
                chain(last)
                last = dve.tensor_scalar(sgn[:, :, :, :], sgn[:, :, :, :], 1.0, None, ALU.subtract)
                chain(last)
                for i, k in enumerate(gates):
                    last = dve.tensor_tensor(c.rowB[:, k, :, :], c.rowB[:, k, :, :], sgn[:, i, :, :], ALU.mult)
                chain(last)
                for i, k in enumerate(gates):
                    last = dve.scalar_tensor_tensor(c.rowB[:, k, :, :].rearrange("p a b -> p (a b)"),
                                                    c.rowB[:, k, :, :].rearrange("p a b -> p (a b)"), 0.25,
                                                    sgn[:, i, :, :].rearrange("p a b -> p (a b)"),
                                                    ALU.max, ALU.mult)
                dve.tensor_scalar(c.rowB[:, 4, :, :], c.rowB[:, 4, :, :], 1.0, None, ALU.add)
                dve.wait_ge(c.act_step.sem, 2)
                chain(dve.tensor_scalar(c.gbT[:, :], c.modT[:, 0, 5, :], 0.0, 2.0, ALU.is_ge, ALU.mult))
                chain(dve.tensor_scalar(c.gbT[:, :], c.gbT[:, :], 1.0, None, ALU.subtract))
                chain(dve.tensor_tensor(gb_abs[:, :], c.gbT[:, :], c.modT[:, 0, 5, :], ALU.mult))
                dve.scalar_tensor_tensor(c.gbT[:, :], gb_abs[:, :], 0.25, c.gbT[:, :], ALU.max, ALU.mult)

            @block.tensor
            def _(pe):
                pe.wait_ge(c.dve_step.sem, 2)
                for b in range(B):
                    pe.matmul(PS[:, b, :], csB[:, 1, b, :], wmod[:, 1, 2 * D:6 * D], start=True, stop=True)
                    pe.matmul(PS[:, 4 + b, 0:D], csB[:, 0, b, :], wmod[:, 0, 2 * D:3 * D], start=True, stop=True)
                    pe.matmul(PS[:, 4 + b, D:2 * D], csB[:, 0, b, :], wmod[:, 0, 5 * D:6 * D], start=True, stop=True)
                for l in range(2):
                    for k in range(6):
                        c0 = 256 + (6 * l + k) * B
                        last = pe.matmul(PS[:, 4, c0:c0 + B], wmod[:, l, k * D:(k + 1) * D], cs[:, l, :],
                                         start=True, stop=True)
                last.then_inc(mod_done.sem, 1)
            c.act_step.base += 2
        c.dve_step.base += 9

def linear_attention(c, A):
    nc, X, PS, bank, ident, identb, signal = c.nc, c.X, c.PS, c.bank, c.ident, c.identb, c.counter
    with ExitStack() as sc:
        def ssb(name, shape, dt=F32):
            return sc.enter_context(nc.sbuf_tensor(name, shape, dt))

        wqv = ssb("wqv", [P, 2 * D])
        bqv = ssb("bqv", [P, 2 * D])
        wo = ssb("wo", [P, D])
        bo = ssb("bo", [P, D])
        bmask = ssb("bmask", [P, P])
        q = ssb("q", [P, 2, G4, D])
        ek = ssb("ek", [P, 2, G4, D])
        v = ssb("v", [P, 2, G4, D + 1])
        qT = ssb("qT", [P, 2, 2, GT])
        mx = ssb("mx", [P, 2, G4 * H0])
        rs = ssb("rs", [P, 2, G4 * H0])
        rk = ssb("rk", [P, 2])
        cx = ssb("cx", [P, 2, D])
        cxT = ssb("cxT", [P, 2, D])
        wctx = ssb("wctx", [P, 2, D])
        bog = ssb("bog", [P, 2, D])
        w_loaded = signal("w_loaded")
        consts = signal("a_consts")
        qv_ready, shifted, exp_ready = signal("qv_ready"), signal("q_shifted"), signal("exp_ready")
        q_soft, qT_psum, ek_ready, qT_ready = signal("q_soft"), signal("qT_psum"), signal("ek_ready"), signal("qT_ready")
        v_ready, ctx_ready = signal("v_ready"), signal("ctx_ready")
        ctx_scaled, ctxT_psum, ctxT_ready = signal("ctx_scaled"), signal("ctxT_psum"), signal("ctxT_ready")
        wctx_psum, wctx_ready, y_ready = signal("wctx_psum"), signal("wctx_ready"), signal("y_ready")

        def tiles(bi, g):
            return [[X[:, 16 * bi + 8 * st + 4 * g + i, :] for i in range(G4)] for st in STREAMS]

        KP = 2 * 2
        with nc.Block() as block:

            @block.sync
            def _(sp):
                for dst, src in ((wqv[:, :], A["a_wqv"]), (bqv[:, :], A["a_bqv"].partition_broadcast(P)),
                                 (wo[:, :], A["L0_attn_Wo"]), (bo[:, :], A["L0_attn_bo"].partition_broadcast(P)),
                                 (bmask[:, :], A["c_bmask"])):
                    sp.dma_start(dst, src).then_inc(w_loaded.sem, 16)

            @block.gpsimd
            def _(pool):
                with pool.Fori(0, 2) as bi:
                    chain = Chain(pool, c.pool_step, bi * KP)
                    for g in range(2):
                        c.ln_rstd(pool, chain, 4 * bi + 2 * g, G4)
                    assert chain.k == KP

            @block.vector
            def _(dve):
                for st in STREAMS:
                    last = dve.memset(v[:, st, :, D:D + 1], 1.0)
                last.then_inc(consts.sem, 1)
                dve.wait_ge(w_loaded.sem, 16 * 5)
                with dve.Fori(0, 2) as bi:
                    chain = Chain(dve, c.dve_step, bi * KDA)
                    for g in range(2):
                        u = 4 * bi + 2 * g
                        c.ln_stats(dve, chain, tiles(bi, g))
                        c.ln_apply(dve, u, tiles(bi, g))
                        for st in STREAMS:
                            dve.wait_ge(qv_ready.sem, qv_ready.at(u + st + 1))
                            qv = bank(st, 1, 2).rearrange("p b (t c) -> p (b t) c", c=2 * D)
                            chain(dve.tensor_tensor(q[:, st, :, :], qv[:, :, 0:D], bc(bqv[:, 0:D], 1, G4), ALU.add))
                            dve.tensor_tensor(v[:, st, :, 0:D], qv[:, :, D:2 * D], bc(bqv[:, D:2 * D], 1, G4),
                                              ALU.add).then_inc(v_ready.sem, 1)
                            qh = q[:, st, :, :].rearrange("p t (h e) -> p (t h) e", e=DH0)
                            chain(dve.tensor_reduce(mx[:, st, :], qh, AX.X, ALU.max))
                            dve.tensor_tensor(qh, qh, bc(mx[:, st, :], 2, DH0), ALU.subtract)\
                               .then_inc(shifted.sem, 1)
                        for st in STREAMS:
                            dve.wait_ge(exp_ready.sem, exp_ready.at(u + st + 1))
                            qh = q[:, st, :, :].rearrange("p t (h e) -> p (t h) e", e=DH0)
                            chain(dve.tensor_reduce(rs[:, st, :], qh, AX.X, ALU.add))
                            chain(dve.reciprocal(rs[:, st, :], rs[:, st, :]))
                            dve.tensor_tensor(qh, qh, bc(rs[:, st, :], 2, DH0), ALU.mult).then_inc(q_soft.sem, 1)
                    for st in STREAMS:
                        dve.wait_ge(ctx_ready.sem, ctx_ready.at(2 * bi + st + 1))
                        chain(dve.reciprocal(rk[:, st:st + 1], bank(st, 3)[:, D:D + 1]))
                        dve.scalar_tensor_tensor(cx[:, st, :], bank(st, 3)[:, 0:D], rk[:, st:st + 1], bmask[:, :],
                                                 ALU.mult, ALU.mult).then_inc(ctx_scaled.sem, 1)
                    for st in STREAMS:
                        ga = c.rowB[:, 0, 2 * bi + st, :]
                        dve.wait_ge(wctx_psum.sem, wctx_psum.at(2 * bi + st + 1))
                        dve.tensor_tensor(wctx[:, st, :], bank(st, 3)[:, 0:D], ga, ALU.mult)\
                           .then_inc(wctx_ready.sem, 1)
                        chain(dve.tensor_tensor(bog[:, st, :], bo[:, :], ga, ALU.mult))
                    for g in range(2):
                        for st in STREAMS:
                            dve.wait_ge(y_ready.sem, y_ready.at(4 * bi + 2 * g + st + 1))
                            xt = X[:, bass.ds(16 * bi + 8 * st + 4 * g, G4), :]
                            y = bank(st, 1 + g).rearrange("p (t d) -> p t d", d=D)
                            chain(dve.tensor_tensor(xt, xt, y, ALU.add))
                            dve.tensor_tensor(xt, xt, bc(bog[:, st, :], 1, G4), ALU.add).then_inc(c.resid_done.sem, 1)
                    assert chain.k == KDA

            @block.scalar
            def _(act):
                with act.Fori(0, 2) as bi:
                    c.mod_of_batch(act, bi, 0, 0, [2 * bi, 2 * bi + 1])
                    for g in range(2):
                        u = 4 * bi + 2 * g
                        for st in STREAMS:
                            act.wait_ge(c.xnT_ready.sem, c.xnT_ready.at(u + st + 1))
                            act.activation(c.hT[:, st, :], bank(st, 0), ACT.Identity,
                                           scale=c.modc[:, st, 1:2], bias=c.modc[:, st, 0:1]).then_inc(c.hT_ready.sem, 1)
                        for st in STREAMS:
                            act.wait_ge(shifted.sem, shifted.at(u + st + 1))
                            act.activation(q[:, st, :, :], q[:, st, :, :], ACT.Exp).then_inc(exp_ready.sem, 1)
                        for st in STREAMS:
                            act.wait_ge(q_soft.sem, q_soft.at(u + st + 1))
                            act.activation(ek[:, st, :, :], q[:, st, :, :], ACT.Exp, scale=S0)\
                               .then_inc(ek_ready.sem, 1)
                            act.wait_ge(qT_psum.sem, qT_psum.at(u + st + 1))
                            act.activation(qT[:, st, g, :], bank(st, 0), ACT.Copy, scale=S0)\
                               .then_inc(qT_ready.sem, 1)
                    for st in STREAMS:
                        act.wait_ge(ctxT_psum.sem, ctxT_psum.at(2 * bi + st + 1))
                        act.activation(cxT[:, st, :], bank(st, 0)[:, 0:D], ACT.Copy).then_inc(ctxT_ready.sem, 1)

            @block.tensor
            def _(pe):
                pe.wait_ge(w_loaded.sem, 16 * 5)
                pe.wait_ge(consts.sem, 1)
                with pe.Fori(0, 2) as bi:
                    for g in range(2):
                        u = 4 * bi + 2 * g
                        if g == 1:
                            pe.wait_ge(qT_ready.sem, qT_ready.at(4 * bi + 2))
                        c.ln_transpose(pe, u, G4)
                        for st in STREAMS:
                            pe.wait_ge(c.hT_ready.sem, c.hT_ready.at(u + st + 1))
                            for i in range(G4):
                                last = pe.matmul(bank(st, 1 + i // 2)[:, (i % 2) * 256:(i % 2) * 256 + 256],
                                                 c.hT[:, st, i * P:(i + 1) * P], wqv[:, :], start=True, stop=True)
                            last.then_inc(qv_ready.sem, 1)
                        for st in STREAMS:
                            pe.wait_ge(q_soft.sem, q_soft.at(u + st + 1))
                            for i in range(G4):
                                last = pe.transpose(bank(st, 0)[:, i * P:(i + 1) * P], q[:, st, i, :], ident[:, :])
                            last.then_inc(qT_psum.sem, 1)
                            pe.wait_ge(ek_ready.sem, ek_ready.at(u + st + 1))
                            pe.wait_ge(v_ready.sem, v_ready.at(u + st + 1))
                            for i in range(G4):
                                last = pe.matmul(bank(st, 3)[:, 0:D + 1], ek[:, st, i, :], v[:, st, i, :],
                                                 start=(g == 0 and i == 0), stop=(g == 1 and i == G4 - 1))
                            if g == 1:
                                last.then_inc(ctx_ready.sem, 1)
                    for st in STREAMS:
                        pe.wait_ge(ctx_scaled.sem, ctx_scaled.at(2 * bi + st + 1))
                        pe.wait_ge(qT_ready.sem, qT_ready.at(4 * bi + 2 + st + 1))
                        pe.transpose(bank(st, 0)[:, 0:D], cx[:, st, :], ident[:, :]).then_inc(ctxT_psum.sem, 1)
                    for st in STREAMS:
                        pe.wait_ge(ctxT_ready.sem, ctxT_ready.at(2 * bi + st + 1))
                        pe.matmul(bank(st, 3)[:, 0:D], cxT[:, st, :], wo[:, :], start=True, stop=True)\
                          .then_inc(wctx_psum.sem, 1)
                    for g in range(2):
                        for st in STREAMS:
                            pe.wait_ge(wctx_ready.sem, wctx_ready.at(2 * bi + st + 1))
                            for i in range(G4):
                                last = pe.matmul(bank(st, 1 + g)[:, i * P:(i + 1) * P],
                                                 qT[:, st, g, i * P:(i + 1) * P], wctx[:, st, :],
                                                 start=True, stop=True)
                            last.then_inc(y_ready.sem, 1)
                    for st in STREAMS:
                        pe.wait_ge(c.resid_done.sem, c.resid_done.at(4 * bi + 4))
        c.ln_advance(8)
        c.resid_done.base += 8
        c.dve_step.base += 2 * KDA
        c.pool_step.base += 2 * KP
        c.act_step.base += 2

def moe(c, A):
    nc, X, PS, bank, ident, identb, signal = c.nc, c.X, c.PS, c.bank, c.ident, c.identb, c.counter
    with ExitStack() as mc:
        def msb(name, shape, dt=F32):
            return mc.enter_context(nc.sbuf_tensor(name, shape, dt))

        h_all = msb("h_all", [P, NT * P])
        combT = msb("combT", [3 * E, NT * P], BF16)
        w1 = msb("w1", [P, (NJ + 1) * P])
        w3 = msb("w3", [P, (NJ + 1) * P])
        w2 = msb("w2", [P, NJ + 1, D])
        sel = msb("sel", [3 * E, NJ, P], BF16)
        moe_loaded = signal("moe_loaded")

        with ExitStack() as sc:
            def ssb(name, shape, dt=F32):
                return sc.enter_context(nc.sbuf_tensor(name, shape, dt))

            gw = ssb("gw", [P, E])
            gbias = ssb("gbias", [P, E])
            self32 = ssb("self32", [3 * E, NJ, P])
            score = ssb("score", [P, NT, E])
            biased = ssb("biased", [P, NT, E])
            gmax = ssb("gmax", [P, NT, NG])
            gwins = ssb("gwins", [P, NG, NT, NG], BF16)
            grank = ssb("grank", [P, NT, NG])
            keep = ssb("keep", [P, NT, NG])
            wins = ssb("wins", [P, E, NT, E], BF16)
            comb = ssb("comb", [P, NT, E])
            part = ssb("part", [P, NT, 3 * E], BF16)
            r_loaded = signal("r_loaded")
            logit_ready, logits_copied, exps_ready = signal("logit_ready"), signal("logits_copied"), signal("exps_ready")
            parts_ready, partsT_ready = signal("parts_ready"), signal("partsT_ready")

            def tiles(n):
                return [[X[:, 8 * n + 4 * st + i, :] for i in range(G4)] for st in STREAMS]

            with nc.Block() as block:

                @block.sync
                def _(sp):
                    for dst, src in ((gw[:, :], A["gwT"]), (gbias[:, :], A["L0_ffn_gate_bias"].partition_broadcast(P)),
                                     (self32[:, :, :], A["c_sel"])):
                        sp.dma_start(dst, src).then_inc(r_loaded.sem, 16)
                    for dst, src in ((w1[:, :], A["w1T"]), (w3[:, :], A["w3T"]), (w2[:, :, :], A["w2T"])):
                        sp.dma_start(dst, src).then_inc(moe_loaded.sem, 16)

                @block.gpsimd
                def _(pool):
                    with pool.Fori(0, 4) as n:
                        c.ln_rstd(pool, Chain(pool, c.pool_step, 2 * n), 2 * n, G4)

                @block.tensor
                def _(pe):
                    pe.wait_ge(r_loaded.sem, 48)
                    with pe.Fori(0, 4) as n:
                        c.ln_transpose(pe, 2 * n, G4)
                        for st in STREAMS:
                            pe.wait_ge(c.hT_ready.sem, c.hT_ready.at(2 * n + st + 1))
                            for i in range(G4):
                                last = pe.matmul(bank(st, 1)[:, i * E:(i + 1) * E], c.hT[:, st, i * P:(i + 1) * P],
                                                 gw[:, :], start=True, stop=True)
                            last.then_inc(logit_ready.sem, 1)
                    pe.wait_ge(logits_copied.sem, 8)
                    pe.wait_ge(parts_ready.sem, 1)
                    for t in range(NT):
                        last = pe.transpose(PS[:, t // 8, :].bitcast(BF16)[0:3 * E, (t % 8) * P:(t % 8 + 1) * P],
                                            part[:, t, :], identb[:, :])
                    last.then_inc(partsT_ready.sem, 1)

                @block.scalar
                def _(act):
                    with act.Fori(0, 4) as n:
                        c.mod_of_batch(act, n, 0, 3, [n, n], 2 * n)
                        for st in STREAMS:
                            act.wait_ge(c.xnT_ready.sem, c.xnT_ready.at(2 * n + st + 1))
                            act.activation(c.hT[:, st, :], bank(st, 0), ACT.Identity,
                                           scale=c.modc[:, st, 1:2], bias=c.modc[:, st, 0:1])
                            act.activation(h_all[:, bass.ds(n * 2 * GT + st * GT, GT)], bank(st, 0), ACT.Identity,
                                           scale=c.modc[:, st, 1:2], bias=c.modc[:, st, 0:1]).then_inc(c.hT_ready.sem, 1)
                    act.wait_ge(logits_copied.sem, 8)
                    act.activation(score[:, :, :], score[:, :, :], ACT.Exp).then_inc(exps_ready.sem, 1)
                    act.wait_ge(partsT_ready.sem, 1)
                    for k in range(NT // 8):
                        act.activation(combT[:, k * 8 * P:(k + 1) * 8 * P], PS[:, k, :].bitcast(BF16)[0:3 * E, :],
                                       ACT.Copy)

                @block.vector
                def _(dve):
                    with dve.Fori(0, 4) as n:
                        c.ln_stats(dve, Chain(dve, c.dve_step, n), tiles(n))
                        c.ln_apply(dve, 2 * n, tiles(n))
                        for st in STREAMS:
                            dve.wait_ge(logit_ready.sem, logit_ready.at(2 * n + st + 1))
                            dve.tensor_scalar(score[:, bass.ds(8 * n + 4 * st, G4), :],
                                              bank(st, 1)[:, 0:G4 * E].rearrange("p (t e) -> p t e", e=E), -1.0, None,
                                              ALU.mult).then_inc(logits_copied.sem, 1)
                    chain = Chain(dve, c.dve_step, 4)
                    dve.wait_ge(r_loaded.sem, 48)
                    dve.tensor_copy(sel[:, :, :], self32[:, :, :])
                    dve.memset(gwins[:, :, :, :], 0.0)
                    dve.memset(wins[:, :, :, :], 0.0)
                    dve.wait_ge(exps_ready.sem, 1)
                    chain(dve.tensor_scalar(score[:, :, :], score[:, :, :], 1.0, None, ALU.add))
                    chain(dve.reciprocal(score[:, :, :], score[:, :, :]))
                    chain(dve.tensor_tensor(biased[:, :, :], score[:, :, :], bc(gbias[:, :], 1, NT), ALU.add))
                    chain(dve.tensor_reduce(gmax[:, :, :], biased[:, :, :].rearrange("p t (g e) -> p t g e", e=EG),
                                            AX.X, ALU.max))

                    def beats(won, value, n):
                        for i in range(n):
                            if i + 1 < n:
                                last = dve.tensor_tensor(won[:, i, :, i + 1:n], bc(value[:, :, i], 2, n - 1 - i),
                                                         value[:, :, i + 1:n], ALU.is_ge)
                            if i:
                                last = dve.tensor_tensor(won[:, i, :, 0:i], bc(value[:, :, i], 2, i),
                                                         value[:, :, 0:i], ALU.is_gt)
                        chain(last)
                        k = n // 2
                        while k:
                            chain(dve.tensor_tensor(won[:, 0:k, :, :], won[:, 0:k, :, :], won[:, k:2 * k, :, :], ALU.add))
                            k //= 2

                    beats(gwins, gmax, NG)
                    chain(dve.tensor_scalar(keep[:, :, :], gwins[:, 0, :, :], float(TOPG), None, ALU.is_lt))
                    chain(dve.tensor_scalar(grank[:, :, :], keep[:, :, :], 1.0, -NEG, ALU.subtract, ALU.mult))
                    b4 = biased[:, :, :].rearrange("p t (g e) -> p (t g) e", e=EG)
                    chain(dve.tensor_tensor(b4, b4, bc(keep[:, :, :].rearrange("p t g -> p (t g)"), 2, EG), ALU.mult))
                    chain(dve.tensor_tensor(b4, b4, bc(grank[:, :, :].rearrange("p t g -> p (t g)"), 2, EG), ALU.add))
                    beats(wins, biased, E)
                    chain(dve.scalar_tensor_tensor(comb[:, :, :], wins[:, 0, :, :], float(TOPK), score[:, :, :],
                                                   ALU.is_lt, ALU.mult))
                    chain(dve.tensor_copy(part[:, :, 0:E], comb[:, :, :]))
                    chain(dve.tensor_tensor(comb[:, :, :], comb[:, :, :], part[:, :, 0:E], ALU.subtract))
                    chain(dve.tensor_copy(part[:, :, E:2 * E], comb[:, :, :]))
                    chain(dve.tensor_tensor(comb[:, :, :], comb[:, :, :], part[:, :, E:2 * E], ALU.subtract))
                    dve.tensor_copy(part[:, :, 2 * E:3 * E], comb[:, :, :]).then_inc(parts_ready.sem, 1)
                    assert chain.k == KDR, chain.k
            c.ln_advance(8)
            c.act_step.base += 4
            c.pool_step.base += 8
            c.dve_step.base += 4 + KDR

        with ExitStack() as sc:
            def ssb(name, shape, dt=F32):
                return sc.enter_context(nc.sbuf_tensor(name, shape, dt))

            sg = ssb("sg", [P, 2, GT])
            uu = ssb("uu", [P, 2, GT])
            yT = ssb("yT", [P, GT])
            gcur = ssb("gcur", [P, 1])
            h_ready, silu_ready = signal("h_ready"), signal("silu_ready")
            u_ready = signal("u_ready", 1)
            acc_ready, yB_ready = signal("acc_ready"), signal("yB_ready")
            yT_ready = signal("yT_ready", 1)
            NU = NJ + 1
            YACC, YTOK = 6, 7

            with nc.Block() as block:

                @block.tensor
                def _(pe):
                    pe.wait_ge(moe_loaded.sem, 48)
                    with pe.Fori(0, B) as b:
                        with pe.Fori(0, 2) as half:
                            g = 2 * b + half
                            tok = bass.ds(g * GT, GT)

                            def down(j):
                                pe.wait_ge(u_ready.sem, u_ready.at(NU * g + j + 1))
                                return pe.matmul(PS[:, YACC, :], w2[:, j, :], uu[:, j % 2, :],
                                                 start=(j == 0), stop=(j == NJ))

                            for j in range(NU):
                                p = j % 2
                                pe.wait_ge(u_ready.sem, u_ready.at(NU * g + max(j - 1, 0)))
                                cols = slice(j * P, (j + 1) * P)
                                pe.matmul(PS[:, 3 * p, :], w1[:, cols], h_all[:, tok], start=True, stop=True)
                                last = pe.matmul(PS[:, 3 * p + 1, :], w3[:, cols], h_all[:, tok], start=True, stop=True)
                                if j < NJ:
                                    last = pe.matmul(PS[:, 3 * p + 2, :], sel[:, j, :], combT[:, tok], start=True, stop=True)
                                last.then_inc(h_ready.sem, 1)
                                if j:
                                    down(j - 1)
                            down(NJ).then_inc(acc_ready.sem, 1)
                            pe.wait_ge(yT_ready.sem, yT_ready.at(g + 1))
                            for i in range(G4):
                                last = pe.transpose(PS[:, YTOK, i * P:(i + 1) * P], yT[:, i * P:(i + 1) * P], ident[:, :])
                            last.then_inc(yB_ready.sem, 1)

                @block.scalar
                def _(act):
                    act.activation(gcur[:, :], c.gbT[:, 0:1], ACT.Copy).then_inc(yT_ready.sem, 1)
                    with act.Fori(0, B) as b:
                        act.wait_ge(yT_ready.sem, yT_ready.at(2 * b))
                        act.activation(gcur[:, :], c.gbT[:, bass.ds(b, 1)], ACT.Copy).then_inc(c.act_step.sem, 1)
                        act.wait_ge(c.act_step.sem, c.act_step.at(b + 1))
                        with act.Fori(0, 2) as half:
                            g = 2 * b + half
                            for j in range(NU):
                                p = j % 2
                                act.wait_ge(h_ready.sem, h_ready.at(NU * g + j + 1))
                                act.activation(sg[:, p, :], PS[:, 3 * p, :], ACT.Silu).then_inc(silu_ready.sem, 1)
                            act.wait_ge(acc_ready.sem, acc_ready.at(g + 1))
                            act.activation(yT[:, :], PS[:, YACC, :], ACT.Copy, scale=gcur[:, 0:1]).then_inc(yT_ready.sem, 1)

                @block.vector
                def _(dve):
                    dve.memset(c.carrier[:, :], 0.0).then_inc(u_ready.sem, 1)
                    with dve.Fori(0, B) as b:
                        with dve.Fori(0, 2) as half:
                            g = 2 * b + half
                            chain = Chain(dve, c.dve_step, NJ * g)
                            for j in range(NU):
                                p = j % 2
                                dve.wait_ge(silu_ready.sem, silu_ready.at(NU * g + j + 1))
                                last = dve.tensor_tensor(uu[:, p, :], sg[:, p, :], PS[:, 3 * p + 1, :], ALU.mult)
                                if j < NJ:
                                    chain(last)
                                    last = dve.tensor_tensor(uu[:, p, :], uu[:, p, :], PS[:, 3 * p + 2, :], ALU.mult)
                                last.then_inc(u_ready.sem, 1)
                            dve.wait_ge(yB_ready.sem, yB_ready.at(g + 1))
                            xt = X[:, bass.ds(G4 * g, G4), :]
                            dve.tensor_tensor(xt, xt, PS[:, YTOK, :].rearrange("p (t d) -> p t d", d=D), ALU.add)
            c.act_step.base += B
            c.dve_step.base += NJ * 8

def windowed_attention(c, A):
    nc, X, bank, ident, identb = c.nc, c.X, c.bank, c.ident, c.identb
    with ExitStack() as sc:
        def ssb(name, shape, dt=F32):
            return c.sb(name, shape, dt, sc)

        wqkv = ssb("d_wqkv", [P, 3 * D])
        wo = ssb("d_wo", [P, D])
        hmask = ssb("hmask", [P, 4])
        mask32 = ssb("mask32", [P, 2, KEYS1])
        mask = ssb("mask", [P, TB, KEYS1], BF16)
        kpre = ssb("kpre", [P, B, 4, PRE])
        vpre = ssb("vpre", [KB1, B, H1, DH1 + 1])
        kx = ssb("kx", [P, 2, 4, KEYS1])
        qT = ssb("d_qT", [P, 2, P])
        va = ssb("va", [P, 2, H1, DH1 + 1])
        vb = ssb("vb", [KB1, 2, H1, DH1 + 1])
        pm = ssb("pm", [P, 2, 4, KEYS1])
        pa = ssb("pa", [P, 2, 4, P])
        pb = ssb("pb", [KB1, 2, 4, P])
        mx = ssb("d_mx", [P, 2, 4])
        kzero = ssb("kzero", [P, 4, W1])
        rz = ssb("rz", [P, 2, 2, 8])
        on = ssb("on", [P, 2, H1, DH1])
        oT = ssb("oT", [P, 2, P])
        yg = ssb("yg", [P, 2, D])
        signal = c.counter
        w_loaded = signal("d_loaded")
        pre_psum, pre_ready, consts = signal("pre_psum"), signal("pre_ready"), signal("d_consts")
        qkv_ready, kx_ready, qv_evac = signal("d_qkv"), signal("kx_ready"), signal("qv_evac")
        s_ready, p_shifted, p_exp = signal("s_ready"), signal("p_shifted"), signal("p_exp")
        pT_psum, pT_ready, o_psum = signal("pT_psum"), signal("pT_ready"), signal("o_psum")
        o_ready, oT_psum, oT_ready, y_ready = signal("o_ready"), signal("oT_psum"), signal("oT_ready"), signal("d_y")

        def first_tiles():
            return [[X[:, TB * (2 * st + i), :] for i in range(2)] for st in STREAMS]

        with nc.Block() as block:

            @block.sync
            def _(sp):
                for dst, src in ((wqkv[:, :], A["d_wqkvT"]), (wo[:, :], A["d_woutT"]), (hmask[:, :], A["c_hmask"]),
                                 (mask32[:, :, :], A["c_mask1"])):
                    sp.dma_start(dst, src).then_inc(w_loaded.sem, 16)

            @block.gpsimd
            def _(pool):
                c.ln_rstd(pool, Chain(pool, c.pool_step, 0), 0, 2)
                pool.memset(kx[:, :, :, :], 0.0)
                pool.memset(vb[:, :, :, :], 0.0)
                pool.memset(kzero[:, :, :], 0.0)

            @block.vector
            def _(dve):
                dve.memset(va[:, :, :, :], 1.0)
                dve.memset(vpre[:, :, :, :], 1.0).then_inc(consts.sem, 1)
                chain = Chain(dve, c.dve_step, 0)
                c.ln_stats(dve, chain, first_tiles())
                c.ln_apply(dve, 0, first_tiles())
                dve.wait_ge(w_loaded.sem, 64)
                dve.tensor_copy(mask[:, 0, :], mask32[:, 0, :])
                dve.tensor_copy(mask[:, 1:TB, :], bc(mask32[:, 1, :], 1, TB - 1))
                dve.wait_ge(pre_psum.sem, 1)
                for b in range(B):
                    k = bank(b // 2, 1)[:, (b % 2) * P:(b % 2) * P + PRE]
                    dve.tensor_tensor(kpre[:, b, :, :], bc(k, 1, 4), bc(hmask[:, :], 2, PRE), ALU.mult)

            @block.scalar
            def _(act):
                for st in STREAMS:
                    act.wait_ge(c.xnT_ready.sem, c.xnT_ready.at(st + 1))
                    for i in range(2):
                        b = 2 * st + i
                        last = act.activation(c.hT[:, st, i * P:(i + 1) * P], bank(st, 0)[:, i * P:(i + 1) * P], ACT.Identity,
                                              scale=c.modT[:, 1, 1, b:b + 1], bias=c.modT[:, 1, 0, b:b + 1])
                    last.then_inc(c.hT_ready.sem, 1)
                act.wait_ge(consts.sem, 1)
                act.wait_ge(pre_psum.sem, 1)
                for b in range(B):
                    v = bank(b // 2, 2)[0:PRE, (b % 2) * P:(b % 2 + 1) * P].rearrange("p (h e) -> p h e", e=DH1)
                    act.activation(vpre[W1:KB1, b, :, 0:DH1], v, ACT.Copy)

            @block.tensor
            def _(pe):
                pe.wait_ge(w_loaded.sem, 64)
                c.ln_transpose(pe, 0, 2)
                for st in STREAMS:
                    pe.wait_ge(c.hT_ready.sem, c.hT_ready.at(st + 1))
                    pe.matmul(bank(st, 1)[:, 0:2 * P], wqkv[:, D:2 * D], c.hT[:, st, 0:2 * P], start=True, stop=True)
                    for i in range(2):
                        last = pe.matmul(bank(st, 2)[0:PRE, i * P:(i + 1) * P], c.hT[:, st, i * P:i * P + PRE],
                                         wqkv[:, 2 * D:3 * D], start=True, stop=True)
                last.then_inc(pre_psum.sem, 1)
        c.ln_advance(2)
        c.pool_step.base += 2
        c.dve_step.base += 1

        PASSES = H1 // 4
        KD = 1 + 2 * PASSES + 2 + 2

        with nc.Block() as block:

            @block.gpsimd
            def _(pool):
                with pool.Fori(0, 2) as bi:
                    for st in STREAMS:
                        pool.tensor_copy(kx[:, st, :, W1:KB1], kpre[:, 2 * bi + st, :, :])
                    with pool.Fori(0, TB) as t:
                        n = TB * bi + t
                        c.ln_rstd(pool, Chain(pool, c.pool_step, 2 * n), 2 * n, 1)
                        for st in STREAMS:
                            pool.wait_ge(s_ready.sem, s_ready.at(2 * PASSES * n + 2 * (PASSES - 1) + st + 1))
                            pool.tensor_tensor(kx[:, st, :, 0:W1], kx[:, st, :, KEYS1 - W1:KEYS1], kzero[:, :, :], ALU.add)

            @block.vector
            def _(dve):
                with dve.Fori(0, 2) as bi:
                    with dve.Fori(0, TB) as t:
                        n = TB * bi + t
                        chain = Chain(dve, c.dve_step, KD * n)
                        tiles = [[X[:, 16 * bi + 8 * st + t, :]] for st in STREAMS]
                        c.ln_stats(dve, chain, tiles)
                        c.ln_apply(dve, 2 * n, tiles)
                        for st in STREAMS:
                            dve.wait_ge(qkv_ready.sem, qkv_ready.at(2 * n + st + 1))
                            dve.tensor_tensor(kx[:, st, :, KB1:KEYS1], bc(bank(st, 2)[:, 0:P], 1, 4),
                                              bc(hmask[:, :], 2, P), ALU.mult).then_inc(kx_ready.sem, 1)
                        for h in range(PASSES):
                            for st in STREAMS:
                                dve.wait_ge(s_ready.sem, s_ready.at(2 * PASSES * n + 2 * h + st + 1))
                                s = bank(st, 2, 2)[:, :, 0:2 * KEYS1].rearrange("p b (j k) -> p b j k", k=KEYS1)
                                m = mx[:, st, :].rearrange("p (b j) -> p b j", j=2)
                                chain(dve.tensor_reduce(m, s, AX.X, ALU.max))
                                dve.tensor_tensor(pm[:, st, :, :].rearrange("p (b j) k -> p b j k", j=2), s,
                                                  bc(m, 3, KEYS1), ALU.subtract).then_inc(p_shifted.sem, 1)
                        for st in STREAMS:
                            dve.wait_ge(o_psum.sem, o_psum.at(2 * n + st + 1))
                            o = bank(st, 2, 2)[:, :, 2 * KEYS1:2 * KEYS1 + 8 * (DH1 + 1)].rearrange("p b (h e) -> p b h e", e=DH1 + 1)
                            chain(dve.reciprocal(rz[:, st, :, :], o[:, :, :, DH1]))
                            dve.tensor_tensor(on[:, st, :, :].rearrange("p (b h) e -> p b h e", b=2), o[:, :, :, 0:DH1],
                                              bc(rz[:, st, :, :], 3, DH1), ALU.mult).then_inc(o_ready.sem, 1)
                        for st in STREAMS:
                            dve.wait_ge(y_ready.sem, y_ready.at(2 * n + st + 1))
                            xt = X[:, 16 * bi + 8 * st + t, :]
                            chain(dve.tensor_tensor(yg[:, st, :], bank(st, 1)[:, 0:D],
                                                    c.rowB[:, c.L1GA, 2 * bi + st, :], ALU.mult))
                            dve.tensor_tensor(xt, xt, yg[:, st, :], ALU.add).then_inc(c.resid_done.sem, 1)
                        assert chain.k == KD

            @block.scalar
            def _(act):
                with act.Fori(0, 2) as bi:
                    c.mod_of_batch(act, bi, 1, 0, [2 * bi, 2 * bi + 1], 2 * TB * bi)
                    for st in STREAMS:
                        act.activation(vb[W1:KB1, st, :, :], vpre[W1:KB1, 2 * bi + st, :, :], ACT.Copy)
                    with act.Fori(0, TB) as t:
                        n = TB * bi + t
                        for st in STREAMS:
                            act.wait_ge(c.xnT_ready.sem, c.xnT_ready.at(2 * n + st + 1))
                            act.activation(c.hT[:, st, 0:P], bank(st, 0)[:, 0:P], ACT.Identity,
                                           scale=c.modc[:, st, 1:2], bias=c.modc[:, st, 0:1]).then_inc(c.hT_ready.sem, 1)
                        for st in STREAMS:
                            act.wait_ge(qkv_ready.sem, qkv_ready.at(2 * n + st + 1))
                            act.activation(qT[:, st, :], bank(st, 1)[:, 0:P], ACT.Copy, scale=float(DH1) ** -0.5)
                            act.activation(va[:, st, :, 0:DH1], bank(st, 3)[:, 0:D].rearrange("p (h e) -> p h e", e=DH1),
                                           ACT.Copy).then_inc(qv_evac.sem, 1)
                        for h in range(PASSES):
                            k = 2 * PASSES * n + 2 * h
                            for st in STREAMS:
                                act.wait_ge(p_shifted.sem, p_shifted.at(k + st + 1))
                                act.activation(pm[:, st, :, :], pm[:, st, :, :], ACT.Exp).then_inc(p_exp.sem, 1)
                            for st in STREAMS:
                                act.wait_ge(pT_psum.sem, pT_psum.at(k + st + 1))
                                act.activation(pa[:, st, :, :].rearrange("p j q -> p (j q)"), bank(st, 0), ACT.Copy)
                                act.activation(pb[:, st, :, :].rearrange("p j q -> p (j q)"), bank(st, 1)[0:KB1, :], ACT.Copy)\
                                   .then_inc(pT_ready.sem, 1)
                        for st in STREAMS:
                            act.wait_ge(oT_psum.sem, oT_psum.at(2 * n + st + 1))
                            act.activation(vb[0:W1, st, :, :], va[W1:P, st, :, :], ACT.Copy)
                            act.activation(oT[:, st, :], bank(st, 0)[:, 0:P], ACT.Copy).then_inc(oT_ready.sem, 1)

            @block.tensor
            def _(pe):
                with pe.Fori(0, 2) as bi:
                    with pe.Fori(0, TB) as t:
                        n = TB * bi + t
                        c.ln_transpose(pe, 2 * n, 1, resid=2 * n - 1)
                        for st in STREAMS:
                            pe.wait_ge(c.hT_ready.sem, c.hT_ready.at(2 * n + st + 1))
                            h = c.hT[:, st, 0:P]
                            pe.matmul(bank(st, 1)[:, 0:P], wqkv[:, 0:D], h, start=True, stop=True)
                            pe.matmul(bank(st, 2)[:, 0:P], wqkv[:, D:2 * D], h, start=True, stop=True)
                            pe.matmul(bank(st, 3)[:, 0:D], h, wqkv[:, 2 * D:3 * D], start=True, stop=True)\
                              .then_inc(qkv_ready.sem, 1)
                        for h in range(PASSES):
                            k = 2 * PASSES * n + 2 * h
                            rows = slice(32 * h, 32 * h + 32)
                            for st in STREAMS:
                                if h == 0:
                                    pe.wait_ge(kx_ready.sem, kx_ready.at(2 * n + st + 1))
                                    pe.wait_ge(qv_evac.sem, qv_evac.at(2 * n + st + 1))
                                for b in range(2):
                                    s = bank(st, 2 + b)[:, 0:2 * KEYS1]
                                    pe.matmul(s.rearrange("p (j k) -> p j k", k=KEYS1), identb[:, :], bc(mask[:, t, :], 1, 2),
                                              start=True, stop=False)
                                    last = pe.matmul(s, qT[rows, st, :],
                                                     kx[rows, st, 2 * b:2 * b + 2, :].rearrange("p j k -> p (j k)"),
                                                     start=False, stop=True)
                                last.then_inc(s_ready.sem, 1)
                            for st in STREAMS:
                                pe.wait_ge(p_exp.sem, p_exp.at(k + st + 1))
                                for j in range(4):
                                    pe.transpose(bank(st, 0)[:, j * P:(j + 1) * P], pm[:, st, j, KB1:KEYS1], ident[:, :])
                                    last = pe.transpose(bank(st, 1)[0:KB1, j * P:(j + 1) * P], pm[:, st, j, 0:KB1], ident[:, :])
                                last.then_inc(pT_psum.sem, 1)
                            for st in STREAMS:
                                pe.wait_ge(pT_ready.sem, pT_ready.at(k + st + 1))
                                for j in range(4):
                                    head = 4 * h + j
                                    col = 2 * KEYS1 + (head % 8) * (DH1 + 1)
                                    o = bank(st, 2 + head // 8)[:, col:col + DH1 + 1]
                                    pe.matmul(o, pa[:, st, j, :], va[:, st, head, :], start=True, stop=False)
                                    last = pe.matmul(o, pb[:, st, j, :], vb[:, st, head, :], start=False, stop=True)
                                if h == PASSES - 1:
                                    last.then_inc(o_psum.sem, 1)
                        for st in STREAMS:
                            pe.wait_ge(o_ready.sem, o_ready.at(2 * n + st + 1))
                            pe.transpose(bank(st, 0)[:, 0:P], on[:, st, :, :].rearrange("p h e -> p (h e)"), ident[:, :])\
                              .then_inc(oT_psum.sem, 1)
                        for st in STREAMS:
                            pe.wait_ge(oT_ready.sem, oT_ready.at(2 * n + st + 1))
                            pe.matmul(bank(st, 1)[:, 0:D], oT[:, st, :], wo[:, :], start=True, stop=True)\
                              .then_inc(y_ready.sem, 1)
        c.ln_advance(2 * 2 * TB)
        c.resid_done.base += 2 * 2 * TB
        c.act_step.base += 2
        c.pool_step.base += 2 * 2 * TB
        c.dve_step.base += KD * 2 * TB


def start_stream(c, A, Z):
    nc, X = c.nc, c.X
    z_ready, stored = c.resid_done, c.counter("z0_stored")
    KD = 1 + 2

    def rows(b, half):
        return c.z_ffn[b, bass.ds(1 + half * GT, GT), :].rearrange("(t p) d -> p t d", p=P)

    with nc.Block() as block:

        @block.gpsimd
        def _(pool):
            with pool.Fori(0, B) as n:
                c.ln_rstd(pool, Chain(pool, c.pool_step, 2 * n), 2 * n, G4)

        @block.vector
        def _(dve):
            with dve.Fori(0, B) as n:
                chain = Chain(dve, c.dve_step, KD * n)
                tiles = [[X[:, TB * n + G4 * st + i, :] for i in range(G4)] for st in STREAMS]
                c.ln_stats(dve, chain, tiles)
                c.ln_apply(dve, 2 * n, tiles)
                for st in STREAMS:
                    z = Z[:, bass.ds(TB * n + G4 * st, G4), :]
                    dve.wait_ge(c.xn_ready.sem, c.xn_ready.at(2 * n + st + 1))
                    chain(dve.tensor_tensor(z, c.xn[:, st, :, :], bc(c.rowB[:, c.L1CB, n, :], 1, G4), ALU.mult))
                    dve.tensor_tensor(z, z, bc(c.rowB[:, c.L1SB, n, :], 1, G4), ALU.add).then_inc(z_ready.sem, 1)
                assert chain.k == KD

        @block.sync
        def _(sp):
            with sp.Fori(0, B) as n:
                for st in STREAMS:
                    sp.wait_ge(z_ready.sem, z_ready.at(2 * n + st + 1))
                    sp.dma_start(rows(n, st), Z[:, bass.ds(TB * n + G4 * st, G4), :]).then_inc(stored.sem, 16)
            sp.wait_ge(stored.sem, 16 * 2 * B)
    for s in (c.stats_ready, c.rstd_ready, c.xn_ready):
        s.base += 2 * B
    z_ready.base += 2 * B
    c.pool_step.base += 2 * B
    c.dve_step.base += KD * B


def local_transformer(c, A, Z):
    nc, bank, ident, identb, signal = c.nc, c.bank, c.ident, c.identb, c.counter
    resid = c.resid_done
    UA, UF = 2 * 2 * TB, 2 * B
    HALVES = H2 // 4
    with ExitStack() as sc:
        def ssb(name, shape, dt=F32):
            return c.sb(name, shape, dt, sc)

        wqkv = ssb("wqkv", [P, 3 * INNER])
        wo = ssb("e_wo", [P, INNER // P, D])
        w1 = ssb("f_w1", [P, 2 * HC, P])
        w2 = ssb("f_w2", [P, HC, D])
        b1 = ssb("f_b1", [P, 2 * HC])
        b2 = ssb("f_b2", [P, D])
        lnp = ssb("lnp", [P, 2])
        qks = ssb("qks", [P, 2, DH2])
        cos0 = ssb("cos0", [P, TB, 2, DH2])
        sin0 = ssb("sin0", [P, TB, 2, DH2])
        cosl = ssb("cosl", [P, TB, 2, DH2])
        sinl = ssb("sinl", [P, TB, 2, DH2])
        mask32 = ssb("e_mask32", [P, 2, KEYS2])
        mask = ssb("e_mask", [P, TB, KEYS2], BF16)
        zs = ssb("zs", [P, 2, D])
        sq = ssb("sq", [P, 2, 2, INNER])
        ss = ssb("ss", [P, 2, 2 * H2])
        rn = ssb("rn", [P, 2, 2 * H2])
        tiny = ssb("tiny", [P, 2 * H2])
        qk = ssb("qk", [P, 2, 2, H2, DH2])
        rot = ssb("rot", [P, 2, 2, H2, DH2])
        qT = ssb("e_qT", [P, 2, 4, P])
        kT = ssb("e_kT", [P, 2, 4, KEYS2])
        va = ssb("e_va", [P, 2, H2, DH2 + 1])
        vb = ssb("e_vb", [W2, 2, H2, DH2 + 1])
        pm = ssb("e_pm", [P, 2, 4, KEYS2])
        pa = ssb("e_pa", [P, 2, 4, P])
        pb = ssb("e_pb", [W2, 2, 4, P])
        mx = ssb("e_mx", [P, 2, 4])
        rz = ssb("e_rz", [P, 2, 4])
        on = ssb("e_on", [P, 2, H2, DH2])
        oT = ssb("e_oT", [P, 2, 4, P])
        zg = ssb("zg", [P, 2, G4, D])
        gate = ssb("gate", [P, 2, GT])
        uu = ssb("f_uu", [P, 2, HC, GT])

        kzero = ssb("e_kzero", [P, 4, W2])
        carrier = ssb("p_carrier", [P, 2])
        stage_stored = signal("stage_stored")
        consts, cos_done = signal("e_consts"), signal("cos_done")
        w_loaded, tables_ready = signal("e_loaded"), signal("tables_ready")
        zs_loaded = [signal(f"zs_loaded{st}") for st in STREAMS]
        zs_stored = [signal(f"zs_stored{st}") for st in STREAMS]
        zsT_psum, eh_ready, eqkv_ready, v_evac, sq_ready = (signal("zsT_psum"), signal("eh_ready"), signal("eqkv_ready"),
                                                            signal("ev_evac"), signal("sq_ready"))
        ss_ready, rn_ready, qk_normed, rot_ready = signal("ss_ready"), signal("rn_ready"), signal("qk_normed"), signal("rot_ready")
        qk_ready, qkT_psum, qkT_ready = signal("qk_ready"), signal("qkT_psum"), signal("qkT_ready")
        s_ready, p_shifted, p_exp = signal("e_s_ready"), signal("e_p_shifted"), signal("e_p_exp")
        pT_psum, pT_ready, o_psum = signal("e_pT_psum"), signal("e_pT_ready"), signal("e_o_psum")
        o_ready, oT_psum, oT_ready, y_ready = signal("e_o_ready"), signal("e_oT_psum"), signal("e_oT_ready"), signal("e_y")
        zg_loaded = [signal(f"zg_loaded{st}") for st in STREAMS]
        zg_stored = [signal(f"zg_stored{st}") for st in STREAMS]
        ag_ready, gelu_ready, u_ready, fy_ready = signal("ag_ready"), signal("gelu_ready"), signal("fu_ready"), signal("f_y")

        with nc.Block() as block:

            @block.sync
            def _(sp):
                for dst, src in ((mask32[:, :, :], A["c_mask2"]), (cos0[:, :, :, :], A["c_cos"]), (sin0[:, :, :, :], A["c_sin"])):
                    sp.dma_start(dst, src).then_inc(consts.sem, 16)
                sp.wait_ge(consts.sem, 48)

            @block.gpsimd
            def _(pool):
                pool.memset(kT[:, :, :, :], 0.0)
                pool.memset(vb[:, :, :, :], 0.0)
                pool.memset(tiny[:, :], 1e-24)
                pool.memset(kzero[:, :, :], 0.0)

            @block.vector
            def _(dve):
                dve.memset(va[:, :, :, :], 1.0)
                dve.wait_ge(consts.sem, 48)
                dve.tensor_copy(mask[:, 0, :], mask32[:, 0, :])
                dve.tensor_copy(mask[:, 1:TB, :], bc(mask32[:, 1, :], 1, TB - 1))

        KA = 2 + 2 * 2 * HALVES
        KF = 1 + 2
        KDL = KA * 2 * TB + KF * B
        KPL = 2 * 2 * TB + 2 * B
        with nc.Fori(0, DEPTH) as L:
            r0 = (UA + UF) * L
            with nc.Block() as block:

                @block.sync
                def _(sp):
                    for dst, src in ((wqkv[:, :], A["e_wqkv"][L]), (wo[:, :, :], A["e_wo"][L]), (w1[:, :, :], A["e_w1"][L]),
                                     (w2[:, :, :], A["e_w2"][L]), (b1[:, :], A["e_b1"][L]),
                                     (b2[:, :], A["e_b2"][L].partition_broadcast(P)), (lnp[:, :], A["e_lnp"][L]),
                                     (qks[:, 0, :], A["e_qs"][L].partition_broadcast(P)),
                                     (qks[:, 1, :], A["e_ks"][L].partition_broadcast(P))):
                        sp.dma_start(dst, src).then_inc(w_loaded.sem, 16)
                    sp.wait_ge(w_loaded.sem, w_loaded.at(16 * 9 * L + 16 * 9))
                    sp.sem_inc(stage_stored.sem, 1)

                @block.vector
                def _(dve):
                    dve.wait_ge(w_loaded.sem, w_loaded.at(16 * 9 * L + 16 * 9))
                    half = DH2 // 2
                    dve.tensor_tensor(cosl[:, :, :, :], cos0[:, :, :, :], bc(qks[:, :, :], 1, TB), ALU.mult)
                    dve.tensor_tensor(sinl[:, :, :, 0:half], sin0[:, :, :, 0:half], bc(qks[:, :, half:], 1, TB), ALU.mult)
                    dve.tensor_tensor(sinl[:, :, :, half:], sin0[:, :, :, half:], bc(qks[:, :, 0:half], 1, TB), ALU.mult)

            with nc.Block() as block:

                @block.sync
                def _(sp):
                    with sp.Fori(0, 2) as bi:
                        def load(t, st):
                            z = c.z_ffn[2 * bi + st]
                            half = D // 2
                            sp.dma_start(zs[:, st, 0:half], z[bass.ds(1 + P * t, P), 0:half]).then_inc(zs_loaded[st].sem, 16)
                            sp.dma_start(zs[:, st, half:D], z[bass.ds(P * t, P), half:D]).then_inc(zs_loaded[st].sem, 16)

                        def store(t, st):
                            sp.wait_ge(resid.sem, resid.at(r0 + 2 * (TB * bi + t) + st + 1))
                            sp.dma_start(c.z_attn[2 * bi + st, bass.ds(1 + P * t, P), :],
                                         Z[:, 16 * bi + 8 * st + t, :]).then_inc(zs_stored[st].sem, 16)

                        for st in STREAMS:
                            load(0, st)
                        with sp.Fori(1, TB) as t:
                            for st in STREAMS:
                                sp.wait_ge(zsT_psum.sem, zsT_psum.at(UA * L + 2 * (TB * bi + t) + st - 1))
                                load(t, st)
                            for st in STREAMS:
                                store(t - 1, st)
                        for st in STREAMS:
                            store(TB - 1, st)
                    for st in STREAMS:
                        sp.wait_ge(zs_stored[st].sem, 16 * 2 * TB * (L + 1))
                    sp.sem_inc(stage_stored.sem, 1)

                @block.gpsimd
                def _(pool):
                    half = DH2 // 2
                    with pool.Fori(0, 2) as bi:
                        with pool.Fori(0, TB) as t:
                            u = UA * L + 2 * (TB * bi + t)
                            chain = Chain(pool, c.pool_step, KPL * L + 2 * (TB * bi + t))
                            for st in STREAMS:
                                pool.wait_ge(ss_ready.sem, ss_ready.at(u + st + 1))
                                pool.tensor_tensor(rn[:, st, :], ss[:, st, :], c.neghalf[:, :], ALU.pow).then_inc(rn_ready.sem, 1)
                            for st in STREAMS:
                                pool.wait_ge(qk_normed.sem, qk_normed.at(u + st + 1))
                                pool.tensor_tensor(carrier[:, st:st + 1], tiny[:, 0:1], tiny[:, 0:1], ALU.add)
                                for s in range(2):
                                    pool.tensor_tensor(rot[:, st, s, :, 0:half], qk[:, st, s, :, half:DH2],
                                                       bc(sinl[:, t, s, 0:half], 1, H2), ALU.mult)
                                    last = pool.tensor_tensor(rot[:, st, s, :, half:DH2], qk[:, st, s, :, 0:half],
                                                              bc(sinl[:, t, s, half:DH2], 1, H2), ALU.mult)
                                last.then_inc(rot_ready.sem, 1)
                            for st in STREAMS:
                                pool.wait_ge(s_ready.sem, s_ready.at(HALVES * u + 2 * (HALVES - 1) + st + 1))
                                chain(pool.tensor_tensor(kT[:, st, :, 0:W2], kT[:, st, :, P:KEYS2], kzero[:, :, :], ALU.add))

                @block.vector
                def _(dve):
                    with dve.Fori(0, 2) as bi:
                        with dve.Fori(0, TB) as t:
                            u = UA * L + 2 * (TB * bi + t)
                            chain = Chain(dve, c.dve_step, KDL * L + KA * (TB * bi + t))
                            for st in STREAMS:
                                dve.wait_ge(sq_ready.sem, sq_ready.at(u + st + 1))
                                chain(dve.tensor_reduce(ss[:, st, :], sq[:, st, :, :].rearrange("p s (h e) -> p (s h) e", e=DH2),
                                                        AX.X, ALU.add))
                                dve.tensor_tensor(ss[:, st, :], ss[:, st, :], tiny[:, :], ALU.max).then_inc(ss_ready.sem, 1)
                            for st in STREAMS:
                                dve.wait_ge(rn_ready.sem, rn_ready.at(u + st + 1))
                                dve.tensor_tensor(qk[:, st, :, :, :].rearrange("p s h e -> p (s h) e"),
                                                  bank(st, 1, 2).rearrange("p s (h e) -> p (s h) e", e=DH2),
                                                  bc(rn[:, st, :], 2, DH2), ALU.mult).then_inc(qk_normed.sem, 1)
                            for st in STREAMS:
                                dve.wait_ge(rot_ready.sem, rot_ready.at(u + st + 1))
                                for s in range(2):
                                    last = dve.tensor_tensor(sq[:, st, s, :].rearrange("p (h e) -> p h e", e=DH2), qk[:, st, s, :, :],
                                                             bc(cosl[:, t, s, :], 1, H2), ALU.mult)
                                last.then_inc(cos_done.sem, 1)
                                dve.wait_ge(cos_done.sem, cos_done.at(u + st + 1))
                                dve.tensor_tensor(qk[:, st, :, :, :].rearrange("p s h e -> p (s h e)"),
                                                  sq[:, st, :, :].rearrange("p s e -> p (s e)"),
                                                  rot[:, st, :, :, :].rearrange("p s h e -> p (s h e)"), ALU.add)\
                                   .then_inc(qk_ready.sem, 1)
                            for h in range(HALVES):
                                for st in STREAMS:
                                    dve.wait_ge(s_ready.sem, s_ready.at(HALVES * u + 2 * h + st + 1))
                                    s = bank(st, 2, 2)[:, :, 0:2 * KEYS2].rearrange("p b (j k) -> p b j k", k=KEYS2)
                                    m = mx[:, st, :].rearrange("p (b j) -> p b j", j=2)
                                    chain(dve.tensor_reduce(m, s, AX.X, ALU.max))
                                    dve.tensor_tensor(pm[:, st, :, :].rearrange("p (b j) k -> p b j k", j=2), s,
                                                      bc(m, 3, KEYS2), ALU.subtract).then_inc(p_shifted.sem, 1)
                                for st in STREAMS:
                                    dve.wait_ge(o_psum.sem, o_psum.at(HALVES * u + 2 * h + st + 1))
                                    o = bank(st, 1)[:, 0:4 * (DH2 + 1)].rearrange("p (h e) -> p h e", e=DH2 + 1)
                                    chain(dve.reciprocal(rz[:, st, :], o[:, :, DH2]))
                                    dve.tensor_tensor(on[:, st, 4 * h:4 * h + 4, :], o[:, :, 0:DH2], bc(rz[:, st, :], 2, DH2),
                                                      ALU.mult).then_inc(o_ready.sem, 1)
                            for st in STREAMS:
                                dve.wait_ge(y_ready.sem, y_ready.at(u + st + 1))
                                z = Z[:, 16 * bi + 8 * st + t, :]
                                dve.tensor_tensor(z, z, bank(st, 1)[:, 0:D], ALU.add).then_inc(resid.sem, 1)
                            assert chain.k == KA

                @block.scalar
                def _(act):
                    with act.Fori(0, 2) as bi:
                        with act.Fori(0, TB) as t:
                            u = UA * L + 2 * (TB * bi + t)
                            for st in STREAMS:
                                act.wait_ge(zsT_psum.sem, zsT_psum.at(u + st + 1))
                                act.activation(c.hT[:, st, 0:P], bank(st, 0)[:, 0:P], ACT.Copy).then_inc(eh_ready.sem, 1)
                            for st in STREAMS:
                                act.wait_ge(eqkv_ready.sem, eqkv_ready.at(u + st + 1))
                                act.activation(sq[:, st, :, :], bank(st, 1, 2), ACT.Square).then_inc(sq_ready.sem, 1)
                                act.activation(va[:, st, :, 0:DH2], bank(st, 3).rearrange("p (h e) -> p h e", e=DH2),
                                               ACT.Copy).then_inc(v_evac.sem, 1)
                            for st in STREAMS:
                                act.wait_ge(qkT_psum.sem, qkT_psum.at(u + st + 1))
                                act.activation(qT[:, st, :, :].rearrange("p j q -> p (j q)"), bank(st, 1), ACT.Copy)
                                act.activation(kT[:, st, :, W2:KEYS2], bank(st, 2).rearrange("p (j q) -> p j q", q=P),
                                               ACT.Copy).then_inc(qkT_ready.sem, 1)
                            for h in range(HALVES):
                                k = HALVES * u + 2 * h
                                for st in STREAMS:
                                    act.wait_ge(p_shifted.sem, p_shifted.at(k + st + 1))
                                    act.activation(pm[:, st, :, :], pm[:, st, :, :], ACT.Exp).then_inc(p_exp.sem, 1)
                                for st in STREAMS:
                                    act.wait_ge(pT_psum.sem, pT_psum.at(k + st + 1))
                                    act.activation(pa[:, st, :, :].rearrange("p j q -> p (j q)"), bank(st, 0), ACT.Copy)
                                    act.activation(pb[:, st, :, :].rearrange("p j q -> p (j q)"), bank(st, 1)[0:W2, :], ACT.Copy)\
                                       .then_inc(pT_ready.sem, 1)
                            for st in STREAMS:
                                act.wait_ge(oT_psum.sem, oT_psum.at(u + st + 1))
                                act.activation(vb[:, st, :, :], va[W2:P, st, :, :], ACT.Copy)
                                act.activation(oT[:, st, :, :].rearrange("p j q -> p (j q)"), bank(st, 0), ACT.Copy)\
                                   .then_inc(oT_ready.sem, 1)

                @block.tensor
                def _(pe):
                    with pe.Fori(0, 2) as bi:
                        with pe.Fori(0, TB) as t:
                            n = TB * bi + t
                            u = UA * L + 2 * n
                            for st in STREAMS:
                                pe.wait_ge(resid.sem, resid.at(r0 + 2 * n + st - 1))
                                pe.wait_ge(zs_loaded[st].sem, zs_loaded[st].at(32 * (2 * TB * L + n) + 32))
                                pe.transpose(bank(st, 0)[:, 0:P], zs[:, st, :], ident[:, :]).then_inc(zsT_psum.sem, 1)
                            for st in STREAMS:
                                pe.wait_ge(eh_ready.sem, eh_ready.at(u + st + 1))
                                for s in range(3):
                                    last = pe.matmul(bank(st, 1 + s), c.hT[:, st, 0:P], wqkv[:, s * INNER:(s + 1) * INNER],
                                                     start=True, stop=True)
                                last.then_inc(eqkv_ready.sem, 1)
                            for st in STREAMS:
                                pe.wait_ge(qk_ready.sem, qk_ready.at(u + st + 1))
                                for s in range(2):
                                    for j in range(4):
                                        last = pe.transpose(bank(st, 1 + s)[:, j * P:(j + 1) * P],
                                                            qk[:, st, s, 2 * j:2 * j + 2, :].rearrange("p h e -> p (h e)"),
                                                            ident[:, :])
                                last.then_inc(qkT_psum.sem, 1)
                            for h in range(HALVES):
                                k = HALVES * u + 2 * h
                                for st in STREAMS:
                                    if h == 0:
                                        pe.wait_ge(qkT_ready.sem, qkT_ready.at(u + st + 1))
                                    s = [bank(st, 2 + r)[:, 0:2 * KEYS2].rearrange("p (j k) -> p j k", k=KEYS2) for r in range(2)]
                                    for r in range(2):
                                        pe.matmul(s[r], identb[:, :], bc(mask[:, t, :], 1, 2), start=True, stop=False)
                                    for j in range(2):
                                        for r in range(2):
                                            rows = slice(64 * r, 64 * r + 64)
                                            last = pe.matmul(s[r][:, j, :], qT[rows, st, 2 * h + j, :], kT[rows, st, 2 * h + j, :],
                                                             start=False, stop=(j == 1))
                                    last.then_inc(s_ready.sem, 1)
                                for st in STREAMS:
                                    pe.wait_ge(p_exp.sem, p_exp.at(k + st + 1))
                                    if h:
                                        pe.wait_ge(o_ready.sem, o_ready.at(k - 2 + st + 1))
                                    for j in range(4):
                                        pe.transpose(bank(st, 0)[:, j * P:(j + 1) * P], pm[:, st, j, W2:KEYS2], ident[:, :])
                                        last = pe.transpose(bank(st, 1)[0:W2, j * P:(j + 1) * P], pm[:, st, j, 0:W2], ident[:, :])
                                    last.then_inc(pT_psum.sem, 1)
                                for st in STREAMS:
                                    pe.wait_ge(pT_ready.sem, pT_ready.at(k + st + 1))
                                    for j in range(4):
                                        i = 2 * (j % 2) + j // 2
                                        o = bank(st, 1)[:, i * (DH2 + 1):(i + 1) * (DH2 + 1)]
                                        pe.matmul(o, pa[:, st, j, :], va[:, st, 4 * h + i, :], start=True, stop=False)
                                        last = pe.matmul(o, pb[:, st, j, :], vb[:, st, 4 * h + i, :], start=False, stop=True)
                                    last.then_inc(o_psum.sem, 1)
                            for st in STREAMS:
                                pe.wait_ge(o_ready.sem, o_ready.at(HALVES * u + 2 * (HALVES - 1) + st + 1))
                                for j in range(4):
                                    last = pe.transpose(bank(st, 0)[:, j * P:(j + 1) * P],
                                                        on[:, st, 2 * j:2 * j + 2, :].rearrange("p h e -> p (h e)"), ident[:, :])
                                last.then_inc(oT_psum.sem, 1)
                            for st in STREAMS:
                                pe.wait_ge(oT_ready.sem, oT_ready.at(u + st + 1))
                                for j in range(4):
                                    last = pe.matmul(bank(st, 1)[:, 0:D], oT[:, st, j, :], wo[:, j, :],
                                                     start=(j == 0), stop=(j == 3))
                                last.then_inc(y_ready.sem, 1)

            with nc.Block() as block:

                @block.sync
                def _(sp):
                    def load(n, st):
                        z, half = c.z_attn[n], D // 2
                        for d0, before in ((0, 1), (half, 0)):
                            src = z[bass.ds(before + GT * st, GT), d0:d0 + half].rearrange("(t p) d -> p t d", p=P)
                            sp.dma_start(zg[:, st, :, d0:d0 + half], src).then_inc(zg_loaded[st].sem, 16)

                    def store(n, st):
                        sp.wait_ge(resid.sem, resid.at(r0 + UA + 2 * n + st + 1))
                        sp.dma_start(c.z_ffn[n, bass.ds(1 + GT * st, GT), :].rearrange("(t p) d -> p t d", p=P),
                                     Z[:, bass.ds(TB * n + G4 * st, G4), :]).then_inc(zg_stored[st].sem, 16)

                    for st in STREAMS:
                        load(0, st)
                    with sp.Fori(1, B) as n:
                        for st in STREAMS:
                            sp.wait_ge(c.xn_ready.sem, c.xn_ready.at(UF * L + 2 * n + st - 1))
                            load(n, st)
                        for st in STREAMS:
                            store(n - 1, st)
                    for st in STREAMS:
                        store(B - 1, st)
                    for st in STREAMS:
                        sp.wait_ge(zg_stored[st].sem, 16 * B * (L + 1))
                    sp.sem_inc(stage_stored.sem, 1)

                @block.gpsimd
                def _(pool):
                    with pool.Fori(0, B) as n:
                        c.ln_rstd(pool, Chain(pool, c.pool_step, KPL * L + 2 * 2 * TB + 2 * n), UF * L + 2 * n, G4)

                @block.vector
                def _(dve):
                    with dve.Fori(0, B) as n:
                        u = UF * L + 2 * n
                        chain = Chain(dve, c.dve_step, KDL * L + KA * 2 * TB + KF * n)
                        tiles = [[zg[:, st, i, :] for i in range(G4)] for st in STREAMS]
                        for st in STREAMS:
                            dve.wait_ge(zg_loaded[st].sem, zg_loaded[st].at(32 * (B * L + n) + 32))
                        c.ln_stats(dve, chain, tiles)
                        c.ln_apply(dve, u, tiles)
                        for j in range(HC):
                            for st in STREAMS:
                                dve.wait_ge(gelu_ready.sem, gelu_ready.at(HC * u + 2 * j + st + 1))
                                dve.scalar_tensor_tensor(uu[:, st, j, :], bank(st, 1), b1[:, j:j + 1], gate[:, st, :],
                                                         ALU.add, ALU.mult).then_inc(u_ready.sem, 1)
                        for st in STREAMS:
                            dve.wait_ge(fy_ready.sem, fy_ready.at(u + st + 1))
                            z = Z[:, bass.ds(TB * n + G4 * st, G4), :]
                            chain(dve.tensor_tensor(z, z, bank(st, 3).rearrange("p (t d) -> p t d", d=D), ALU.add))
                            dve.tensor_tensor(z, z, bc(b2[:, :], 1, G4), ALU.add).then_inc(resid.sem, 1)
                        assert chain.k == KF

                @block.scalar
                def _(act):
                    with act.Fori(0, B) as n:
                        u = UF * L + 2 * n
                        for st in STREAMS:
                            act.wait_ge(c.xnT_ready.sem, c.xnT_ready.at(u + st + 1))
                            act.activation(c.hT[:, st, :], bank(st, 0), ACT.Identity, scale=lnp[:, 1:2],
                                           bias=lnp[:, 0:1]).then_inc(c.hT_ready.sem, 1)
                        for j in range(HC):
                            for st in STREAMS:
                                act.wait_ge(ag_ready.sem, ag_ready.at(HC * u + 2 * j + st + 1))
                                act.activation(gate[:, st, :], bank(st, 2), ACT.Gelu, bias=b1[:, HC + j:HC + j + 1])\
                                   .then_inc(gelu_ready.sem, 1)

                @block.tensor
                def _(pe):
                    with pe.Fori(0, B) as n:
                        u = UF * L + 2 * n
                        c.ln_transpose(pe, u, G4, resid=r0 + UA + 2 * n - 1)
                        for j in range(HC):
                            for st in STREAMS:
                                if j == 0:
                                    pe.wait_ge(c.hT_ready.sem, c.hT_ready.at(u + st + 1))
                                else:
                                    pe.wait_ge(u_ready.sem, u_ready.at(HC * u + 2 * (j - 1) + st + 1))
                                pe.matmul(bank(st, 1), w1[:, j, :], c.hT[:, st, :], start=True, stop=True)
                                pe.matmul(bank(st, 2), w1[:, HC + j, :], c.hT[:, st, :], start=True, stop=True)\
                                  .then_inc(ag_ready.sem, 1)
                        for st in STREAMS:
                            pe.wait_ge(u_ready.sem, u_ready.at(HC * u + 2 * (HC - 1) + st + 1))
                            for i in range(G4):
                                for j in range(HC):
                                    last = pe.matmul(bank(st, 3)[:, i * P:(i + 1) * P], uu[:, st, j, i * P:(i + 1) * P], w2[:, j, :],
                                                     start=(j == 0), stop=(j == HC - 1))
                            last.then_inc(fy_ready.sem, 1)
        c.ln_advance(UF * DEPTH)
        resid.base += DEPTH * (UA + UF)


def finish(c, Z, out):
    nc, X = c.nc, c.X
    gated, summed, stored = c.counter("gated"), c.counter("summed"), c.counter("stored")

    def batch(t, b):
        return t[:, TB * b:TB * (b + 1), :]

    with nc.Block() as block:

        @block.vector
        def _(dve):
            for b in range(B):
                dve.tensor_tensor(batch(Z, b), batch(Z, b), bc(c.rowB[:, c.L1GB, b, :], 1, TB), ALU.mult).then_inc(gated.sem, 1)
            for b in range(B):
                dve.wait_ge(gated.sem, b + 1)
                dve.tensor_tensor(batch(X, b), batch(X, b), batch(Z, b), ALU.add).then_inc(summed.sem, 1)

        @block.sync
        def _(sp):
            for b in range(B):
                sp.wait_ge(summed.sem, b + 1)
                sp.dma_start(out[b].rearrange("(t p) d -> p t d", p=P), batch(X, b)).then_inc(stored.sem, 16)
            sp.wait_ge(stored.sem, 16 * B)


def build(nc, A, out):
    with ExitStack() as ctx:
        c = Core(nc, ctx)
        setup(c, A)
        linear_attention(c, A)
        moe(c, A)
        windowed_attention(c, A)
        Z = c.sb("Z", [P, NT, D])
        start_stream(c, A, Z)
        local_transformer(c, A, Z)
        finish(c, Z, out)


KDA = 26
KDR = 21


def constants():
    c = {"c_ident": np.eye(P, dtype=np.float32)}
    h = np.arange(P) // DH0
    c["c_bmask"] = ((h[:, None] == h[None, :]) * S0).astype(np.float32)
    row, col = np.arange(3 * E) % E, np.arange(NJ * P) // INTER
    c["c_sel"] = (row[:, None] == col[None, :]).astype(np.float32).reshape(3 * E, NJ, P)
    c["c_hmask"] = (np.arange(P)[:, None] // DH1 % 4 == np.arange(4)[None, :]).astype(np.float32)
    q, k = np.arange(P)[:, None], np.arange(P)[None, :]
    before, pre = np.arange(W1)[None, :] - W1, np.arange(PRE)[None, :] + 0 * q
    own = (k <= q) & (q - k < W1)
    first = np.concatenate([before + 0 * q > 0, pre < 0, own | ((k <= q) & (k < PRE))], 1)
    other = np.concatenate([q - before < W1, pre >= 0, own], 1)
    own2 = (k <= q) & (q - k <= W2)
    before2 = np.arange(W2)[None, :] - W2
    first2, other2 = np.concatenate([before2 + 0 * q > 0, own2], 1), np.concatenate([q - before2 <= W2, own2], 1)
    c["c_mask2"] = np.where(np.stack([first2, other2], 1), 0.0, NEG).astype(np.float32)
    f = np.float32
    idx = np.arange(0, DH2, 2, dtype=f)
    inv_freq = f(1.0) / f(10000.0) ** (idx / f(DH2))
    pos = np.arange(S, dtype=f)
    freqs = pos[:, None] * inv_freq[None, :]
    base = (idx + f(0.4 * DH2)) / f(1.4 * DH2)
    xpos = base[None, :] ** ((pos - f(S // 2)) / f(W2 // 2))[:, None]
    cos, sin = np.cos(freqs), np.sin(freqs)
    cos, sin = np.concatenate([cos, cos], 1), np.concatenate([-sin, sin], 1)
    xpos = np.concatenate([xpos, xpos], 1)
    for name, tab in (("c_cos", cos), ("c_sin", sin)):
        both = np.stack([f(8.0) * tab * xpos, tab / xpos], 1).astype(f)
        c[name] = both.reshape(TB, P, 2, DH2).transpose(1, 0, 2, 3)
    c["c_mask1"] = np.where(np.stack([first, other], 1), 0.0, NEG).astype(np.float32)
    return c


def moe_layout(i):
    none = np.zeros((P - INTER, D), np.float32)
    up = lambda w, ws: np.concatenate([w.reshape(E * INTER, D), ws, none], 0).T
    down = np.concatenate([i["L0_ffn_w2"].transpose(0, 2, 1).reshape(E * INTER, D), i["L0_ffn_ws2"].T, none], 0)
    return {"gwT": i["L0_ffn_gate_w"].T, "L0_ffn_gate_bias": i["L0_ffn_gate_bias"],
            "w1T": up(i["L0_ffn_w1"], i["L0_ffn_ws1"]), "w3T": up(i["L0_ffn_w3"], i["L0_ffn_ws3"]),
            "w2T": down.reshape(NJ + 1, P, D).transpose(1, 0, 2)}


def local_layout(i):
    n = HC * P - HID

    def halves(w):
        w = w.reshape(w.shape[:-1] + (2, HID))
        w = np.pad(w, [(0, 0)] * (w.ndim - 1) + [(0, n)])
        return w.reshape(w.shape[:-2] + (2 * HC, P))

    w2 = np.pad(i["L1_ffn_w2"], [(0, 0), (0, n), (0, 0)])
    return {"e_wqkv": i["L1_ffn_wqkv"],
            "e_wo": i["L1_ffn_wo"].reshape(DEPTH, INNER // P, P, D).transpose(0, 2, 1, 3),
            "e_w1": halves(i["L1_ffn_w1"]), "e_b1": halves(i["L1_ffn_b1"]).transpose(0, 2, 1),
            "e_w2": w2.reshape(DEPTH, HC, P, D).transpose(0, 2, 1, 3), "e_b2": i["L1_ffn_b2"],
            "e_lnp": np.stack([i["L1_ffn_ln_b"], i["L1_ffn_ln_g"]], -1),
            "e_qs": i["L1_ffn_q_scale"], "e_ks": i["L1_ffn_k_scale"]}


def layout(i):
    a = {"L0_attn_x": i["L0_attn_x"], "L0_wmod": i["L0_wmod"], "L1_wmod": i["L1_wmod"],
         "L0_cT": i["L0_c"].T, "L1_cT": i["L1_c"].T,
         "a_wqv": np.concatenate([i["L0_attn_Wq"], i["L0_attn_Wv"]], 1),
         "a_bqv": np.concatenate([i["L0_attn_bq"], i["L0_attn_bv"]]),
         "L0_attn_Wo": i["L0_attn_Wo"], "L0_attn_bo": i["L0_attn_bo"]}
    a.update(moe_layout(i))
    a.update(local_layout(i))
    a.update({"d_wqkvT": i["L1_attn_w_qkv"].T, "d_woutT": i["L1_attn_w_out"].T})
    return a


def kernel(**inputs):
    import concourse.bacc as bacc
    from concourse.bass_utils import run_bass_kernel_spmd

    nc = bacc.Bacc("TRN2", target_bir_lowering=False, num_devices=1)
    arrays, args = {}, {}
    host = {k: np.asarray(v) for k, v in inputs.items()}
    for name, a in {**layout(host), **constants()}.items():
        arrays[f"in_{name}"] = a = np.ascontiguousarray(a)
        args[name] = nc.dram_tensor(f"in_{name}", a.shape, mybir.dt.from_np(a.dtype), kind="ExternalInput").ap()
    out = nc.dram_tensor("out_x", (B, S, D), F32, kind="ExternalOutput").ap()
    build(nc, args, out)
    r = run_bass_kernel_spmd(nc, [arrays], core_ids=[0])
    return r.results[0]["out_x"]
```

```python
from contextlib import ExitStack

import numpy as np
import concourse.bass as bass
from concourse import mybir

F32 = mybir.dt.float32
BF16 = mybir.dt.bfloat16
ALU = mybir.AluOpType
ACT = mybir.ActivationFunctionType
AX = mybir.AxisListType

P = 128
B, S, D = 4, 1024, 128
TB = S // P
NT = B * TB
G4 = 4
GT = G4 * P
EPS = 1e-5
STREAMS = (0, 1)
NEG = -1e30

H0, DH0 = 16, 8
S0 = float((DH0 ** 0.5) ** -0.25)
E, INTER, TOPK, NG, TOPG = 16, 64, 4, 4, 2
EG = E // NG
NJ = E * INTER // P
H1, DH1, W1, PRE = 16, 8, 64, 16
KEYS1 = W1 + PRE + P
KB1 = W1 + PRE
DEPTH, H2, DH2, W2 = 2, 8, 64, 64
INNER = H2 * DH2
KEYS2 = W2 + P
HID = int(D * 4 * 2 / 3)
HC = -(-HID // P)


class Signal:

    def __init__(self, sem, base=0):
        self.sem, self.base = sem, base

    def at(self, n):
        return self.base + n


class Chain:

    def __init__(self, eng, signal, start):
        self.eng, self.counter, self.start, self.k = eng, signal, start, 0

    def __call__(self, ins):
        self.k += 1
        ins.then_inc(self.counter.sem, 1)
        self.eng.wait_ge(self.counter.sem, self.counter.base + self.start + self.k)


class Steps:

    def __init__(self, eng, signal, start=0):
        self.eng, self.counter, self.start, self.k = eng, signal, start, 0

    def __call__(self, ins):
        self.k = self.k + 1
        ins.then_inc(self.counter.sem, 1)
        self.eng.wait_ge(self.counter.sem, self.counter.at(self.start + self.k))


def bc(ap, axis, n):
    a = ap.unsqueeze(axis)
    shape = list(a.shape)
    shape[axis] = n
    return a.broadcast_to(shape)


class Core:

    L0GA, L0GB, L1GA, L1SB, L1CB, L1GB = range(6)

    def __init__(self, nc, ctx):
        self.nc, self.ctx = nc, ctx
        sb = self.sb
        self.X = sb("X", [P, NT, D])
        self.ident = sb("ident", [P, P])
        self.identb = sb("identb", [P, P], BF16)
        self.neghalf = sb("neghalf", [P, 2 * H2])
        self.epsv = sb("epsv", [P, G4])
        self.carrier = sb("carrier", [P, 1])
        self.modc = sb("modc", [P, 2, 2])
        self.modT = sb("modT", [P, 2, 6, B])
        self.gbT = sb("gbT", [P, B])
        self.rowB = sb("rowB", [P, 6, B, D])
        self.PS = ctx.enter_context(nc.psum_tensor("PS", [P, 8, 512], F32))
        self.z_attn = nc.dram_tensor("z_attn", [B, S + 1, D], F32, kind="Internal").ap()
        self.z_ffn = nc.dram_tensor("z_ffn", [B, S + 1, D], F32, kind="Internal").ap()

        signal = self.counter
        self.dve_step, self.act_step, self.pool_step = signal("dve_step"), signal("act_step"), signal("pool_step")
        self.stats_ready, self.rstd_ready = signal("stats_ready"), signal("rstd_ready")
        self.xn_ready, self.xnT_ready, self.hT_ready = signal("xn_ready"), signal("xnT_ready"), signal("hT_ready")
        self.resid_done = signal("resid_done")

        self.stat6 = sb("stat6", [P, 2, G4, 6])
        self.meanvar = sb("meanvar", [P, 2, G4, 2])
        self.vareps = sb("vareps", [P, 2, G4])
        self.rstd = sb("rstd", [P, 2, G4])
        self.xn = sb("xn", [P, 2, G4, D])
        self.hT = sb("hT", [P, 2, GT])

    def sb(self, name, shape, dt=F32, ctx=None):
        return (ctx or self.ctx).enter_context(self.nc.sbuf_tensor(name, shape, dt))

    def counter(self, name, base=0):
        return Signal(self.ctx.enter_context(self.nc.semaphore(name)), base)

    def bank(self, st, k, n=1):
        if n == 1:
            return self.PS[:, 4 * st + k, :]
        return self.PS[:, 4 * st + k:4 * st + k + n, :]

    def ln_stats(self, dve, chain, tiles):
        for st in STREAMS:
            for i, tile in enumerate(tiles[st]):
                last = dve.bn_stats(self.stat6[:, st, i, :], tile)
        chain(last)
        dve.memset(self.carrier[:, :], 0.0)
        for st in STREAMS:
            for i, tile in enumerate(tiles[st]):
                last = dve.bn_aggr(self.meanvar[:, st, i, :], self.stat6[:, st, i, :])
            last.then_inc(self.stats_ready.sem, 1)

    def ln_rstd(self, pool, chain, u, n):
        for st in STREAMS:
            pool.wait_ge(self.stats_ready.sem, self.stats_ready.at(u + st + 1))
            chain(pool.tensor_tensor(self.vareps[:, st, 0:n], self.meanvar[:, st, 0:n, 1], self.epsv[:, 0:n], ALU.add))
            pool.tensor_tensor(self.rstd[:, st, 0:n], self.vareps[:, st, 0:n], self.neghalf[:, 0:n],
                               ALU.pow).then_inc(self.rstd_ready.sem, 1)

    def ln_apply(self, dve, u, tiles):
        for st in STREAMS:
            dve.wait_ge(self.rstd_ready.sem, self.rstd_ready.at(u + st + 1))
            for i, tile in enumerate(tiles[st]):
                last = dve.tensor_scalar(self.xn[:, st, i, :], tile, self.meanvar[:, st, i, 0:1],
                                         self.rstd[:, st, i:i + 1], ALU.subtract, ALU.mult)
            last.then_inc(self.xn_ready.sem, 1)

    def ln_transpose(self, pe, u, n, resid=None):
        for st in STREAMS:
            if resid is not None:
                pe.wait_ge(self.resid_done.sem, self.resid_done.at(resid + st))
            pe.wait_ge(self.xn_ready.sem, self.xn_ready.at(u + st + 1))
            for i in range(n):
                last = pe.transpose(self.bank(st, 0)[:, i * P:(i + 1) * P], self.xn[:, st, i, :], self.ident[:, :])
            last.then_inc(self.xnT_ready.sem, 1)

    def mod_of_batch(self, act, turn, l, k, batches, units=None):
        if units is not None:
            act.wait_ge(self.hT_ready.sem, self.hT_ready.at(units))
        for st in STREAMS:
            last = act.activation(self.modc[:, st, :], self.modT[:, l, k:k + 2, batches[st]], ACT.Copy)
        last.then_inc(self.act_step.sem, 1)
        act.wait_ge(self.act_step.sem, self.act_step.at(turn + 1))

    def ln_advance(self, units):
        for s in (self.stats_ready, self.rstd_ready, self.xn_ready, self.xnT_ready, self.hT_ready):
            s.base += units


def setup(c, A):
    nc, X, PS, bank, ident, identb, signal = c.nc, c.X, c.PS, c.bank, c.ident, c.identb, c.counter
    with ExitStack() as sc:
        def ssb(name, shape, dt=F32):
            return sc.enter_context(nc.sbuf_tensor(name, shape, dt))

        cT = ssb("cT", [P, 2, B])
        cs = ssb("cs", [P, 2, B])
        csB = ssb("csB", [P, 2, B, P])
        wmod = ssb("wmod", [P, 2, 6 * D])
        sgn = ssb("sgn", [P, 4, B, D])
        zrow = ssb("zrow", [B, D])
        gb_abs = ssb("gb_abs", [P, B])
        mod_done = signal("mod_done")
        zero_stored = signal("zero_stored")
        loaded = signal("loaded")
        with nc.Block() as block:

            @block.sync
            def _(sp):
                n = 0
                for dst, src in ((ident[:, :], A["c_ident"]), (cT[:, 0, :], A["L0_cT"]), (cT[:, 1, :], A["L1_cT"]),
                                 (wmod[:, 0, :], A["L0_wmod"]), (wmod[:, 1, :], A["L1_wmod"])):
                    sp.dma_start(dst, src).then_inc(loaded.sem, 16)
                    n += 16
                for b in range(B):
                    sp.dma_start(X[:, TB * b:TB * (b + 1), :],
                                 A["L0_attn_x"][b].rearrange("(t p) d -> p t d", p=P)).then_inc(loaded.sem, 16)
                    n += 16
                sp.wait_ge(c.dve_step.sem, 1)
                for z in (c.z_attn, c.z_ffn):
                    sp.dma_start(z[:, 0, :], zrow[:, :]).then_inc(zero_stored.sem, 16)
                sp.wait_ge(zero_stored.sem, 32)

            @block.scalar
            def _(act):
                act.wait_ge(loaded.sem, 16 * 9)
                act.activation(cs[:, :, :], cT[:, :, :], ACT.Silu).then_inc(c.act_step.sem, 1)
                act.wait_ge(mod_done.sem, 1)
                act.wait_ge(c.dve_step.sem, 3)
                for l in range(2):
                    for k in range(6):
                        c0 = 256 + (6 * l + k) * B
                        last = act.activation(c.modT[:, l, k, :], PS[:, 4, c0:c0 + B], ACT.Copy,
                                              bias=float(k in (1, 4)))
                last.then_inc(c.act_step.sem, 1)

            @block.vector
            def _(dve):
                dve.memset(zrow[:, :], 0.0).then_inc(c.dve_step.sem, 1)
                dve.memset(c.neghalf[:, :], -0.5)
                dve.memset(c.epsv[:, :], EPS)
                dve.wait_ge(c.act_step.sem, 1)
                dve.tensor_copy(csB[:, :, :, :].rearrange("p a b c -> p (a b) c"),
                                bc(cs[:, :, :].rearrange("p a b -> p (a b)"), 2, P)).then_inc(c.dve_step.sem, 1)
                dve.tensor_copy(identb[:, :], ident[:, :])
                dve.wait_ge(mod_done.sem, 1)
                for b in range(B):
                    dve.tensor_copy(c.rowB[:, 2:6, b, :],
                                    PS[:, b, :].rearrange("p (k d) -> p k d", d=D))
                    last = dve.tensor_copy(c.rowB[:, 0:2, b, :],
                                           PS[:, 4 + b, 0:256].rearrange("p (k d) -> p k d", d=D))
                chain = Chain(dve, c.dve_step, 2)
                chain(last)
                gates = (0, 1, 2, 5)
                for i, k in enumerate(gates):
                    last = dve.tensor_scalar(sgn[:, i, :, :], c.rowB[:, k, :, :], 0.0, 2.0, ALU.is_ge, ALU.mult)
                chain(last)
                last = dve.tensor_scalar(sgn[:, :, :, :], sgn[:, :, :, :], 1.0, None, ALU.subtract)
                chain(last)
                for i, k in enumerate(gates):
                    last = dve.tensor_tensor(c.rowB[:, k, :, :], c.rowB[:, k, :, :], sgn[:, i, :, :], ALU.mult)
                chain(last)
                for i, k in enumerate(gates):
                    last = dve.scalar_tensor_tensor(c.rowB[:, k, :, :].rearrange("p a b -> p (a b)"),
                                                    c.rowB[:, k, :, :].rearrange("p a b -> p (a b)"), 0.25,
                                                    sgn[:, i, :, :].rearrange("p a b -> p (a b)"),
                                                    ALU.max, ALU.mult)
                dve.tensor_scalar(c.rowB[:, 4, :, :], c.rowB[:, 4, :, :], 1.0, None, ALU.add)
                dve.wait_ge(c.act_step.sem, 2)
                chain(dve.tensor_scalar(c.gbT[:, :], c.modT[:, 0, 5, :], 0.0, 2.0, ALU.is_ge, ALU.mult))
                chain(dve.tensor_scalar(c.gbT[:, :], c.gbT[:, :], 1.0, None, ALU.subtract))
                chain(dve.tensor_tensor(gb_abs[:, :], c.gbT[:, :], c.modT[:, 0, 5, :], ALU.mult))
                dve.scalar_tensor_tensor(c.gbT[:, :], gb_abs[:, :], 0.25, c.gbT[:, :], ALU.max, ALU.mult)

            @block.tensor
            def _(pe):
                pe.wait_ge(c.dve_step.sem, 2)
                for b in range(B):
                    pe.matmul(PS[:, b, :], csB[:, 1, b, :], wmod[:, 1, 2 * D:6 * D], start=True, stop=True)
                    pe.matmul(PS[:, 4 + b, 0:D], csB[:, 0, b, :], wmod[:, 0, 2 * D:3 * D], start=True, stop=True)
                    pe.matmul(PS[:, 4 + b, D:2 * D], csB[:, 0, b, :], wmod[:, 0, 5 * D:6 * D], start=True, stop=True)
                for l in range(2):
                    for k in range(6):
                        c0 = 256 + (6 * l + k) * B
                        last = pe.matmul(PS[:, 4, c0:c0 + B], wmod[:, l, k * D:(k + 1) * D], cs[:, l, :],
                                         start=True, stop=True)
                last.then_inc(mod_done.sem, 1)
            c.act_step.base += 2
        c.dve_step.base += 9

def linear_attention(c, A):
    nc, X, PS, bank, ident, identb, signal = c.nc, c.X, c.PS, c.bank, c.ident, c.identb, c.counter
    with ExitStack() as sc:
        def ssb(name, shape, dt=F32):
            return sc.enter_context(nc.sbuf_tensor(name, shape, dt))

        wqv = ssb("wqv", [P, 2 * D])
        bqv = ssb("bqv", [P, 2 * D])
        wo = ssb("wo", [P, D])
        bo = ssb("bo", [P, D])
        bmask = ssb("bmask", [P, P])
        q = ssb("q", [P, 2, G4, D])
        ek = ssb("ek", [P, 2, G4, D])
        v = ssb("v", [P, 2, G4, D + 1])
        qT = ssb("qT", [P, 2, 2, GT])
        mx = ssb("mx", [P, 2, G4 * H0])
        rs = ssb("rs", [P, 2, G4 * H0])
        rk = ssb("rk", [P, 2])
        cx = ssb("cx", [P, 2, D])
        cxT = ssb("cxT", [P, 2, D])
        wctx = ssb("wctx", [P, 2, D])
        bog = ssb("bog", [P, 2, D])
        w_loaded = signal("w_loaded")
        consts = signal("a_consts")
        qv_ready, shifted, exp_ready = signal("qv_ready"), signal("q_shifted"), signal("exp_ready")
        q_soft, qT_psum, ek_ready, qT_ready = signal("q_soft"), signal("qT_psum"), signal("ek_ready"), signal("qT_ready")
        v_ready, ctx_ready = signal("v_ready"), signal("ctx_ready")
        ctx_scaled, ctxT_psum, ctxT_ready = signal("ctx_scaled"), signal("ctxT_psum"), signal("ctxT_ready")
        wctx_psum, wctx_ready, y_ready = signal("wctx_psum"), signal("wctx_ready"), signal("y_ready")

        def tiles(bi, g):
            return [[X[:, 16 * bi + 8 * st + 4 * g + i, :] for i in range(G4)] for st in STREAMS]

        KP = 2 * 2
        with nc.Block() as block:

            @block.sync
            def _(sp):
                for dst, src in ((wqv[:, :], A["a_wqv"]), (bqv[:, :], A["a_bqv"].partition_broadcast(P)),
                                 (wo[:, :], A["L0_attn_Wo"]), (bo[:, :], A["L0_attn_bo"].partition_broadcast(P)),
                                 (bmask[:, :], A["c_bmask"])):
                    sp.dma_start(dst, src).then_inc(w_loaded.sem, 16)

            @block.gpsimd
            def _(pool):
                with pool.Fori(0, 2) as bi:
                    chain = Chain(pool, c.pool_step, bi * KP)
                    for g in range(2):
                        c.ln_rstd(pool, chain, 4 * bi + 2 * g, G4)
                    assert chain.k == KP

            @block.vector
            def _(dve):
                for st in STREAMS:
                    last = dve.memset(v[:, st, :, D:D + 1], 1.0)
                last.then_inc(consts.sem, 1)
                dve.wait_ge(w_loaded.sem, 16 * 5)
                with dve.Fori(0, 2) as bi:
                    chain = Chain(dve, c.dve_step, bi * KDA)
                    for g in range(2):
                        u = 4 * bi + 2 * g
                        c.ln_stats(dve, chain, tiles(bi, g))
                        c.ln_apply(dve, u, tiles(bi, g))
                        for st in STREAMS:
                            dve.wait_ge(qv_ready.sem, qv_ready.at(u + st + 1))
                            qv = bank(st, 1, 2).rearrange("p b (t c) -> p (b t) c", c=2 * D)
                            chain(dve.tensor_tensor(q[:, st, :, :], qv[:, :, 0:D], bc(bqv[:, 0:D], 1, G4), ALU.add))
                            dve.tensor_tensor(v[:, st, :, 0:D], qv[:, :, D:2 * D], bc(bqv[:, D:2 * D], 1, G4),
                                              ALU.add).then_inc(v_ready.sem, 1)
                            qh = q[:, st, :, :].rearrange("p t (h e) -> p (t h) e", e=DH0)
                            chain(dve.tensor_reduce(mx[:, st, :], qh, AX.X, ALU.max))
                            dve.tensor_tensor(qh, qh, bc(mx[:, st, :], 2, DH0), ALU.subtract)\
                               .then_inc(shifted.sem, 1)
                        for st in STREAMS:
                            dve.wait_ge(exp_ready.sem, exp_ready.at(u + st + 1))
                            qh = q[:, st, :, :].rearrange("p t (h e) -> p (t h) e", e=DH0)
                            chain(dve.tensor_reduce(rs[:, st, :], qh, AX.X, ALU.add))
                            chain(dve.reciprocal(rs[:, st, :], rs[:, st, :]))
                            dve.tensor_tensor(qh, qh, bc(rs[:, st, :], 2, DH0), ALU.mult).then_inc(q_soft.sem, 1)
                    for st in STREAMS:
                        dve.wait_ge(ctx_ready.sem, ctx_ready.at(2 * bi + st + 1))
                        chain(dve.reciprocal(rk[:, st:st + 1], bank(st, 3)[:, D:D + 1]))
                        dve.scalar_tensor_tensor(cx[:, st, :], bank(st, 3)[:, 0:D], rk[:, st:st + 1], bmask[:, :],
                                                 ALU.mult, ALU.mult).then_inc(ctx_scaled.sem, 1)
                    for st in STREAMS:
                        ga = c.rowB[:, 0, 2 * bi + st, :]
                        dve.wait_ge(wctx_psum.sem, wctx_psum.at(2 * bi + st + 1))
                        dve.tensor_tensor(wctx[:, st, :], bank(st, 3)[:, 0:D], ga, ALU.mult)\
                           .then_inc(wctx_ready.sem, 1)
                        chain(dve.tensor_tensor(bog[:, st, :], bo[:, :], ga, ALU.mult))
                    for g in range(2):
                        for st in STREAMS:
                            dve.wait_ge(y_ready.sem, y_ready.at(4 * bi + 2 * g + st + 1))
                            xt = X[:, bass.ds(16 * bi + 8 * st + 4 * g, G4), :]
                            y = bank(st, 1 + g).rearrange("p (t d) -> p t d", d=D)
                            chain(dve.tensor_tensor(xt, xt, y, ALU.add))
                            dve.tensor_tensor(xt, xt, bc(bog[:, st, :], 1, G4), ALU.add).then_inc(c.resid_done.sem, 1)
                    assert chain.k == KDA

            @block.scalar
            def _(act):
                with act.Fori(0, 2) as bi:
                    c.mod_of_batch(act, bi, 0, 0, [2 * bi, 2 * bi + 1])
                    for g in range(2):
                        u = 4 * bi + 2 * g
                        for st in STREAMS:
                            act.wait_ge(c.xnT_ready.sem, c.xnT_ready.at(u + st + 1))
                            act.activation(c.hT[:, st, :], bank(st, 0), ACT.Identity,
                                           scale=c.modc[:, st, 1:2], bias=c.modc[:, st, 0:1]).then_inc(c.hT_ready.sem, 1)
                        for st in STREAMS:
                            act.wait_ge(shifted.sem, shifted.at(u + st + 1))
                            act.activation(q[:, st, :, :], q[:, st, :, :], ACT.Exp).then_inc(exp_ready.sem, 1)
                        for st in STREAMS:
                            act.wait_ge(q_soft.sem, q_soft.at(u + st + 1))
                            act.activation(ek[:, st, :, :], q[:, st, :, :], ACT.Exp, scale=S0)\
                               .then_inc(ek_ready.sem, 1)
                            act.wait_ge(qT_psum.sem, qT_psum.at(u + st + 1))
                            act.activation(qT[:, st, g, :], bank(st, 0), ACT.Copy, scale=S0)\
                               .then_inc(qT_ready.sem, 1)
                    for st in STREAMS:
                        act.wait_ge(ctxT_psum.sem, ctxT_psum.at(2 * bi + st + 1))
                        act.activation(cxT[:, st, :], bank(st, 0)[:, 0:D], ACT.Copy).then_inc(ctxT_ready.sem, 1)

            @block.tensor
            def _(pe):
                pe.wait_ge(w_loaded.sem, 16 * 5)
                pe.wait_ge(consts.sem, 1)
                with pe.Fori(0, 2) as bi:
                    for g in range(2):
                        u = 4 * bi + 2 * g
                        if g == 1:
                            pe.wait_ge(qT_ready.sem, qT_ready.at(4 * bi + 2))
                        c.ln_transpose(pe, u, G4)
                        for st in STREAMS:
                            pe.wait_ge(c.hT_ready.sem, c.hT_ready.at(u + st + 1))
                            for i in range(G4):
                                last = pe.matmul(bank(st, 1 + i // 2)[:, (i % 2) * 256:(i % 2) * 256 + 256],
                                                 c.hT[:, st, i * P:(i + 1) * P], wqv[:, :], start=True, stop=True)
                            last.then_inc(qv_ready.sem, 1)
                        for st in STREAMS:
                            pe.wait_ge(q_soft.sem, q_soft.at(u + st + 1))
                            for i in range(G4):
                                last = pe.transpose(bank(st, 0)[:, i * P:(i + 1) * P], q[:, st, i, :], ident[:, :])
                            last.then_inc(qT_psum.sem, 1)
                            pe.wait_ge(ek_ready.sem, ek_ready.at(u + st + 1))
                            pe.wait_ge(v_ready.sem, v_ready.at(u + st + 1))
                            for i in range(G4):
                                last = pe.matmul(bank(st, 3)[:, 0:D + 1], ek[:, st, i, :], v[:, st, i, :],
                                                 start=(g == 0 and i == 0), stop=(g == 1 and i == G4 - 1))
                            if g == 1:
                                last.then_inc(ctx_ready.sem, 1)
                    for st in STREAMS:
                        pe.wait_ge(ctx_scaled.sem, ctx_scaled.at(2 * bi + st + 1))
                        pe.wait_ge(qT_ready.sem, qT_ready.at(4 * bi + 2 + st + 1))
                        pe.transpose(bank(st, 0)[:, 0:D], cx[:, st, :], ident[:, :]).then_inc(ctxT_psum.sem, 1)
                    for st in STREAMS:
                        pe.wait_ge(ctxT_ready.sem, ctxT_ready.at(2 * bi + st + 1))
                        pe.matmul(bank(st, 3)[:, 0:D], cxT[:, st, :], wo[:, :], start=True, stop=True)\
                          .then_inc(wctx_psum.sem, 1)
                    for g in range(2):
                        for st in STREAMS:
                            pe.wait_ge(wctx_ready.sem, wctx_ready.at(2 * bi + st + 1))
                            for i in range(G4):
                                last = pe.matmul(bank(st, 1 + g)[:, i * P:(i + 1) * P],
                                                 qT[:, st, g, i * P:(i + 1) * P], wctx[:, st, :],
                                                 start=True, stop=True)
                            last.then_inc(y_ready.sem, 1)
                    for st in STREAMS:
                        pe.wait_ge(c.resid_done.sem, c.resid_done.at(4 * bi + 4))
        c.ln_advance(8)
        c.resid_done.base += 8
        c.dve_step.base += 2 * KDA
        c.pool_step.base += 2 * KP
        c.act_step.base += 2

def moe(c, A):
    nc, X, PS, bank, ident, identb, signal = c.nc, c.X, c.PS, c.bank, c.ident, c.identb, c.counter
    with ExitStack() as mc:
        def msb(name, shape, dt=F32):
            return mc.enter_context(nc.sbuf_tensor(name, shape, dt))

        h_all = msb("h_all", [P, NT * P])
        combT = msb("combT", [3 * E, NT * P], BF16)
        w1 = msb("w1", [P, (NJ + 1) * P])
        w3 = msb("w3", [P, (NJ + 1) * P])
        w2 = msb("w2", [P, NJ + 1, D])
        sel = msb("sel", [3 * E, NJ, P], BF16)
        moe_loaded = signal("moe_loaded")

        with ExitStack() as sc:
            def ssb(name, shape, dt=F32):
                return sc.enter_context(nc.sbuf_tensor(name, shape, dt))

            gw = ssb("gw", [P, E])
            gbias = ssb("gbias", [P, E])
            self32 = ssb("self32", [3 * E, NJ, P])
            score = ssb("score", [P, NT, E])
            biased = ssb("biased", [P, NT, E])
            gmax = ssb("gmax", [P, NT, NG])
            gwins = ssb("gwins", [P, NG, NT, NG], BF16)
            grank = ssb("grank", [P, NT, NG])
            keep = ssb("keep", [P, NT, NG])
            wins = ssb("wins", [P, E, NT, E], BF16)
            comb = ssb("comb", [P, NT, E])
            part = ssb("part", [P, NT, 3 * E], BF16)
            r_loaded = signal("r_loaded")
            logit_ready, logits_copied, exps_ready = signal("logit_ready"), signal("logits_copied"), signal("exps_ready")
            parts_ready, partsT_ready = signal("parts_ready"), signal("partsT_ready")

            def tiles(n):
                return [[X[:, 8 * n + 4 * st + i, :] for i in range(G4)] for st in STREAMS]

            with nc.Block() as block:

                @block.sync
                def _(sp):
                    for dst, src in ((gw[:, :], A["gwT"]), (gbias[:, :], A["L0_ffn_gate_bias"].partition_broadcast(P)),
                                     (self32[:, :, :], A["c_sel"])):
                        sp.dma_start(dst, src).then_inc(r_loaded.sem, 16)
                    for dst, src in ((w1[:, :], A["w1T"]), (w3[:, :], A["w3T"]), (w2[:, :, :], A["w2T"])):
                        sp.dma_start(dst, src).then_inc(moe_loaded.sem, 16)

                @block.gpsimd
                def _(pool):
                    with pool.Fori(0, 4) as n:
                        c.ln_rstd(pool, Chain(pool, c.pool_step, 2 * n), 2 * n, G4)

                @block.tensor
                def _(pe):
                    pe.wait_ge(r_loaded.sem, 48)
                    with pe.Fori(0, 4) as n:
                        c.ln_transpose(pe, 2 * n, G4)
                        for st in STREAMS:
                            pe.wait_ge(c.hT_ready.sem, c.hT_ready.at(2 * n + st + 1))
                            for i in range(G4):
                                last = pe.matmul(bank(st, 1)[:, i * E:(i + 1) * E], c.hT[:, st, i * P:(i + 1) * P],
                                                 gw[:, :], start=True, stop=True)
                            last.then_inc(logit_ready.sem, 1)
                    pe.wait_ge(logits_copied.sem, 8)
                    pe.wait_ge(parts_ready.sem, 1)
                    for t in range(NT):
                        last = pe.transpose(PS[:, t // 8, :].bitcast(BF16)[0:3 * E, (t % 8) * P:(t % 8 + 1) * P],
                                            part[:, t, :], identb[:, :])
                    last.then_inc(partsT_ready.sem, 1)

                @block.scalar
                def _(act):
                    with act.Fori(0, 4) as n:
                        c.mod_of_batch(act, n, 0, 3, [n, n], 2 * n)
                        for st in STREAMS:
                            act.wait_ge(c.xnT_ready.sem, c.xnT_ready.at(2 * n + st + 1))
                            act.activation(c.hT[:, st, :], bank(st, 0), ACT.Identity,
                                           scale=c.modc[:, st, 1:2], bias=c.modc[:, st, 0:1])
                            act.activation(h_all[:, bass.ds(n * 2 * GT + st * GT, GT)], bank(st, 0), ACT.Identity,
                                           scale=c.modc[:, st, 1:2], bias=c.modc[:, st, 0:1]).then_inc(c.hT_ready.sem, 1)
                    act.wait_ge(logits_copied.sem, 8)
                    act.activation(score[:, :, :], score[:, :, :], ACT.Exp).then_inc(exps_ready.sem, 1)
                    act.wait_ge(partsT_ready.sem, 1)
                    for k in range(NT // 8):
                        act.activation(combT[:, k * 8 * P:(k + 1) * 8 * P], PS[:, k, :].bitcast(BF16)[0:3 * E, :],
                                       ACT.Copy)

                @block.vector
                def _(dve):
                    with dve.Fori(0, 4) as n:
                        c.ln_stats(dve, Chain(dve, c.dve_step, n), tiles(n))
                        c.ln_apply(dve, 2 * n, tiles(n))
                        for st in STREAMS:
                            dve.wait_ge(logit_ready.sem, logit_ready.at(2 * n + st + 1))
                            dve.tensor_scalar(score[:, bass.ds(8 * n + 4 * st, G4), :],
                                              bank(st, 1)[:, 0:G4 * E].rearrange("p (t e) -> p t e", e=E), -1.0, None,
                                              ALU.mult).then_inc(logits_copied.sem, 1)
                    chain = Chain(dve, c.dve_step, 4)
                    dve.wait_ge(r_loaded.sem, 48)
                    dve.tensor_copy(sel[:, :, :], self32[:, :, :])
                    dve.memset(gwins[:, :, :, :], 0.0)
                    dve.memset(wins[:, :, :, :], 0.0)
                    dve.wait_ge(exps_ready.sem, 1)
                    chain(dve.tensor_scalar(score[:, :, :], score[:, :, :], 1.0, None, ALU.add))
                    chain(dve.reciprocal(score[:, :, :], score[:, :, :]))
                    chain(dve.tensor_tensor(biased[:, :, :], score[:, :, :], bc(gbias[:, :], 1, NT), ALU.add))
                    chain(dve.tensor_reduce(gmax[:, :, :], biased[:, :, :].rearrange("p t (g e) -> p t g e", e=EG),
                                            AX.X, ALU.max))

                    def beats(won, value, n):
                        for i in range(n):
                            if i + 1 < n:
                                last = dve.tensor_tensor(won[:, i, :, i + 1:n], bc(value[:, :, i], 2, n - 1 - i),
                                                         value[:, :, i + 1:n], ALU.is_ge)
                            if i:
                                last = dve.tensor_tensor(won[:, i, :, 0:i], bc(value[:, :, i], 2, i),
                                                         value[:, :, 0:i], ALU.is_gt)
                        chain(last)
                        k = n // 2
                        while k:
                            chain(dve.tensor_tensor(won[:, 0:k, :, :], won[:, 0:k, :, :], won[:, k:2 * k, :, :], ALU.add))
                            k //= 2

                    beats(gwins, gmax, NG)
                    chain(dve.tensor_scalar(keep[:, :, :], gwins[:, 0, :, :], float(TOPG), None, ALU.is_lt))
                    chain(dve.tensor_scalar(grank[:, :, :], keep[:, :, :], 1.0, -NEG, ALU.subtract, ALU.mult))
                    b4 = biased[:, :, :].rearrange("p t (g e) -> p (t g) e", e=EG)
                    chain(dve.tensor_tensor(b4, b4, bc(keep[:, :, :].rearrange("p t g -> p (t g)"), 2, EG), ALU.mult))
                    chain(dve.tensor_tensor(b4, b4, bc(grank[:, :, :].rearrange("p t g -> p (t g)"), 2, EG), ALU.add))
                    beats(wins, biased, E)
                    chain(dve.scalar_tensor_tensor(comb[:, :, :], wins[:, 0, :, :], float(TOPK), score[:, :, :],
                                                   ALU.is_lt, ALU.mult))
                    chain(dve.tensor_copy(part[:, :, 0:E], comb[:, :, :]))
                    chain(dve.tensor_tensor(comb[:, :, :], comb[:, :, :], part[:, :, 0:E], ALU.subtract))
                    chain(dve.tensor_copy(part[:, :, E:2 * E], comb[:, :, :]))
                    chain(dve.tensor_tensor(comb[:, :, :], comb[:, :, :], part[:, :, E:2 * E], ALU.subtract))
                    dve.tensor_copy(part[:, :, 2 * E:3 * E], comb[:, :, :]).then_inc(parts_ready.sem, 1)
                    assert chain.k == KDR, chain.k
            c.ln_advance(8)
            c.act_step.base += 4
            c.pool_step.base += 8
            c.dve_step.base += 4 + KDR

        with ExitStack() as sc:
            def ssb(name, shape, dt=F32):
                return sc.enter_context(nc.sbuf_tensor(name, shape, dt))

            sg = ssb("sg", [P, 2, GT])
            uu = ssb("uu", [P, 2, GT])
            yT = ssb("yT", [P, GT])
            gcur = ssb("gcur", [P, 1])
            h_ready, silu_ready = signal("h_ready"), signal("silu_ready")
            u_ready = signal("u_ready", 1)
            acc_ready, yB_ready = signal("acc_ready"), signal("yB_ready")
            yT_ready = signal("yT_ready", 1)
            NU = NJ + 1
            YACC, YTOK = 6, 7

            with nc.Block() as block:

                @block.tensor
                def _(pe):
                    pe.wait_ge(moe_loaded.sem, 48)
                    with pe.Fori(0, B) as b:
                        with pe.Fori(0, 2) as half:
                            g = 2 * b + half
                            tok = bass.ds(g * GT, GT)

                            def down(j):
                                pe.wait_ge(u_ready.sem, u_ready.at(NU * g + j + 1))
                                return pe.matmul(PS[:, YACC, :], w2[:, j, :], uu[:, j % 2, :],
                                                 start=(j == 0), stop=(j == NJ))

                            for j in range(NU):
                                p = j % 2
                                pe.wait_ge(u_ready.sem, u_ready.at(NU * g + max(j - 1, 0)))
                                cols = slice(j * P, (j + 1) * P)
                                pe.matmul(PS[:, 3 * p, :], w1[:, cols], h_all[:, tok], start=True, stop=True)
                                last = pe.matmul(PS[:, 3 * p + 1, :], w3[:, cols], h_all[:, tok], start=True, stop=True)
                                if j < NJ:
                                    last = pe.matmul(PS[:, 3 * p + 2, :], sel[:, j, :], combT[:, tok], start=True, stop=True)
                                last.then_inc(h_ready.sem, 1)
                                if j:
                                    down(j - 1)
                            down(NJ).then_inc(acc_ready.sem, 1)
                            pe.wait_ge(yT_ready.sem, yT_ready.at(g + 1))
                            for i in range(G4):
                                last = pe.transpose(PS[:, YTOK, i * P:(i + 1) * P], yT[:, i * P:(i + 1) * P], ident[:, :])
                            last.then_inc(yB_ready.sem, 1)

                @block.scalar
                def _(act):
                    act.activation(gcur[:, :], c.gbT[:, 0:1], ACT.Copy).then_inc(yT_ready.sem, 1)
                    with act.Fori(0, B) as b:
                        act.wait_ge(yT_ready.sem, yT_ready.at(2 * b))
                        act.activation(gcur[:, :], c.gbT[:, bass.ds(b, 1)], ACT.Copy).then_inc(c.act_step.sem, 1)
                        act.wait_ge(c.act_step.sem, c.act_step.at(b + 1))
                        with act.Fori(0, 2) as half:
                            g = 2 * b + half
                            for j in range(NU):
                                p = j % 2
                                act.wait_ge(h_ready.sem, h_ready.at(NU * g + j + 1))
                                act.activation(sg[:, p, :], PS[:, 3 * p, :], ACT.Silu).then_inc(silu_ready.sem, 1)
                            act.wait_ge(acc_ready.sem, acc_ready.at(g + 1))
                            act.activation(yT[:, :], PS[:, YACC, :], ACT.Copy, scale=gcur[:, 0:1]).then_inc(yT_ready.sem, 1)

                @block.vector
                def _(dve):
                    dve.memset(c.carrier[:, :], 0.0).then_inc(u_ready.sem, 1)
                    with dve.Fori(0, B) as b:
                        with dve.Fori(0, 2) as half:
                            g = 2 * b + half
                            chain = Chain(dve, c.dve_step, NJ * g)
                            for j in range(NU):
                                p = j % 2
                                dve.wait_ge(silu_ready.sem, silu_ready.at(NU * g + j + 1))
                                last = dve.tensor_tensor(uu[:, p, :], sg[:, p, :], PS[:, 3 * p + 1, :], ALU.mult)
                                if j < NJ:
                                    chain(last)
                                    last = dve.tensor_tensor(uu[:, p, :], uu[:, p, :], PS[:, 3 * p + 2, :], ALU.mult)
                                last.then_inc(u_ready.sem, 1)
                            dve.wait_ge(yB_ready.sem, yB_ready.at(g + 1))
                            xt = X[:, bass.ds(G4 * g, G4), :]
                            dve.tensor_tensor(xt, xt, PS[:, YTOK, :].rearrange("p (t d) -> p t d", d=D), ALU.add)
            c.act_step.base += B
            c.dve_step.base += NJ * 8

def windowed_attention(c, A):
    nc, X, PS, ident, identb = c.nc, c.X, c.PS, c.ident, c.identb
    PASSES = H1 // 4
    VW = 32
    with ExitStack() as sc:
        def ssb(name, shape, dt=F32):
            return c.sb(name, shape, dt, sc)

        wqkv = ssb("d_wqkv", [P, 3 * D])
        wo = ssb("d_wo", [P, D])
        hmask = ssb("hmask", [P, 4])
        mask32 = ssb("mask32", [P, 2, KEYS1])
        mask = ssb("mask", [P, TB, KEYS1], BF16)
        kx = ssb("kx", [P, B, 4, KEYS1])
        kraw = ssb("kraw", [P, 2, P])
        qT = ssb("d_qT", [P, B, P])
        va = ssb("va", [P, B, H1, VW])
        vb = ssb("vb", [KB1, B, H1, VW])
        pm = ssb("pm", [P, 2, 4, KEYS1])
        pa = ssb("pa", [P, 2, 4, P])
        pb = ssb("pb", [KB1, 2, 4, P])
        mx = ssb("d_mx", [P, 2, 4])
        kzero = ssb("kzero", [P, 4, W1])
        usum = ssb("usum", [P, 2, PASSES, P])
        rz = ssb("rz", [P, H1])
        on = ssb("on", [P, 2, H1, DH1])
        oT = ssb("oT", [P, 2, P])
        yg = ssb("yg", [P, 2, D])
        SBANK, TBANK, UBANK, YBANK, RBANK, FBANK = 0, 2, 4, 5, 6, 7
        signal = c.counter
        w_loaded = signal("d_loaded")
        pre_psum, kx_zeroed, v_init, v_filled = signal("pre_psum"), signal("kx_zeroed"), signal("v_init"), signal("v_filled")
        qkv_ready, qkv_evac, before_ready, kx_ready = signal("d_qkv"), signal("qkv_evac"), signal("before_ready"), signal("kx_ready")
        s_ready, p_shifted, p_exp = signal("s_ready"), signal("p_shifted"), signal("p_exp")
        pT_psum, pT_ready, u_psum, u_evac = signal("pT_psum"), signal("pT_ready"), signal("u_psum"), signal("u_evac")
        uT_psum, o_ready, oT_psum, oT_ready, y_ready = (signal("uT_psum"), signal("o_ready"), signal("oT_psum"), signal("oT_ready"),
                                                        signal("d_y"))

        def first_tiles():
            return [[X[:, TB * (2 * st + i), :] for i in range(2)] for st in STREAMS]

        with nc.Block() as block:

            @block.sync
            def _(sp):
                for dst, src in ((wqkv[:, :], A["d_wqkvT"]), (wo[:, :], A["d_woutT"]), (hmask[:, :], A["c_hmask"]),
                                 (mask32[:, :, :], A["c_mask1"])):
                    sp.dma_start(dst, src).then_inc(w_loaded.sem, 16)

            @block.gpsimd
            def _(pool):
                c.ln_rstd(pool, Chain(pool, c.pool_step, 0), 0, 2)
                pool.memset(kzero[:, :, :], 0.0)
                pool.memset(kx[:, :, :, :], 0.0).then_inc(kx_zeroed.sem, 1)

            @block.vector
            def _(dve):
                dve.memset(va[:, :, :, :], 0.0)
                dve.memset(vb[:, :, :, :], 0.0).then_inc(v_init.sem, 1)
                dve.wait_ge(v_init.sem, 1)
                dve.memset(va[:, :, :, DH1:DH1 + 1], 1.0)
                dve.memset(vb[:, :, :, DH1:DH1 + 1], 1.0).then_inc(v_filled.sem, 1)
                chain = Chain(dve, c.dve_step, 0)
                c.ln_stats(dve, chain, first_tiles())
                c.ln_apply(dve, 0, first_tiles())
                dve.wait_ge(w_loaded.sem, 64)
                dve.tensor_copy(mask[:, 0, :], mask32[:, 0, :])
                dve.tensor_copy(mask[:, 1:TB, :], bc(mask32[:, 1, :], 1, TB - 1))
                dve.wait_ge(pre_psum.sem, 1)
                dve.wait_ge(kx_zeroed.sem, 1)
                for b in range(B):
                    k = c.bank(b // 2, 1)[:, (b % 2) * P:(b % 2) * P + PRE]
                    dve.tensor_tensor(kx[:, b, :, W1:KB1], bc(k, 1, 4), bc(hmask[:, :], 2, PRE), ALU.mult)

            @block.scalar
            def _(act):
                for st in STREAMS:
                    act.wait_ge(c.xnT_ready.sem, c.xnT_ready.at(st + 1))
                    for i in range(2):
                        b = 2 * st + i
                        last = act.activation(c.hT[:, st, i * P:(i + 1) * P], c.bank(st, 0)[:, i * P:(i + 1) * P], ACT.Identity,
                                              scale=c.modT[:, 1, 1, b:b + 1], bias=c.modT[:, 1, 0, b:b + 1])
                    last.then_inc(c.hT_ready.sem, 1)
                act.wait_ge(v_filled.sem, 1)
                act.wait_ge(pre_psum.sem, 1)
                for b in range(B):
                    v = c.bank(b // 2, 2)[0:PRE, (b % 2) * P:(b % 2 + 1) * P].rearrange("p (h e) -> p h e", e=DH1)
                    act.activation(vb[W1:KB1, b, :, 0:DH1], v, ACT.Copy)

            @block.tensor
            def _(pe):
                pe.wait_ge(w_loaded.sem, 64)
                c.ln_transpose(pe, 0, 2)
                for st in STREAMS:
                    pe.wait_ge(c.hT_ready.sem, c.hT_ready.at(st + 1))
                    pe.matmul(c.bank(st, 1)[:, 0:2 * P], wqkv[:, D:2 * D], c.hT[:, st, 0:2 * P], start=True, stop=True)
                    for i in range(2):
                        last = pe.matmul(c.bank(st, 2)[0:PRE, i * P:(i + 1) * P], c.hT[:, st, i * P:i * P + PRE],
                                         wqkv[:, 2 * D:3 * D], start=True, stop=True)
                last.then_inc(pre_psum.sem, 1)
        c.ln_advance(2)
        c.pool_step.base += 2
        c.dve_step.base += 1

        def unit(t, b):
            return B * t + b

        def before(t, b, n=1):
            t, b = (t, b - n) if b >= n else (t - 1, b - n + B)
            return None if isinstance(t, int) and t < 0 else (t, b)

        def after(t, b, n=1):
            t, b = (t, b + n) if b + n < B else (t + 1, b + n - B)
            return None if isinstance(t, int) and t >= TB else (t, b)

        def turns(eng, turn, drain):
            turn(0)
            with eng.Fori(1, TB - 1) as t:
                turn(t)
            turn(TB - 1)
            drain()

        def slots(t):
            for b in range(B):
                for h in range(PASSES):
                    yield b, h, PASSES * unit(t, b) + h

        def some(k):
            return not isinstance(k, int) or k >= 0

        with nc.Block() as block:

            @block.gpsimd
            def _(pool):
                KP = 1

                def front(t, b):
                    u, st = unit(t, b), b % 2
                    chain = Chain(pool, c.pool_step, KP * u)
                    pool.wait_ge(c.stats_ready.sem, c.stats_ready.at(u + 1))
                    chain(pool.tensor_tensor(c.vareps[:, st, 0:1], c.meanvar[:, st, 0:1, 1], c.epsv[:, 0:1], ALU.add))
                    pool.tensor_tensor(c.rstd[:, st, 0:1], c.vareps[:, st, 0:1], c.neghalf[:, 0:1],
                                       ALU.pow).then_inc(c.rstd_ready.sem, 1)
                    if not (isinstance(t, int) and t == 0):
                        pool.wait_ge(s_ready.sem, s_ready.at(2 * PASSES * (u - B + 1)))
                        pool.tensor_tensor(kx[:, b, :, 0:W1], kx[:, b, :, KEYS1 - W1:KEYS1], kzero[:, :, :],
                                           ALU.add).then_inc(before_ready.sem, 1)

                def turn(t):
                    for b in range(B):
                        if after(t, b, 2):
                            front(*after(t, b, 2))

                front(0, 0)
                front(0, 1)
                turns(pool, turn, lambda: None)

            @block.vector
            def _(dve):
                chain = Steps(dve, c.dve_step)

                def stats(t, b):
                    st = b % 2
                    chain(dve.bn_stats(c.stat6[:, st, 0, :], X[:, TB * b + t, :]))
                    dve.memset(c.carrier[:, :], 0.0)
                    dve.bn_aggr(c.meanvar[:, st, 0, :], c.stat6[:, st, 0, :]).then_inc(c.stats_ready.sem, 1)

                def apply(t, b):
                    st = b % 2
                    dve.wait_ge(c.rstd_ready.sem, c.rstd_ready.at(unit(t, b) + 1))
                    dve.tensor_scalar(c.xn[:, st, 0, :], X[:, TB * b + t, :], c.meanvar[:, st, 0, 0:1], c.rstd[:, st, 0:1],
                                      ALU.subtract, ALU.mult).then_inc(c.xn_ready.sem, 1)

                def keys(t, b):
                    u = unit(t, b)
                    if not (isinstance(t, int) and t == 0):
                        dve.wait_ge(before_ready.sem, before_ready.at(u - B + 1))
                    dve.wait_ge(qkv_evac.sem, qkv_evac.at(u + 1))
                    dve.tensor_tensor(kx[:, b, :, KB1:KEYS1], bc(kraw[:, b % 2, :], 1, 4), bc(hmask[:, :], 2, P),
                                      ALU.mult).then_inc(kx_ready.sem, 1)

                def divide(t, b):
                    dve.wait_ge(uT_psum.sem, uT_psum.at(unit(t, b) + 1))
                    o = PS[:, RBANK, :].rearrange("p (h e) -> p h e", e=VW)
                    chain(dve.reciprocal(rz[:, :], o[:, :, DH1]))
                    dve.tensor_tensor(on[:, b % 2, :, :], o[:, :, 0:DH1], bc(rz[:, :], 2, DH1), ALU.mult).then_inc(o_ready.sem, 1)

                def resid(t, b):
                    dve.wait_ge(y_ready.sem, y_ready.at(unit(t, b) + 1))
                    chain(dve.tensor_tensor(yg[:, b % 2, :], PS[:, YBANK, 0:D], c.rowB[:, c.L1GA, b, :], ALU.mult))
                    xt = X[:, TB * b + t, :]
                    dve.tensor_tensor(xt, xt, yg[:, b % 2, :], ALU.add).then_inc(c.resid_done.sem, 1)

                def turn(t):
                    for b, h, k in slots(t):
                        if h == 0:
                            if before(t, b, 3):
                                resid(*before(t, b, 3))
                            if after(t, b):
                                apply(*after(t, b))
                        for i in range(2):
                            dve.wait_ge(s_ready.sem, s_ready.at(2 * k + i + 1))
                            s = PS[:, SBANK + i, 0:2 * KEYS1].rearrange("p (j k) -> p j k", k=KEYS1)
                            m = mx[:, h % 2, 2 * i:2 * i + 2]
                            chain(dve.tensor_reduce(m, s, AX.X, ALU.max))
                            if i == 0 and some(k - 2):
                                dve.wait_ge(pT_psum.sem, pT_psum.at(k - 1))
                            dve.tensor_tensor(pm[:, h % 2, 2 * i:2 * i + 2, :], s, bc(m, 2, KEYS1),
                                              ALU.subtract).then_inc(p_shifted.sem, 1)
                        if h == 0 and before(t, b, 2):
                            divide(*before(t, b, 2))
                        elif h == 2 and after(t, b):
                            keys(*after(t, b))
                        elif h == 3 and after(t, b, 2):
                            stats(*after(t, b, 2))

                stats(0, 0)
                apply(0, 0)
                keys(0, 0)
                stats(0, 1)
                turn(0)
                first, each = chain.k, B * (2 * PASSES + 3)
                with dve.Fori(1, TB - 1) as t:
                    chain.k = first + each * (t - 1)
                    turn(t)
                chain.k = first + each * (TB - 2)
                turn(TB - 1)
                resid(TB - 1, B - 3)
                for b in (B - 2, B - 1):
                    divide(TB - 1, b)
                    resid(TB - 1, b)
                c.dve_step.base += chain.k

            @block.scalar
            def _(act):
                def front_h(t, b):
                    u, st = unit(t, b), b % 2
                    act.wait_ge(c.xnT_ready.sem, c.xnT_ready.at(u + 1))
                    act.activation(c.hT[:, st, 0:P], PS[:, FBANK, 0:P], ACT.Identity,
                                   scale=c.modT[:, 1, 1, b:b + 1], bias=c.modT[:, 1, 0, b:b + 1]).then_inc(c.hT_ready.sem, 1)

                def front_qkv(t, b):
                    u = unit(t, b)
                    act.wait_ge(qkv_ready.sem, qkv_ready.at(u + 1))
                    if not (isinstance(t, int) and t == 0):
                        act.activation(vb[0:W1, b, :, 0:DH1], va[W1:P, b, :, 0:DH1], ACT.Copy).then_inc(c.act_step.sem, 1)
                    act.activation(kraw[:, b % 2, :], PS[:, FBANK, 2 * P:3 * P], ACT.Copy)
                    act.activation(qT[:, b, :], PS[:, FBANK, P:2 * P], ACT.Copy, scale=float(DH1) ** -0.5)
                    if not (isinstance(t, int) and t == 0):
                        act.wait_ge(c.act_step.sem, c.act_step.at(u - B + 1))
                    act.activation(va[:, b, :, 0:DH1], PS[:, FBANK, 3 * P:4 * P].rearrange("p (h e) -> p h e", e=DH1),
                                   ACT.Copy).then_inc(qkv_evac.sem, 1)

                def take_u(t, b):
                    act.wait_ge(u_psum.sem, u_psum.at(unit(t, b) + 1))
                    act.activation(usum[:, b % 2, :, :].rearrange("p h q -> p (h q)"), PS[:, UBANK, :],
                                   ACT.Copy).then_inc(u_evac.sem, 1)

                def take_o(t, b):
                    act.wait_ge(oT_psum.sem, oT_psum.at(unit(t, b) + 1))
                    act.activation(oT[:, b % 2, :], PS[:, YBANK, P:2 * P], ACT.Copy).then_inc(oT_ready.sem, 1)

                def take_p(k, par):
                    act.wait_ge(pT_psum.sem, pT_psum.at(k + 1))
                    act.activation(pa[:, par, :, :].rearrange("p j q -> p (j q)"), PS[:, TBANK, :], ACT.Copy)
                    act.activation(pb[:, par, :, :].rearrange("p j q -> p (j q)"), PS[0:KB1, TBANK + 1, :],
                                   ACT.Copy).then_inc(pT_ready.sem, 1)

                def turn(t):
                    for b, h, k in slots(t):
                        if h == 1 and after(t, b):
                            front_h(*after(t, b))
                        if h == 2:
                            if before(t, b):
                                take_u(*before(t, b))
                            if before(t, b, 2):
                                take_o(*before(t, b, 2))
                            if after(t, b):
                                front_qkv(*after(t, b))
                        if some(k - 1):
                            take_p(k - 1, (h - 1) % 2)
                        act.wait_ge(p_shifted.sem, p_shifted.at(2 * k + 2))
                        act.activation(pm[:, h % 2, :, :], pm[:, h % 2, :, :], ACT.Exp).then_inc(p_exp.sem, 1)

                def drain():
                    take_p(PASSES * B * TB - 1, 1)
                    take_o(TB - 1, B - 2)
                    take_u(TB - 1, B - 1)
                    take_o(TB - 1, B - 1)

                front_h(0, 0)
                front_qkv(0, 0)
                turns(act, turn, drain)

            @block.tensor
            def _(pe):
                def front_t(t, b):
                    u = unit(t, b)
                    if some(u - 1):
                        pe.wait_ge(qkv_evac.sem, qkv_evac.at(u))
                    pe.wait_ge(c.xn_ready.sem, c.xn_ready.at(u + 1))
                    pe.transpose(PS[:, FBANK, 0:P], c.xn[:, b % 2, 0, :], ident[:, :]).then_inc(c.xnT_ready.sem, 1)

                def front_qkv(t, b):
                    pe.wait_ge(c.hT_ready.sem, c.hT_ready.at(unit(t, b) + 1))
                    h = c.hT[:, b % 2, 0:P]
                    pe.matmul(PS[:, FBANK, P:2 * P], wqkv[:, 0:D], h, start=True, stop=True)
                    pe.matmul(PS[:, FBANK, 2 * P:3 * P], wqkv[:, D:2 * D], h, start=True, stop=True)
                    pe.matmul(PS[:, FBANK, 3 * P:4 * P], h, wqkv[:, 2 * D:3 * D], start=True, stop=True).then_inc(qkv_ready.sem, 1)

                def scores(t, b, h, k):
                    if h == 0:
                        pe.wait_ge(kx_ready.sem, kx_ready.at(unit(t, b) + 1))
                        pe.wait_ge(qkv_evac.sem, qkv_evac.at(unit(t, b) + 1))
                    rows = slice(32 * h, 32 * h + 32)
                    for i in range(2):
                        if some(k - 1):
                            pe.wait_ge(p_shifted.sem, p_shifted.at(2 * k - 1 + i))
                        s = PS[:, SBANK + i, 0:2 * KEYS1]
                        pe.matmul(s.rearrange("p (j k) -> p j k", k=KEYS1), identb[:, :], bc(mask[:, t, :], 1, 2),
                                  start=True, stop=False)
                        pe.matmul(s, qT[rows, b, :], kx[rows, b, 2 * i:2 * i + 2, :].rearrange("p j k -> p (j k)"),
                                  start=False, stop=True).then_inc(s_ready.sem, 1)

                def transpose_p(k, par):
                    pe.wait_ge(p_exp.sem, p_exp.at(k + 1))
                    if some(k - 1):
                        pe.wait_ge(pT_ready.sem, pT_ready.at(k))
                    for j in range(4):
                        pe.transpose(PS[:, TBANK, j * P:(j + 1) * P], pm[:, par, j, KB1:KEYS1], ident[:, :])
                        last = pe.transpose(PS[0:KB1, TBANK + 1, j * P:(j + 1) * P], pm[:, par, j, 0:KB1], ident[:, :])
                    last.then_inc(pT_psum.sem, 1)

                def weigh(t, b, h, k):
                    pe.wait_ge(pT_ready.sem, pT_ready.at(k + 1))
                    if h == 0 and before(t, b):
                        pe.wait_ge(u_evac.sem, u_evac.at(unit(*before(t, b)) + 1))
                    for j in range(4):
                        o = PS[32 * j:32 * j + 32, UBANK, h * P:(h + 1) * P]
                        pe.matmul(o, va[:, b, 4 * h + j, :], pa[:, h % 2, j, :], start=True, stop=False)
                        last = pe.matmul(o, vb[:, b, 4 * h + j, :], pb[:, h % 2, j, :], start=False, stop=True)
                    if h == PASSES - 1:
                        last.then_inc(u_psum.sem, 1)

                def turn_u(t, b):
                    u = unit(t, b)
                    pe.wait_ge(u_evac.sem, u_evac.at(u + 1))
                    if some(u - 1):
                        pe.wait_ge(o_ready.sem, o_ready.at(u))
                    for h in range(PASSES):
                        last = pe.transpose(PS[:, RBANK, h * P:(h + 1) * P], usum[:, b % 2, h, :], ident[:, :])
                    last.then_inc(uT_psum.sem, 1)

                def turn_o(t, b):
                    u = unit(t, b)
                    pe.wait_ge(o_ready.sem, o_ready.at(u + 1))
                    if some(u - 1):
                        pe.wait_ge(c.resid_done.sem, c.resid_done.at(u))
                    pe.transpose(PS[:, YBANK, P:2 * P], on[:, b % 2, :, :].rearrange("p h e -> p (h e)"),
                                 ident[:, :]).then_inc(oT_psum.sem, 1)

                def project(t, b):
                    pe.wait_ge(oT_ready.sem, oT_ready.at(unit(t, b) + 1))
                    pe.matmul(PS[:, YBANK, 0:D], oT[:, b % 2, :], wo[:, :], start=True, stop=True).then_inc(y_ready.sem, 1)

                def turn(t):
                    for b, h, k in slots(t):
                        scores(t, b, h, k)
                        if h == 1:
                            if after(t, b):
                                front_t(*after(t, b))
                            if before(t, b, 2):
                                turn_o(*before(t, b, 2))
                        elif h == 2 and after(t, b):
                            front_qkv(*after(t, b))
                        elif h == 3:
                            if before(t, b):
                                turn_u(*before(t, b))
                            if before(t, b, 2):
                                project(*before(t, b, 2))
                        if some(k - 1):
                            transpose_p(k - 1, (h - 1) % 2)
                        if some(k - 2):
                            where = (t, b) if h >= 2 else before(t, b)
                            weigh(*where, (h - 2) % PASSES, k - 2)

                def drain():
                    k, t, b = PASSES * B * TB, TB - 1, B - 1
                    transpose_p(k - 1, 1)
                    weigh(t, b, PASSES - 2, k - 2)
                    turn_o(t, b - 1)
                    weigh(t, b, PASSES - 1, k - 1)
                    project(t, b - 1)
                    turn_u(t, b)
                    turn_o(t, b)
                    project(t, b)

                front_t(0, 0)
                front_qkv(0, 0)
                turns(pe, turn, drain)
        c.ln_advance(B * TB)
        c.resid_done.base += B * TB
        c.act_step.base += B * (TB - 1)
        c.pool_step.base += B * TB


def start_stream(c, A, Z):
    nc, X = c.nc, c.X
    z_ready, stored = c.resid_done, c.counter("z0_stored")
    KD = 1 + 2

    def rows(b, half):
        return c.z_ffn[b, bass.ds(1 + half * GT, GT), :].rearrange("(t p) d -> p t d", p=P)

    with nc.Block() as block:

        @block.gpsimd
        def _(pool):
            with pool.Fori(0, B) as n:
                c.ln_rstd(pool, Chain(pool, c.pool_step, 2 * n), 2 * n, G4)

        @block.vector
        def _(dve):
            with dve.Fori(0, B) as n:
                chain = Chain(dve, c.dve_step, KD * n)
                tiles = [[X[:, TB * n + G4 * st + i, :] for i in range(G4)] for st in STREAMS]
                c.ln_stats(dve, chain, tiles)
                c.ln_apply(dve, 2 * n, tiles)
                for st in STREAMS:
                    z = Z[:, bass.ds(TB * n + G4 * st, G4), :]
                    dve.wait_ge(c.xn_ready.sem, c.xn_ready.at(2 * n + st + 1))
                    chain(dve.tensor_tensor(z, c.xn[:, st, :, :], bc(c.rowB[:, c.L1CB, n, :], 1, G4), ALU.mult))
                    dve.tensor_tensor(z, z, bc(c.rowB[:, c.L1SB, n, :], 1, G4), ALU.add).then_inc(z_ready.sem, 1)
                assert chain.k == KD

        @block.sync
        def _(sp):
            with sp.Fori(0, B) as n:
                for st in STREAMS:
                    sp.wait_ge(z_ready.sem, z_ready.at(2 * n + st + 1))
                    sp.dma_start(rows(n, st), Z[:, bass.ds(TB * n + G4 * st, G4), :]).then_inc(stored.sem, 16)
            sp.wait_ge(stored.sem, 16 * 2 * B)
    for s in (c.stats_ready, c.rstd_ready, c.xn_ready):
        s.base += 2 * B
    z_ready.base += 2 * B
    c.pool_step.base += 2 * B
    c.dve_step.base += KD * B


def local_transformer(c, A, Z):
    nc, bank, ident, identb, signal = c.nc, c.bank, c.ident, c.identb, c.counter
    resid = c.resid_done
    UA, UF = 2 * 2 * TB, 2 * B
    HALVES = H2 // 4
    with ExitStack() as sc:
        def ssb(name, shape, dt=F32):
            return c.sb(name, shape, dt, sc)

        wqkv = ssb("wqkv", [P, 3 * INNER])
        wo = ssb("e_wo", [P, INNER // P, D])
        w1 = ssb("f_w1", [P, 2 * HC, P])
        w2 = ssb("f_w2", [P, HC, D])
        b1 = ssb("f_b1", [P, 2 * HC])
        b2 = ssb("f_b2", [P, D])
        lnp = ssb("lnp", [P, 2])
        qks = ssb("qks", [P, 2, DH2])
        cos0 = ssb("cos0", [P, TB, 2, DH2])
        sin0 = ssb("sin0", [P, TB, 2, DH2])
        cosl = ssb("cosl", [P, TB, 2, DH2])
        sinl = ssb("sinl", [P, TB, 2, DH2])
        mask32 = ssb("e_mask32", [P, 2, KEYS2])
        mask = ssb("e_mask", [P, TB, KEYS2], BF16)
        zs = ssb("zs", [P, B, D])
        sq = ssb("sq", [P, 2, 2, INNER])
        ss = ssb("ss", [P, 2, 2 * H2])
        rn = ssb("rn", [P, 2, 2 * H2])
        tiny = ssb("tiny", [P, 2 * H2])
        qk = ssb("qk", [P, 2, 2, H2, DH2])
        rot = ssb("rot", [P, 2, 2, H2, DH2])
        qT = ssb("e_qT", [P, 2, 4, P])
        kT = ssb("e_kT", [P, B, 4, KEYS2])
        va = ssb("e_va", [P, B, H2, DH2 + 1])
        vb = ssb("e_vb", [P, B, HALVES, 2, 2, DH2 + 1])
        pm = ssb("e_pm", [P, 2, 4 * KEYS2])
        pa = ssb("e_pa", [P, 2, 4, P])
        pb = ssb("e_pb", [P, 2, 2, P])
        mx = ssb("e_mx", [P, 2, 4])
        rz = ssb("e_rz", [P, 2, 4])
        on = ssb("e_on", [P, 2, H2, DH2])
        oT = ssb("e_oT", [P, 2, 4, P])
        zg = ssb("zg", [P, 2, G4, D])
        gate = ssb("gate", [P, 2, GT])
        uu = ssb("f_uu", [P, 2, HC, GT])

        kzero = ssb("e_kzero", [P, 4, W2])
        carrier = ssb("p_carrier", [P, 2])
        stage_stored = signal("stage_stored")
        consts, cos_done, before_ready, qk_taken = signal("e_consts"), signal("cos_done"), signal("e_before"), signal("qk_taken")
        w_loaded, tables_ready = signal("e_loaded"), signal("tables_ready")
        zs_loaded = [signal(f"zs_loaded{b}") for b in range(B)]
        zs_stored = [signal(f"zs_stored{b}") for b in range(B)]
        zsT_psum, eh_ready, eqkv_ready, v_evac, sq_ready = (signal("zsT_psum"), signal("eh_ready"), signal("eqkv_ready"),
                                                            signal("ev_evac"), signal("sq_ready"))
        ss_ready, rn_ready, qk_normed, rot_ready = signal("ss_ready"), signal("rn_ready"), signal("qk_normed"), signal("rot_ready")
        qk_ready, qkT_psum, qkT_ready = signal("qk_ready"), signal("qkT_psum"), signal("qkT_ready")
        s_ready, p_shifted, p_exp = signal("e_s_ready"), signal("e_p_shifted"), signal("e_p_exp")
        pT_psum, pT_ready, o_psum = signal("e_pT_psum"), signal("e_pT_ready"), signal("e_o_psum")
        o_ready, oT_psum, oT_ready, y_ready = signal("e_o_ready"), signal("e_oT_psum"), signal("e_oT_ready"), signal("e_y")
        zg_loaded = [signal(f"zg_loaded{st}") for st in STREAMS]
        zg_stored = [signal(f"zg_stored{st}") for st in STREAMS]
        ag_ready, gelu_ready, u_ready, fy_ready = signal("ag_ready"), signal("gelu_ready"), signal("fu_ready"), signal("f_y")

        with nc.Block() as block:

            @block.sync
            def _(sp):
                for dst, src in ((mask32[:, :, :], A["c_mask2"]), (cos0[:, :, :, :], A["c_cos"]), (sin0[:, :, :, :], A["c_sin"])):
                    sp.dma_start(dst, src).then_inc(consts.sem, 16)
                sp.wait_ge(consts.sem, 48)

            @block.gpsimd
            def _(pool):
                pool.memset(kT[:, :, :, :], 0.0)
                pool.memset(vb[:, :, :, :, :, :], 0.0)
                pool.memset(tiny[:, :], 1e-24)
                pool.memset(kzero[:, :, :], 0.0)

            @block.vector
            def _(dve):
                dve.memset(va[:, :, :, :], 1.0)
                dve.wait_ge(consts.sem, 48)
                dve.tensor_copy(mask[:, 0, :], mask32[:, 0, :])
                dve.tensor_copy(mask[:, 1:TB, :], bc(mask32[:, 1, :], 1, TB - 1))

        KA = B * (1 + 2 * HALVES)
        KF = 1 + 2
        KDL = KA * TB + KF * B
        KPL = 2 * B
        with nc.Fori(0, DEPTH) as L:
            r0 = (UA + UF) * L
            with nc.Block() as block:

                @block.sync
                def _(sp):
                    for dst, src in ((wqkv[:, :], A["e_wqkv"][L]), (wo[:, :, :], A["e_wo"][L]), (w1[:, :, :], A["e_w1"][L]),
                                     (w2[:, :, :], A["e_w2"][L]), (b1[:, :], A["e_b1"][L]),
                                     (b2[:, :], A["e_b2"][L].partition_broadcast(P)), (lnp[:, :], A["e_lnp"][L]),
                                     (qks[:, 0, :], A["e_qs"][L].partition_broadcast(P)),
                                     (qks[:, 1, :], A["e_ks"][L].partition_broadcast(P))):
                        sp.dma_start(dst, src).then_inc(w_loaded.sem, 16)
                    sp.wait_ge(w_loaded.sem, w_loaded.at(16 * 9 * L + 16 * 9))
                    sp.sem_inc(stage_stored.sem, 1)

                @block.vector
                def _(dve):
                    dve.wait_ge(w_loaded.sem, w_loaded.at(16 * 9 * L + 16 * 9))
                    half = DH2 // 2
                    dve.tensor_tensor(cosl[:, :, :, :], cos0[:, :, :, :], bc(qks[:, :, :], 1, TB), ALU.mult)
                    dve.tensor_tensor(sinl[:, :, :, 0:half], sin0[:, :, :, 0:half], bc(qks[:, :, half:], 1, TB), ALU.mult)
                    dve.tensor_tensor(sinl[:, :, :, half:], sin0[:, :, :, half:], bc(qks[:, :, 0:half], 1, TB), ALU.mult)

            def unit(t, b):
                return B * t + b

            def off(t, b, n):
                t, b = t + (b + n) // B, (b + n) % B
                return (t, b) if not isinstance(t, int) or 0 <= t < TB else None

            def off_half(t, b, h, n):
                at = off(t, b, (h + n) // HALVES)
                return at and at + ((h + n) % HALVES,)

            def first_tile(t):
                return isinstance(t, int) and t == 0

            def count(x):
                return UA * L + unit(*x) + 1 if len(x) == 2 else HALVES * (UA * L + unit(*x[:2])) + x[2] + 1

            def slots(t, units=range(B)):
                for b in units:
                    for h in range(HALVES):
                        yield t, b, h

            def turns(eng, slot):
                for where in slots(-1, range(1, B)):
                    slot(*where)
                for where in slots(0):
                    slot(*where)
                with eng.Fori(1, TB - 1) as t:
                    for where in slots(t):
                        slot(*where)
                for where in slots(TB - 1):
                    slot(*where)
                for where in slots(TB, range(3)):
                    slot(*where)

            SBANK, TBANK, OBANK, QBANK, VBANK = 0, 2, 4, 5, 7

            with nc.Block() as block:

                @block.sync
                def _(sp):
                    def load(t, b):
                        z, half = c.z_ffn[b], D // 2
                        sp.dma_start(zs[:, b, 0:half], z[bass.ds(1 + P * t, P), 0:half]).then_inc(zs_loaded[b].sem, 16)
                        sp.dma_start(zs[:, b, half:D], z[bass.ds(P * t, P), half:D]).then_inc(zs_loaded[b].sem, 16)

                    def store(t, b):
                        sp.wait_ge(resid.sem, resid.at(r0 + unit(t, b) + 1))
                        sp.dma_start(c.z_attn[b, bass.ds(1 + P * t, P), :], Z[:, TB * b + t, :]).then_inc(zs_stored[b].sem, 16)

                    def loads(t):
                        for b in range(B):
                            sp.wait_ge(zsT_psum.sem, zsT_psum.at(count((t - 1, b))))
                            load(t, b)

                    for b in range(B):
                        load(0, b)
                    loads(1)
                    with sp.Fori(2, TB) as t:
                        loads(t)
                        for b in range(B):
                            store(t - 2, b)
                    for t in (TB - 2, TB - 1):
                        for b in range(B):
                            store(t, b)
                    for b in range(B):
                        sp.wait_ge(zs_stored[b].sem, 16 * TB * (L + 1))
                    sp.sem_inc(stage_stored.sem, 1)

                @block.gpsimd
                def _(pool):
                    def slot(t, b, h):
                        far = off(t, b, 2)
                        if h == 0 or not far:
                            return
                        u, par, half = count(far), far[1] % 2, DH2 // 2
                        pool.wait_ge(ss_ready.sem, ss_ready.at(u))
                        pool.tensor_tensor(rn[:, par, :], ss[:, par, :], c.neghalf[:, :], ALU.pow).then_inc(rn_ready.sem, 1)
                        if not first_tile(far[0]):
                            pool.wait_ge(s_ready.sem, s_ready.at(HALVES * (u - B)))
                            pool.tensor_tensor(kT[:, far[1], :, 0:W2], kT[:, far[1], :, P:KEYS2], kzero[:, :, :],
                                               ALU.add).then_inc(before_ready.sem, 1)
                        pool.wait_ge(qk_normed.sem, qk_normed.at(u))
                        pool.tensor_tensor(carrier[:, par:par + 1], tiny[:, 0:1], tiny[:, 0:1], ALU.add)
                        for s in range(2):
                            pool.tensor_tensor(rot[:, par, s, :, 0:half], qk[:, par, s, :, half:DH2],
                                               bc(sinl[:, far[0], s, 0:half], 1, H2), ALU.mult)
                            last = pool.tensor_tensor(rot[:, par, s, :, half:DH2], qk[:, par, s, :, 0:half],
                                                      bc(sinl[:, far[0], s, half:DH2], 1, H2), ALU.mult)
                        last.then_inc(rot_ready.sem, 1)

                    turns(pool, slot)

                @block.vector
                def _(dve):
                    steps = Steps(dve, c.dve_step, KDL * L)

                    def resid_sum(t, b):
                        dve.wait_ge(y_ready.sem, y_ready.at(count((t, b))))
                        z = Z[:, TB * b + t, :]
                        dve.tensor_tensor(z, z, c.PS[:, VBANK, 0:D], ALU.add).then_inc(resid.sem, 1)

                    def divide(t, b, h):
                        dve.wait_ge(o_psum.sem, o_psum.at(count((t, b, h))))
                        o = c.PS[:, OBANK, 0:4 * (DH2 + 1)].rearrange("p (r i e) -> p r i e", i=2, e=DH2 + 1)
                        steps(dve.reciprocal(rz[:, h, :].rearrange("p (r i) -> p r i", i=2), o[:, :, :, DH2]))
                        dve.tensor_tensor(on[:, b % 2, 4 * h:4 * h + 4, :].rearrange("p (i r) e -> p r i e", r=2),
                                          o[:, :, :, 0:DH2], bc(rz[:, h, :].rearrange("p (r i) -> p r i", i=2), 3, DH2),
                                          ALU.mult).then_inc(o_ready.sem, 1)

                    def shift(t, b, h):
                        k = count((t, b, h))
                        dve.wait_ge(s_ready.sem, s_ready.at(k))
                        s = c.PS[:, SBANK:SBANK + 2, 0:2 * KEYS2].rearrange("p b (j k) -> p b j k", k=KEYS2)
                        m = mx[:, h, :].rearrange("p (b j) -> p b j", j=2)
                        steps(dve.tensor_reduce(m, s, AX.X, ALU.max))
                        if off(t, b, -1):
                            dve.wait_ge(pT_psum.sem, pT_psum.at(k - HALVES))
                        for k0, k1 in ((0, W2), (W2, KEYS2)):
                            out = pm[:, h, 4 * k0:4 * k1].rearrange("p (b j k) -> p b j k", b=2, j=2)
                            last = dve.tensor_tensor(out, s[:, :, :, k0:k1], bc(m, 3, k1 - k0), ALU.subtract)
                        last.then_inc(p_shifted.sem, 1)

                    def square_sums(t, b):
                        par = b % 2
                        dve.wait_ge(sq_ready.sem, sq_ready.at(count((t, b))))
                        steps(dve.tensor_reduce(ss[:, par, :], sq[:, par, :, :].rearrange("p s (h e) -> p (s h) e", e=DH2),
                                                AX.X, ALU.add))
                        dve.tensor_tensor(ss[:, par, :], ss[:, par, :], tiny[:, :], ALU.max).then_inc(ss_ready.sem, 1)

                    def norm(t, b):
                        par = b % 2
                        dve.wait_ge(qk_taken.sem, qk_taken.at(count((t, b))))
                        dve.wait_ge(rn_ready.sem, rn_ready.at(count((t, b))))
                        x = qk[:, par, :, :, :].rearrange("p s h e -> p (s h) e")
                        dve.tensor_tensor(x, x, bc(rn[:, par, :], 2, DH2), ALU.mult).then_inc(qk_normed.sem, 1)

                    def by_cosine(t, b):
                        par = b % 2
                        dve.wait_ge(qk_normed.sem, qk_normed.at(count((t, b))))
                        for s in range(2):
                            last = dve.tensor_tensor(sq[:, par, s, :].rearrange("p (h e) -> p h e", e=DH2), qk[:, par, s, :, :],
                                                     bc(cosl[:, t, s, :], 1, H2), ALU.mult)
                        last.then_inc(cos_done.sem, 1)

                    def rotated(t, b):
                        u, par = count((t, b)), b % 2
                        dve.wait_ge(rot_ready.sem, rot_ready.at(u))
                        dve.wait_ge(cos_done.sem, cos_done.at(u))
                        dve.tensor_tensor(qk[:, par, :, :, :].rearrange("p s h e -> p (s h e)"),
                                          sq[:, par, :, :].rearrange("p s e -> p (s e)"),
                                          rot[:, par, :, :, :].rearrange("p s h e -> p (s h e)"), ALU.add)\
                           .then_inc(qk_ready.sem, 1)

                    def slot(t, b, h):
                        if h == 0 and off(t, b, -3):
                            resid_sum(*off(t, b, -3))
                        if off_half(t, b, h, -3):
                            divide(*off_half(t, b, h, -3))
                        if off(t, b, 0):
                            shift(t, b, h)
                        if h == 1 and off(t, b, 2):
                            norm(*off(t, b, 2))
                        if h == 0:
                            if off(t, b, 1):
                                rotated(*off(t, b, 1))
                            if off(t, b, 2):
                                square_sums(*off(t, b, 2))
                        elif off(t, b, 2):
                            by_cosine(*off(t, b, 2))

                    for where in slots(-1, range(1, B)):
                        slot(*where)
                    for where in slots(0):
                        slot(*where)
                    first = steps.k
                    with dve.Fori(1, TB - 1) as t:
                        steps.k = first + KA * (t - 1)
                        for where in slots(t):
                            slot(*where)
                    steps.k = first + KA * (TB - 2)
                    for where in slots(TB - 1):
                        slot(*where)
                    for where in slots(TB, range(3)):
                        slot(*where)
                    assert steps.k == KA * TB

                @block.scalar
                def _(act):
                    def features(t, b):
                        u = count((t, b))
                        act.wait_ge(zsT_psum.sem, zsT_psum.at(u))
                        act.activation(c.hT[:, b % 2, 0:P], c.PS[:, QBANK, 0:P], ACT.Copy).then_inc(eh_ready.sem, 1)

                    def squares(t, b):
                        act.wait_ge(eqkv_ready.sem, eqkv_ready.at(count((t, b))))
                        act.activation(sq[:, b % 2, :, :], c.PS[:, QBANK:QBANK + 2, :], ACT.Square).then_inc(sq_ready.sem, 1)
                        act.activation(qk[:, b % 2, :, :, :].rearrange("p s h e -> p s (h e)"), c.PS[:, QBANK:QBANK + 2, :],
                                       ACT.Copy).then_inc(qk_taken.sem, 1)
                        if not first_tile(t):
                            for i in range(2):
                                own = va[W2:P, b, :, :].rearrange("p (h i r) e -> p h r i e", i=2, r=2)[:, :, :, i, :]
                                last = act.activation(vb[W2 * i:W2 * i + W2, b, :, :, i, :], own, ACT.Copy)
                            last.then_inc(c.act_step.sem, 1)

                    def values(t, b):
                        if not first_tile(t):
                            act.wait_ge(c.act_step.sem, c.act_step.at((UA - B) * L + unit(t, b) - B + 1))
                        act.activation(va[:, b, :, 0:DH2], c.PS[:, VBANK, :].rearrange("p (h e) -> p h e", e=DH2),
                                       ACT.Copy).then_inc(v_evac.sem, 1)

                    def take_qk(t, b):
                        act.wait_ge(qkT_psum.sem, qkT_psum.at(count((t, b))))
                        act.activation(qT[:, b % 2, :, :].rearrange("p j q -> p (j q)"), c.PS[:, QBANK, :], ACT.Copy)
                        if not first_tile(t):
                            act.wait_ge(before_ready.sem, before_ready.at((UA - B) * L + unit(t, b) - B + 1))
                        act.activation(kT[:, b, :, W2:KEYS2], c.PS[:, QBANK + 1, :].rearrange("p (j q) -> p j q", q=P),
                                       ACT.Copy).then_inc(qkT_ready.sem, 1)

                    def take_o(t, b):
                        act.wait_ge(oT_psum.sem, oT_psum.at(count((t, b))))
                        act.activation(oT[:, b % 2, :, :].rearrange("p j q -> p (j q)"), c.PS[:, VBANK, :],
                                       ACT.Copy).then_inc(oT_ready.sem, 1)

                    def exponent(t, b, h):
                        act.wait_ge(p_shifted.sem, p_shifted.at(count((t, b, h))))
                        act.activation(pm[:, h, :], pm[:, h, :], ACT.Exp).then_inc(p_exp.sem, 1)

                    def take_p(t, b, h):
                        act.wait_ge(pT_psum.sem, pT_psum.at(count((t, b, h))))
                        act.activation(pa[:, h, :, :].rearrange("p j q -> p (j q)"), c.PS[:, TBANK, :], ACT.Copy)
                        act.activation(pb[:, h, :, :].rearrange("p r q -> p (r q)"), c.PS[:, TBANK + 1, 0:2 * P], ACT.Copy)\
                           .then_inc(pT_ready.sem, 1)

                    def slot(t, b, h):
                        ahead, back = off(t, b, 2), off_half(t, b, h, -1)
                        if h == 0:
                            if ahead:
                                features(*ahead)
                            if off(t, b, 0):
                                exponent(t, b, h)
                            if ahead:
                                squares(*ahead)
                        else:
                            if off(t, b, -2):
                                take_o(*off(t, b, -2))
                            if off(t, b, 1):
                                take_qk(*off(t, b, 1))
                            if off(t, b, 0):
                                exponent(t, b, h)
                        if h == 0 and ahead:
                            values(*ahead)
                        if back:
                            take_p(*back)

                    turns(act, slot)

                @block.tensor
                def _(pe):
                    def turn_z(t, b):
                        before = off(t, b, -2)
                        if before:
                            pe.wait_ge(qkT_ready.sem, qkT_ready.at(count(before)))
                        elif off(t, b, -1):
                            pe.wait_ge(qk_taken.sem, qk_taken.at(count(off(t, b, -1))))
                        pe.wait_ge(zs_loaded[b].sem, zs_loaded[b].at(32 * (TB * L + t) + 32))
                        pe.transpose(c.PS[:, QBANK, 0:P], zs[:, b, :], ident[:, :]).then_inc(zsT_psum.sem, 1)

                    def project(t, b):
                        pe.wait_ge(eh_ready.sem, eh_ready.at(count((t, b))))
                        for s in range(3):
                            if s == 2 and off(t, b, -5):
                                pe.wait_ge(resid.sem, resid.at(r0 + unit(*off(t, b, -5)) + 1))
                            last = pe.matmul(c.PS[:, QBANK + s, :], c.hT[:, b % 2, 0:P], wqkv[:, s * INNER:(s + 1) * INNER],
                                             start=True, stop=True)
                        last.then_inc(eqkv_ready.sem, 1)

                    def turn_qk(t, b):
                        pe.wait_ge(qk_ready.sem, qk_ready.at(count((t, b))))
                        if off(t, b, 1):
                            pe.wait_ge(qk_taken.sem, qk_taken.at(count(off(t, b, 1))))
                        for s in range(2):
                            for j in range(4):
                                last = pe.transpose(c.PS[:, QBANK + s, j * P:(j + 1) * P],
                                                    qk[:, b % 2, s, 2 * j:2 * j + 2, :].rearrange("p h e -> p (h e)"), ident[:, :])
                        last.then_inc(qkT_psum.sem, 1)

                    def scores(t, b, h):
                        back = off_half(t, b, h, -1)
                        if back:
                            pe.wait_ge(p_shifted.sem, p_shifted.at(count(back)))
                        if h == 0:
                            pe.wait_ge(qkT_ready.sem, qkT_ready.at(count((t, b))))
                        s = [c.PS[:, SBANK + r, 0:2 * KEYS2].rearrange("p (j k) -> p j k", k=KEYS2) for r in range(2)]
                        for r in range(2):
                            pe.matmul(s[r], identb[:, :], bc(mask[:, t, :], 1, 2), start=True, stop=False)
                        for j in range(2):
                            for r in range(2):
                                rows = slice(64 * r, 64 * r + 64)
                                last = pe.matmul(s[r][:, j, :], qT[rows, b % 2, 2 * h + j, :], kT[rows, b, 2 * h + j, :],
                                                 start=False, stop=(j == 1))
                        last.then_inc(s_ready.sem, 1)

                    def turn_p(t, b, h):
                        pe.wait_ge(p_exp.sem, p_exp.at(count((t, b, h))))
                        back = off_half(t, b, h, -1)
                        if back:
                            pe.wait_ge(pT_ready.sem, pT_ready.at(count(back)))
                        for j in range(4):
                            pe.transpose(c.PS[:, TBANK, j * P:(j + 1) * P], pm[:, h, 4 * W2 + j * P:4 * W2 + (j + 1) * P], ident[:, :])
                        for r in range(2):
                            last = pe.transpose(c.PS[:, TBANK + 1, r * P:(r + 1) * P], pm[:, h, r * P:(r + 1) * P], ident[:, :])
                        last.then_inc(pT_psum.sem, 1)

                    def weigh(t, b, h):
                        pe.wait_ge(pT_ready.sem, pT_ready.at(count((t, b, h))))
                        back = off_half(t, b, h, -1)
                        if back:
                            pe.wait_ge(o_ready.sem, o_ready.at(count(back)))
                        for r in range(2):
                            o = c.PS[:, OBANK, 2 * r * (DH2 + 1):2 * (r + 1) * (DH2 + 1)]
                            last = pe.matmul(o, pb[:, h, r, :], vb[:, b, h, r, :, :].rearrange("p i e -> p (i e)"),
                                             start=True, stop=False)
                            for i in range(2):
                                last = pe.matmul(o[:, i * (DH2 + 1):(i + 1) * (DH2 + 1)], pa[:, h, 2 * r + i, :],
                                                 va[:, b, 4 * h + 2 * i + r, :], start=False, stop=(i == 1))
                        last.then_inc(o_psum.sem, 1)

                    def turn_o(t, b):
                        pe.wait_ge(o_ready.sem, o_ready.at(count((t, b, HALVES - 1))))
                        if off(t, b, 4):
                            pe.wait_ge(v_evac.sem, v_evac.at(count(off(t, b, 4))))
                        if off(t, b, -1):
                            pe.wait_ge(resid.sem, resid.at(r0 + unit(*off(t, b, -1)) + 1))
                        for j in range(4):
                            last = pe.transpose(c.PS[:, VBANK, j * P:(j + 1) * P],
                                                on[:, b % 2, 2 * j:2 * j + 2, :].rearrange("p h e -> p (h e)"), ident[:, :])
                        last.then_inc(oT_psum.sem, 1)

                    def project_o(t, b):
                        pe.wait_ge(oT_ready.sem, oT_ready.at(count((t, b))))
                        for j in range(4):
                            last = pe.matmul(c.PS[:, VBANK, 0:D], oT[:, b % 2, j, :], wo[:, j, :], start=(j == 0), stop=(j == 3))
                        last.then_inc(y_ready.sem, 1)

                    def slot(t, b, h):
                        if off(t, b, 0):
                            scores(t, b, h)
                        if h == 0 and off(t, b, 2):
                            project(*off(t, b, 2))
                        if h == 1 and off(t, b, -2):
                            turn_o(*off(t, b, -2))
                        if h == 1 and off(t, b, 1):
                            turn_qk(*off(t, b, 1))
                        if off_half(t, b, h, -1):
                            turn_p(*off_half(t, b, h, -1))
                        if off_half(t, b, h, -2):
                            weigh(*off_half(t, b, h, -2))
                        if h == 1 and off(t, b, -2):
                            project_o(*off(t, b, -2))
                        if h == 1 and off(t, b, 3):
                            turn_z(*off(t, b, 3))

                    turns(pe, slot)

            with nc.Block() as block:

                @block.sync
                def _(sp):
                    def load(n, st):
                        z, half = c.z_attn[n], D // 2
                        for d0, before in ((0, 1), (half, 0)):
                            src = z[bass.ds(before + GT * st, GT), d0:d0 + half].rearrange("(t p) d -> p t d", p=P)
                            sp.dma_start(zg[:, st, :, d0:d0 + half], src).then_inc(zg_loaded[st].sem, 16)

                    def store(n, st):
                        sp.wait_ge(resid.sem, resid.at(r0 + UA + 2 * n + st + 1))
                        sp.dma_start(c.z_ffn[n, bass.ds(1 + GT * st, GT), :].rearrange("(t p) d -> p t d", p=P),
                                     Z[:, bass.ds(TB * n + G4 * st, G4), :]).then_inc(zg_stored[st].sem, 16)

                    for st in STREAMS:
                        load(0, st)
                    with sp.Fori(1, B) as n:
                        for st in STREAMS:
                            sp.wait_ge(c.xn_ready.sem, c.xn_ready.at(UF * L + 2 * n + st - 1))
                            load(n, st)
                        for st in STREAMS:
                            store(n - 1, st)
                    for st in STREAMS:
                        store(B - 1, st)
                    for st in STREAMS:
                        sp.wait_ge(zg_stored[st].sem, 16 * B * (L + 1))
                    sp.sem_inc(stage_stored.sem, 1)

                @block.gpsimd
                def _(pool):
                    with pool.Fori(0, B) as n:
                        c.ln_rstd(pool, Chain(pool, c.pool_step, KPL * L + 2 * n), UF * L + 2 * n, G4)

                @block.vector
                def _(dve):
                    with dve.Fori(0, B) as n:
                        u = UF * L + 2 * n
                        chain = Chain(dve, c.dve_step, KDL * L + KA * TB + KF * n)
                        tiles = [[zg[:, st, i, :] for i in range(G4)] for st in STREAMS]
                        for st in STREAMS:
                            dve.wait_ge(zg_loaded[st].sem, zg_loaded[st].at(32 * (B * L + n) + 32))
                        c.ln_stats(dve, chain, tiles)
                        c.ln_apply(dve, u, tiles)
                        for j in range(HC):
                            for st in STREAMS:
                                dve.wait_ge(gelu_ready.sem, gelu_ready.at(HC * u + 2 * j + st + 1))
                                dve.scalar_tensor_tensor(uu[:, st, j, :], bank(st, 1), b1[:, j:j + 1], gate[:, st, :],
                                                         ALU.add, ALU.mult).then_inc(u_ready.sem, 1)
                        for st in STREAMS:
                            dve.wait_ge(fy_ready.sem, fy_ready.at(u + st + 1))
                            z = Z[:, bass.ds(TB * n + G4 * st, G4), :]
                            chain(dve.tensor_tensor(z, z, bank(st, 3).rearrange("p (t d) -> p t d", d=D), ALU.add))
                            dve.tensor_tensor(z, z, bc(b2[:, :], 1, G4), ALU.add).then_inc(resid.sem, 1)
                        assert chain.k == KF

                @block.scalar
                def _(act):
                    with act.Fori(0, B) as n:
                        u = UF * L + 2 * n
                        for st in STREAMS:
                            act.wait_ge(c.xnT_ready.sem, c.xnT_ready.at(u + st + 1))
                            act.activation(c.hT[:, st, :], bank(st, 0), ACT.Identity, scale=lnp[:, 1:2],
                                           bias=lnp[:, 0:1]).then_inc(c.hT_ready.sem, 1)
                        for j in range(HC):
                            for st in STREAMS:
                                act.wait_ge(ag_ready.sem, ag_ready.at(HC * u + 2 * j + st + 1))
                                act.activation(gate[:, st, :], bank(st, 2), ACT.Gelu, bias=b1[:, HC + j:HC + j + 1])\
                                   .then_inc(gelu_ready.sem, 1)

                @block.tensor
                def _(pe):
                    with pe.Fori(0, B) as n:
                        u = UF * L + 2 * n
                        c.ln_transpose(pe, u, G4, resid=r0 + UA + 2 * n - 1)
                        for j in range(HC):
                            for st in STREAMS:
                                if j == 0:
                                    pe.wait_ge(c.hT_ready.sem, c.hT_ready.at(u + st + 1))
                                else:
                                    pe.wait_ge(u_ready.sem, u_ready.at(HC * u + 2 * (j - 1) + st + 1))
                                pe.matmul(bank(st, 1), w1[:, j, :], c.hT[:, st, :], start=True, stop=True)
                                pe.matmul(bank(st, 2), w1[:, HC + j, :], c.hT[:, st, :], start=True, stop=True)\
                                  .then_inc(ag_ready.sem, 1)
                        for st in STREAMS:
                            pe.wait_ge(u_ready.sem, u_ready.at(HC * u + 2 * (HC - 1) + st + 1))
                            for i in range(G4):
                                for j in range(HC):
                                    last = pe.matmul(bank(st, 3)[:, i * P:(i + 1) * P], uu[:, st, j, i * P:(i + 1) * P], w2[:, j, :],
                                                     start=(j == 0), stop=(j == HC - 1))
                            last.then_inc(fy_ready.sem, 1)
        c.ln_advance(UF * DEPTH)
        resid.base += DEPTH * (UA + UF)


def finish(c, Z, out):
    nc, X = c.nc, c.X
    gated, summed, stored = c.counter("gated"), c.counter("summed"), c.counter("stored")

    def batch(t, b):
        return t[:, TB * b:TB * (b + 1), :]

    with nc.Block() as block:

        @block.vector
        def _(dve):
            for b in range(B):
                dve.tensor_tensor(batch(Z, b), batch(Z, b), bc(c.rowB[:, c.L1GB, b, :], 1, TB), ALU.mult).then_inc(gated.sem, 1)
            for b in range(B):
                dve.wait_ge(gated.sem, b + 1)
                dve.tensor_tensor(batch(X, b), batch(X, b), batch(Z, b), ALU.add).then_inc(summed.sem, 1)

        @block.sync
        def _(sp):
            for b in range(B):
                sp.wait_ge(summed.sem, b + 1)
                sp.dma_start(out[b].rearrange("(t p) d -> p t d", p=P), batch(X, b)).then_inc(stored.sem, 16)
            sp.wait_ge(stored.sem, 16 * B)


def build(nc, A, out):
    with ExitStack() as ctx:
        c = Core(nc, ctx)
        setup(c, A)
        linear_attention(c, A)
        moe(c, A)
        windowed_attention(c, A)
        Z = c.sb("Z", [P, NT, D])
        start_stream(c, A, Z)
        local_transformer(c, A, Z)
        finish(c, Z, out)


KDA = 26
KDR = 21


def constants():
    c = {"c_ident": np.eye(P, dtype=np.float32)}
    h = np.arange(P) // DH0
    c["c_bmask"] = ((h[:, None] == h[None, :]) * S0).astype(np.float32)
    row, col = np.arange(3 * E) % E, np.arange(NJ * P) // INTER
    c["c_sel"] = (row[:, None] == col[None, :]).astype(np.float32).reshape(3 * E, NJ, P)
    c["c_hmask"] = (np.arange(P)[:, None] // DH1 % 4 == np.arange(4)[None, :]).astype(np.float32)
    q, k = np.arange(P)[:, None], np.arange(P)[None, :]
    before, pre = np.arange(W1)[None, :] - W1, np.arange(PRE)[None, :] + 0 * q
    own = (k <= q) & (q - k < W1)
    first = np.concatenate([before + 0 * q > 0, pre < 0, own | ((k <= q) & (k < PRE))], 1)
    other = np.concatenate([q - before < W1, pre >= 0, own], 1)
    own2 = (k <= q) & (q - k <= W2)
    before2 = np.arange(W2)[None, :] - W2
    first2, other2 = np.concatenate([before2 + 0 * q > 0, own2], 1), np.concatenate([q - before2 <= W2, own2], 1)
    c["c_mask2"] = np.where(np.stack([first2, other2], 1), 0.0, NEG).astype(np.float32)
    f = np.float32
    idx = np.arange(0, DH2, 2, dtype=f)
    inv_freq = f(1.0) / f(10000.0) ** (idx / f(DH2))
    pos = np.arange(S, dtype=f)
    freqs = pos[:, None] * inv_freq[None, :]
    base = (idx + f(0.4 * DH2)) / f(1.4 * DH2)
    xpos = base[None, :] ** ((pos - f(S // 2)) / f(W2 // 2))[:, None]
    cos, sin = np.cos(freqs), np.sin(freqs)
    cos, sin = np.concatenate([cos, cos], 1), np.concatenate([-sin, sin], 1)
    xpos = np.concatenate([xpos, xpos], 1)
    for name, tab in (("c_cos", cos), ("c_sin", sin)):
        both = np.stack([f(8.0) * tab * xpos, tab / xpos], 1).astype(f)
        c[name] = both.reshape(TB, P, 2, DH2).transpose(1, 0, 2, 3)
    c["c_mask1"] = np.where(np.stack([first, other], 1), 0.0, NEG).astype(np.float32)
    return c


def moe_layout(i):
    none = np.zeros((P - INTER, D), np.float32)
    up = lambda w, ws: np.concatenate([w.reshape(E * INTER, D), ws, none], 0).T
    down = np.concatenate([i["L0_ffn_w2"].transpose(0, 2, 1).reshape(E * INTER, D), i["L0_ffn_ws2"].T, none], 0)
    return {"gwT": i["L0_ffn_gate_w"].T, "L0_ffn_gate_bias": i["L0_ffn_gate_bias"],
            "w1T": up(i["L0_ffn_w1"], i["L0_ffn_ws1"]), "w3T": up(i["L0_ffn_w3"], i["L0_ffn_ws3"]),
            "w2T": down.reshape(NJ + 1, P, D).transpose(1, 0, 2)}


def local_layout(i):
    n = HC * P - HID

    def halves(w):
        w = w.reshape(w.shape[:-1] + (2, HID))
        w = np.pad(w, [(0, 0)] * (w.ndim - 1) + [(0, n)])
        return w.reshape(w.shape[:-2] + (2 * HC, P))

    w2 = np.pad(i["L1_ffn_w2"], [(0, 0), (0, n), (0, 0)])
    return {"e_wqkv": i["L1_ffn_wqkv"],
            "e_wo": i["L1_ffn_wo"].reshape(DEPTH, INNER // P, P, D).transpose(0, 2, 1, 3),
            "e_w1": halves(i["L1_ffn_w1"]), "e_b1": halves(i["L1_ffn_b1"]).transpose(0, 2, 1),
            "e_w2": w2.reshape(DEPTH, HC, P, D).transpose(0, 2, 1, 3), "e_b2": i["L1_ffn_b2"],
            "e_lnp": np.stack([i["L1_ffn_ln_b"], i["L1_ffn_ln_g"]], -1),
            "e_qs": i["L1_ffn_q_scale"], "e_ks": i["L1_ffn_k_scale"]}


def layout(i):
    a = {"L0_attn_x": i["L0_attn_x"], "L0_wmod": i["L0_wmod"], "L1_wmod": i["L1_wmod"],
         "L0_cT": i["L0_c"].T, "L1_cT": i["L1_c"].T,
         "a_wqv": np.concatenate([i["L0_attn_Wq"], i["L0_attn_Wv"]], 1),
         "a_bqv": np.concatenate([i["L0_attn_bq"], i["L0_attn_bv"]]),
         "L0_attn_Wo": i["L0_attn_Wo"], "L0_attn_bo": i["L0_attn_bo"]}
    a.update(moe_layout(i))
    a.update(local_layout(i))
    a.update({"d_wqkvT": i["L1_attn_w_qkv"].T, "d_woutT": i["L1_attn_w_out"].T})
    return a


def kernel(**inputs):
    import concourse.bacc as bacc
    from concourse.bass_utils import run_bass_kernel_spmd

    nc = bacc.Bacc("TRN2", target_bir_lowering=False, num_devices=1)
    arrays, args = {}, {}
    host = {k: np.asarray(v) for k, v in inputs.items()}
    for name, a in {**layout(host), **constants()}.items():
        arrays[f"in_{name}"] = a = np.ascontiguousarray(a)
        args[name] = nc.dram_tensor(f"in_{name}", a.shape, mybir.dt.from_np(a.dtype), kind="ExternalInput").ap()
    out = nc.dram_tensor("out_x", (B, S, D), F32, kind="ExternalOutput").ap()
    build(nc, args, out)
    r = run_bass_kernel_spmd(nc, [arrays], core_ids=[0])
    return r.results[0]["out_x"]
```

```python
from contextlib import ExitStack

import numpy as np
import concourse.bass as bass
from concourse import mybir

F32 = mybir.dt.float32
BF16 = mybir.dt.bfloat16
F32R = mybir.dt.float32r
ALU = mybir.AluOpType
ACT = mybir.ActivationFunctionType
AX = mybir.AxisListType

P = 128
B, S, D = 4, 1024, 128
TB = S // P
NT = B * TB
G4 = 4
GT = G4 * P
EPS = 1e-5
STREAMS = (0, 1)
NEG = -1e30

H0, DH0 = 16, 8
S0 = float((DH0 ** 0.5) ** -0.25)
E, INTER, TOPK, NG, TOPG = 16, 64, 4, 4, 2
EG = E // NG
NJ = E * INTER // P
H1, DH1, W1, PRE = 16, 8, 64, 16
KEYS1 = W1 + PRE + P
KB1 = W1 + PRE
DEPTH, H2, DH2, W2 = 2, 8, 64, 64
INNER = H2 * DH2
KEYS2 = W2 + P
HID = int(D * 4 * 2 / 3)
HC = -(-HID // P)


class Signal:

    def __init__(self, sem, base=0):
        self.sem, self.base = sem, base

    def at(self, n):
        return self.base + n


class Chain:

    def __init__(self, eng, signal, start):
        self.eng, self.counter, self.start, self.k = eng, signal, start, 0

    def __call__(self, ins):
        self.k += 1
        ins.then_inc(self.counter.sem, 1)
        self.eng.wait_ge(self.counter.sem, self.counter.base + self.start + self.k)


class Steps:

    def __init__(self, eng, signal, start=0):
        self.eng, self.counter, self.start, self.k = eng, signal, start, 0

    def __call__(self, ins):
        self.k = self.k + 1
        ins.then_inc(self.counter.sem, 1)
        self.eng.wait_ge(self.counter.sem, self.counter.at(self.start + self.k))


def bc(ap, axis, n):
    a = ap.unsqueeze(axis)
    shape = list(a.shape)
    shape[axis] = n
    return a.broadcast_to(shape)


class Core:

    L0GA, L1GA, L1SB, L1CB, L1GB = range(5)

    def __init__(self, nc, ctx):
        self.nc, self.ctx = nc, ctx
        sb = self.sb
        self.X = sb("X", [P, NT, D])
        self.ident = sb("ident", [P, P])
        self.identb = sb("identb", [P, P], BF16)
        self.neghalf = sb("neghalf", [P, 2 * H2])
        self.epsv = sb("epsv", [P, G4])
        self.carrier = sb("carrier", [P, 1])
        self.modc = sb("modc", [P, 2, 2])
        self.modT = sb("modT", [P, 2, 6, B])
        self.gbT = sb("gbT", [P, B])
        self.rowB = sb("rowB", [P, 5, B, D])
        self.PS = ctx.enter_context(nc.psum_tensor("PS", [P, 8, 512], F32))
        self.z_attn = nc.dram_tensor("z_attn", [B, S + 1, D], F32, kind="Internal").ap()
        self.z_ffn = nc.dram_tensor("z_ffn", [B, S + 1, D], F32, kind="Internal").ap()

        signal = self.counter
        self.dve_step, self.act_step, self.pool_step = signal("dve_step"), signal("act_step"), signal("pool_step")
        self.stats_ready, self.rstd_ready = signal("stats_ready"), signal("rstd_ready")
        self.xn_ready, self.xnT_ready, self.hT_ready = signal("xn_ready"), signal("xnT_ready"), signal("hT_ready")
        self.resid_done = signal("resid_done")
        self.x_loaded = signal("x_loaded")

        self.stat6 = sb("stat6", [P, 2, G4, 6])
        self.meanvar = sb("meanvar", [P, 2, G4, 2])
        self.vareps = sb("vareps", [P, 2, G4])
        self.rstd = sb("rstd", [P, 2, G4])
        self.xn = sb("xn", [P, 2, G4, D])
        self.hT = sb("hT", [P, 2, GT])

    def sb(self, name, shape, dt=F32, ctx=None):
        return (ctx or self.ctx).enter_context(self.nc.sbuf_tensor(name, shape, dt))

    def counter(self, name, base=0):
        return Signal(self.ctx.enter_context(self.nc.semaphore(name)), base)

    def bank(self, st, k, n=1):
        if n == 1:
            return self.PS[:, 4 * st + k, :]
        return self.PS[:, 4 * st + k:4 * st + k + n, :]

    def ln_stats(self, dve, chain, tiles):
        for st in STREAMS:
            for i, tile in enumerate(tiles[st]):
                last = dve.bn_stats(self.stat6[:, st, i, :], tile)
        chain(last)
        dve.memset(self.carrier[:, :], 0.0)
        for st in STREAMS:
            for i, tile in enumerate(tiles[st]):
                last = dve.bn_aggr(self.meanvar[:, st, i, :], self.stat6[:, st, i, :])
            last.then_inc(self.stats_ready.sem, 1)

    def ln_rstd(self, pool, chain, u, n):
        for st in STREAMS:
            pool.wait_ge(self.stats_ready.sem, self.stats_ready.at(u + st + 1))
            chain(pool.tensor_tensor(self.vareps[:, st, 0:n], self.meanvar[:, st, 0:n, 1], self.epsv[:, 0:n], ALU.add))
            pool.tensor_tensor(self.rstd[:, st, 0:n], self.vareps[:, st, 0:n], self.neghalf[:, 0:n],
                               ALU.pow).then_inc(self.rstd_ready.sem, 1)

    def ln_apply(self, dve, u, tiles):
        for st in STREAMS:
            dve.wait_ge(self.rstd_ready.sem, self.rstd_ready.at(u + st + 1))
            for i, tile in enumerate(tiles[st]):
                last = dve.tensor_scalar(self.xn[:, st, i, :], tile, self.meanvar[:, st, i, 0:1],
                                         self.rstd[:, st, i:i + 1], ALU.subtract, ALU.mult)
            last.then_inc(self.xn_ready.sem, 1)

    def ln_transpose(self, pe, u, n, resid=None):
        for st in STREAMS:
            if resid is not None:
                pe.wait_ge(self.resid_done.sem, self.resid_done.at(resid + st))
            pe.wait_ge(self.xn_ready.sem, self.xn_ready.at(u + st + 1))
            for i in range(n):
                last = pe.transpose(self.bank(st, 0)[:, i * P:(i + 1) * P], self.xn[:, st, i, :], self.ident[:, :])
            last.then_inc(self.xnT_ready.sem, 1)

    def mod_of_batch(self, act, turn, l, k, batches, units=None):
        if units is not None:
            act.wait_ge(self.hT_ready.sem, self.hT_ready.at(units))
        for st in STREAMS:
            last = act.activation(self.modc[:, st, :], self.modT[:, l, k:k + 2, batches[st]], ACT.Copy)
        last.then_inc(self.act_step.sem, 1)
        act.wait_ge(self.act_step.sem, self.act_step.at(turn + 1))

    def ln_advance(self, units):
        for s in (self.stats_ready, self.rstd_ready, self.xn_ready, self.xnT_ready, self.hT_ready):
            s.base += units


def setup(c, A):
    nc, X, PS, bank, ident, identb, signal = c.nc, c.X, c.PS, c.bank, c.ident, c.identb, c.counter
    with ExitStack() as sc:
        def ssb(name, shape, dt=F32):
            return sc.enter_context(nc.sbuf_tensor(name, shape, dt))

        cT = ssb("cT", [P, 2, B])
        cs = ssb("cs", [P, 2, B])
        csB = ssb("csB", [P, 2, B, P])
        wmod = ssb("wmod", [P, 2, 6 * D])
        sgn = ssb("sgn", [P, B, D])
        zrow = ssb("zrow", [B, D])
        gb_abs = ssb("gb_abs", [P, B])
        mod_done = signal("mod_done")
        zero_stored = signal("zero_stored")
        loaded = signal("loaded")
        with nc.Block() as block:

            @block.sync
            def _(sp):
                for dst, src in ((ident[:, :], A["c_ident"]), (cT[:, 0, :], A["L0_cT"]), (cT[:, 1, :], A["L1_cT"]),
                                 (wmod[:, 0, :], A["L0_wmod"]), (wmod[:, 1, :], A["L1_wmod"])):
                    sp.dma_start(dst, src).then_inc(loaded.sem, 16)
                for b in range(B):
                    sp.dma_start(X[:, TB * b:TB * (b + 1), :],
                                 A["L0_attn_x"][b].rearrange("(t p) d -> p t d", p=P)).then_inc(c.x_loaded.sem, 16)
                sp.wait_ge(c.dve_step.sem, 1)
                for z in (c.z_attn, c.z_ffn):
                    sp.dma_start(z[:, 0, :], zrow[:, :]).then_inc(zero_stored.sem, 16)
                sp.wait_ge(zero_stored.sem, 32)

            @block.scalar
            def _(act):
                act.wait_ge(loaded.sem, 16 * 5)
                act.activation(cs[:, :, :], cT[:, :, :], ACT.Silu).then_inc(c.act_step.sem, 1)
                act.wait_ge(mod_done.sem, 1)
                act.wait_ge(c.dve_step.sem, 3)
                for l in range(2):
                    for k in range(6):
                        c0 = 256 + (6 * l + k) * B
                        last = act.activation(c.modT[:, l, k, :], PS[:, 4, c0:c0 + B], ACT.Copy,
                                              bias=float(k in (1, 4)))
                last.then_inc(c.act_step.sem, 1)

            @block.vector
            def _(dve):
                dve.memset(zrow[:, :], 0.0).then_inc(c.dve_step.sem, 1)
                dve.memset(c.neghalf[:, :], -0.5)
                dve.memset(c.epsv[:, :], EPS)
                dve.wait_ge(c.act_step.sem, 1)
                dve.tensor_copy(csB[:, :, :, :].rearrange("p a b c -> p (a b) c"),
                                bc(cs[:, :, :].rearrange("p a b -> p (a b)"), 2, P)).then_inc(c.dve_step.sem, 1)
                dve.tensor_copy(identb[:, :], ident[:, :])
                dve.wait_ge(mod_done.sem, 1)
                for b in range(B):
                    dve.tensor_copy(c.rowB[:, 1:5, b, :],
                                    PS[:, b, :].rearrange("p (k d) -> p k d", d=D))
                    last = dve.tensor_copy(c.rowB[:, 0, b, :], PS[:, 4 + b, 0:D])
                chain = Chain(dve, c.dve_step, 2)
                chain(last)
                ga = c.rowB[:, c.L0GA, :, :]
                chain(dve.tensor_scalar(sgn[:, :, :], ga, 0.0, 2.0, ALU.is_ge, ALU.mult))
                chain(dve.tensor_scalar(sgn[:, :, :], sgn[:, :, :], 1.0, None, ALU.subtract))
                chain(dve.tensor_tensor(ga, ga, sgn[:, :, :], ALU.mult))
                dve.scalar_tensor_tensor(ga.rearrange("p a b -> p (a b)"), ga.rearrange("p a b -> p (a b)"), 0.25,
                                         sgn[:, :, :].rearrange("p a b -> p (a b)"), ALU.max, ALU.mult)
                dve.wait_ge(c.act_step.sem, 2)
                chain(dve.tensor_scalar(c.gbT[:, :], c.modT[:, 0, 5, :], 0.0, 2.0, ALU.is_ge, ALU.mult))
                chain(dve.tensor_scalar(c.gbT[:, :], c.gbT[:, :], 1.0, None, ALU.subtract))
                chain(dve.tensor_tensor(gb_abs[:, :], c.gbT[:, :], c.modT[:, 0, 5, :], ALU.mult))
                dve.scalar_tensor_tensor(c.gbT[:, :], gb_abs[:, :], 0.25, c.gbT[:, :], ALU.max, ALU.mult)

            @block.tensor
            def _(pe):
                pe.wait_ge(c.dve_step.sem, 2)
                for b in range(B):
                    pe.matmul(PS[:, b, :], csB[:, 1, b, :], wmod[:, 1, 2 * D:6 * D], start=True, stop=True)
                    pe.matmul(PS[:, 4 + b, 0:D], csB[:, 0, b, :], wmod[:, 0, 2 * D:3 * D], start=True, stop=True)
                for l in range(2):
                    for k in range(6):
                        c0 = 256 + (6 * l + k) * B
                        last = pe.matmul(PS[:, 4, c0:c0 + B], wmod[:, l, k * D:(k + 1) * D], cs[:, l, :],
                                         start=True, stop=True)
                last.then_inc(mod_done.sem, 1)
            c.act_step.base += 2
        c.dve_step.base += 9

def linear_attention(c, A):
    nc, X, PS, bank, ident, identb, signal = c.nc, c.X, c.PS, c.bank, c.ident, c.identb, c.counter
    with ExitStack() as sc:
        def ssb(name, shape, dt=F32):
            return sc.enter_context(nc.sbuf_tensor(name, shape, dt))

        wqv = ssb("wqv", [P, 2 * D])
        bqv = ssb("bqv", [P, 2 * D])
        wo = ssb("wo", [P, D])
        bo = ssb("bo", [P, D])
        bmask = ssb("bmask", [P, P])
        q = ssb("q", [P, 2, G4, D])
        ek = ssb("ek", [P, 2, G4, D])
        v = ssb("v", [P, 2, G4, D + 1])
        qT = ssb("qT", [P, 2, 2, GT])
        mx = ssb("mx", [P, 2, G4 * H0])
        rs = ssb("rs", [P, 2, G4 * H0])
        rk = ssb("rk", [P, 2])
        cx = ssb("cx", [P, 2, D])
        cxT = ssb("cxT", [P, 2, D])
        wctx = ssb("wctx", [P, 2, D])
        bog = ssb("bog", [P, 2, D])
        w_loaded = signal("w_loaded")
        consts = signal("a_consts")
        qv_ready, shifted, exp_ready = signal("qv_ready"), signal("q_shifted"), signal("exp_ready")
        q_soft, qT_psum, ek_ready, qT_ready = signal("q_soft"), signal("qT_psum"), signal("ek_ready"), signal("qT_ready")
        v_ready, ctx_ready = signal("v_ready"), signal("ctx_ready")
        ctx_scaled, ctxT_psum, ctxT_ready = signal("ctx_scaled"), signal("ctxT_psum"), signal("ctxT_ready")
        wctx_psum, wctx_ready, y_ready = signal("wctx_psum"), signal("wctx_ready"), signal("y_ready")

        def tiles(bi, g):
            return [[X[:, 16 * bi + 8 * st + 4 * g + i, :] for i in range(G4)] for st in STREAMS]

        KP = 2 * 2
        with nc.Block() as block:

            @block.sync
            def _(sp):
                for dst, src in ((wqv[:, :], A["a_wqv"]), (bqv[:, :], A["a_bqv"].partition_broadcast(P)),
                                 (wo[:, :], A["L0_attn_Wo"]), (bo[:, :], A["L0_attn_bo"].partition_broadcast(P)),
                                 (bmask[:, :], A["c_bmask"])):
                    sp.dma_start(dst, src).then_inc(w_loaded.sem, 16)

            @block.gpsimd
            def _(pool):
                with pool.Fori(0, 2) as bi:
                    chain = Chain(pool, c.pool_step, bi * KP)
                    for g in range(2):
                        c.ln_rstd(pool, chain, 4 * bi + 2 * g, G4)
                    assert chain.k == KP

            @block.vector
            def _(dve):
                for st in STREAMS:
                    last = dve.memset(v[:, st, :, D:D + 1], 1.0)
                last.then_inc(consts.sem, 1)
                dve.wait_ge(c.x_loaded.sem, 16 * B)
                with dve.Fori(0, 2) as bi:
                    chain = Chain(dve, c.dve_step, bi * KDA)
                    for g in range(2):
                        u = 4 * bi + 2 * g
                        if g == 0:
                            c.ln_stats(dve, chain, tiles(bi, 0))
                            c.ln_apply(dve, u, tiles(bi, 0))
                            c.ln_stats(dve, chain, tiles(bi, 1))
                            dve.wait_ge(w_loaded.sem, 16 * 5)
                        for st in STREAMS:
                            dve.wait_ge(qv_ready.sem, qv_ready.at(u + st + 1))
                            qv = bank(st, 1, 2).rearrange("p b (t c) -> p (b t) c", c=2 * D)
                            chain(dve.tensor_tensor(q[:, st, :, :], qv[:, :, 0:D], bc(bqv[:, 0:D], 1, G4), ALU.add))
                            dve.tensor_tensor(v[:, st, :, 0:D], qv[:, :, D:2 * D], bc(bqv[:, D:2 * D], 1, G4),
                                              ALU.add).then_inc(v_ready.sem, 1)
                            qh = q[:, st, :, :].rearrange("p t (h e) -> p (t h) e", e=DH0)
                            chain(dve.tensor_reduce(mx[:, st, :], qh, AX.X, ALU.max))
                            dve.tensor_tensor(qh, qh, bc(mx[:, st, :], 2, DH0), ALU.subtract)\
                               .then_inc(shifted.sem, 1)
                        if g == 0:
                            c.ln_apply(dve, u + 2, tiles(bi, 1))
                        for st in STREAMS:
                            dve.wait_ge(exp_ready.sem, exp_ready.at(u + st + 1))
                            qh = q[:, st, :, :].rearrange("p t (h e) -> p (t h) e", e=DH0)
                            chain(dve.tensor_reduce(rs[:, st, :], qh, AX.X, ALU.add))
                            chain(dve.reciprocal(rs[:, st, :], rs[:, st, :]))
                            dve.tensor_tensor(qh, qh, bc(rs[:, st, :], 2, DH0), ALU.mult).then_inc(q_soft.sem, 1)
                    for st in STREAMS:
                        dve.wait_ge(ctx_ready.sem, ctx_ready.at(2 * bi + st + 1))
                        chain(dve.reciprocal(rk[:, st:st + 1], bank(st, 3)[:, D:D + 1]))
                        dve.scalar_tensor_tensor(cx[:, st, :], bank(st, 3)[:, 0:D], rk[:, st:st + 1], bmask[:, :],
                                                 ALU.mult, ALU.mult).then_inc(ctx_scaled.sem, 1)
                    for st in STREAMS:
                        ga = c.rowB[:, c.L0GA, 2 * bi + st, :]
                        dve.wait_ge(wctx_psum.sem, wctx_psum.at(2 * bi + st + 1))
                        dve.tensor_tensor(wctx[:, st, :], bank(st, 3)[:, 0:D], ga, ALU.mult)\
                           .then_inc(wctx_ready.sem, 1)
                        chain(dve.tensor_tensor(bog[:, st, :], bo[:, :], ga, ALU.mult))
                    for g in range(2):
                        for st in STREAMS:
                            dve.wait_ge(y_ready.sem, y_ready.at(4 * bi + 2 * g + st + 1))
                            xt = X[:, bass.ds(16 * bi + 8 * st + 4 * g, G4), :]
                            y = bank(st, 1 + g).rearrange("p (t d) -> p t d", d=D)
                            chain(dve.tensor_tensor(xt, xt, y, ALU.add))
                            dve.tensor_tensor(xt, xt, bc(bog[:, st, :], 1, G4), ALU.add).then_inc(c.resid_done.sem, 1)
                    assert chain.k == KDA

            @block.scalar
            def _(act):
                with act.Fori(0, 2) as bi:
                    c.mod_of_batch(act, bi, 0, 0, [2 * bi, 2 * bi + 1])
                    for g in range(2):
                        u = 4 * bi + 2 * g
                        for st in STREAMS:
                            act.wait_ge(c.xnT_ready.sem, c.xnT_ready.at(u + st + 1))
                            act.activation(c.hT[:, st, :], bank(st, 0), ACT.Identity,
                                           scale=c.modc[:, st, 1:2], bias=c.modc[:, st, 0:1]).then_inc(c.hT_ready.sem, 1)
                        for st in STREAMS:
                            act.wait_ge(shifted.sem, shifted.at(u + st + 1))
                            act.activation(q[:, st, :, :], q[:, st, :, :], ACT.Exp).then_inc(exp_ready.sem, 1)
                        for st in STREAMS:
                            act.wait_ge(q_soft.sem, q_soft.at(u + st + 1))
                            act.activation(ek[:, st, :, :], q[:, st, :, :], ACT.Exp, scale=S0)\
                               .then_inc(ek_ready.sem, 1)
                            act.wait_ge(qT_psum.sem, qT_psum.at(u + st + 1))
                            act.activation(qT[:, st, g, :], bank(st, 0), ACT.Copy, scale=S0)\
                               .then_inc(qT_ready.sem, 1)
                    for st in STREAMS:
                        act.wait_ge(ctxT_psum.sem, ctxT_psum.at(2 * bi + st + 1))
                        act.activation(cxT[:, st, :], bank(st, 0)[:, 0:D], ACT.Copy).then_inc(ctxT_ready.sem, 1)

            @block.tensor
            def _(pe):
                pe.wait_ge(w_loaded.sem, 16 * 5)
                pe.wait_ge(consts.sem, 1)
                with pe.Fori(0, 2) as bi:
                    for g in range(2):
                        u = 4 * bi + 2 * g
                        if g == 1:
                            pe.wait_ge(qT_ready.sem, qT_ready.at(4 * bi + 2))
                        c.ln_transpose(pe, u, G4)
                        for st in STREAMS:
                            pe.wait_ge(c.hT_ready.sem, c.hT_ready.at(u + st + 1))
                            for i in range(G4):
                                last = pe.matmul(bank(st, 1 + i // 2)[:, (i % 2) * 256:(i % 2) * 256 + 256],
                                                 c.hT[:, st, i * P:(i + 1) * P], wqv[:, :], start=True, stop=True)
                            last.then_inc(qv_ready.sem, 1)
                        for st in STREAMS:
                            pe.wait_ge(q_soft.sem, q_soft.at(u + st + 1))
                            for i in range(G4):
                                last = pe.transpose(bank(st, 0)[:, i * P:(i + 1) * P], q[:, st, i, :], ident[:, :])
                            last.then_inc(qT_psum.sem, 1)
                            pe.wait_ge(ek_ready.sem, ek_ready.at(u + st + 1))
                            pe.wait_ge(v_ready.sem, v_ready.at(u + st + 1))
                            for i in range(G4):
                                last = pe.matmul(bank(st, 3)[:, 0:D + 1], ek[:, st, i, :], v[:, st, i, :],
                                                 start=(g == 0 and i == 0), stop=(g == 1 and i == G4 - 1))
                            if g == 1:
                                last.then_inc(ctx_ready.sem, 1)
                    for st in STREAMS:
                        pe.wait_ge(ctx_scaled.sem, ctx_scaled.at(2 * bi + st + 1))
                        pe.wait_ge(qT_ready.sem, qT_ready.at(4 * bi + 2 + st + 1))
                        pe.transpose(bank(st, 0)[:, 0:D], cx[:, st, :], ident[:, :]).then_inc(ctxT_psum.sem, 1)
                    for st in STREAMS:
                        pe.wait_ge(ctxT_ready.sem, ctxT_ready.at(2 * bi + st + 1))
                        pe.matmul(bank(st, 3)[:, 0:D], cxT[:, st, :], wo[:, :], start=True, stop=True)\
                          .then_inc(wctx_psum.sem, 1)
                    for g in range(2):
                        for st in STREAMS:
                            pe.wait_ge(wctx_ready.sem, wctx_ready.at(2 * bi + st + 1))
                            for i in range(G4):
                                last = pe.matmul(bank(st, 1 + g)[:, i * P:(i + 1) * P],
                                                 qT[:, st, g, i * P:(i + 1) * P], wctx[:, st, :],
                                                 start=True, stop=True)
                            last.then_inc(y_ready.sem, 1)
                    for st in STREAMS:
                        pe.wait_ge(c.resid_done.sem, c.resid_done.at(4 * bi + 4))
        c.ln_advance(8)
        c.resid_done.base += 8
        c.dve_step.base += 2 * KDA
        c.pool_step.base += 2 * KP
        c.act_step.base += 2

def moe(c, A):
    nc, X, PS, bank, ident, identb, signal = c.nc, c.X, c.PS, c.bank, c.ident, c.identb, c.counter
    with ExitStack() as mc:
        def msb(name, shape, dt=F32):
            return mc.enter_context(nc.sbuf_tensor(name, shape, dt))

        h_hi, h_lo = msb("h_hi", [P, NT * P], F32R), msb("h_lo", [P, NT * P], F32R)
        combT = msb("combT", [3 * E, NT * P], BF16)
        w1 = msb("w1", [P, (NJ + 1) * P])
        w3 = msb("w3", [P, (NJ + 1) * P])
        w2 = msb("w2", [P, NJ + 1, D])
        w1_hi, w1_lo, w3_hi, w3_lo = (msb(name, [P, (NJ + 1) * P], F32R) for name in ("w1_hi", "w1_lo", "w3_hi", "w3_lo"))
        sel = msb("sel", [3 * E, NJ, P], BF16)
        acarrier, pcarrier = msb("acarrier", [P, 1]), msb("pcarrier", [P, 2])
        moe_loaded = signal("moe_loaded")

        with ExitStack() as sc:
            def ssb(name, shape, dt=F32):
                return sc.enter_context(nc.sbuf_tensor(name, shape, dt))

            gw = ssb("gw", [P, E])
            gbias = ssb("gbias", [P, E])
            self32 = ssb("self32", [3 * E, NJ, P])
            exps = ssb("exps", [P, TB, E])
            score = ssb("score", [P, TB, E])
            biased = ssb("biased", [P, TB, E])
            gmax = ssb("gmax", [P, TB, NG])
            gwins = ssb("gwins", [P, NG, TB, NG], BF16)
            grank = ssb("grank", [P, TB, NG])
            keep = ssb("keep", [P, TB, NG])
            wins = ssb("wins", [P, E, TB, E], BF16)
            beaten = ssb("beaten", [P, E // 2, TB, E], BF16)
            comb = ssb("comb", [P, TB, E])
            part = ssb("part", [P, TB, P], BF16)
            r_loaded, wins_zeroed = signal("r_loaded"), signal("wins_zeroed")
            logit_ready, exps_ready, exps_read = signal("logit_ready"), signal("exps_ready"), signal("exps_read")
            parts_ready, partsT_ready, partsT_read = signal("parts_ready"), signal("partsT_ready"), signal("partsT_read")
            h_split = signal("h_split")
            PBANK = 2

            def tiles(n):
                return [[X[:, TB * n + G4 * st + i, :] for i in range(G4)] for st in STREAMS]

            with nc.Block() as block:

                @block.sync
                def _(sp):
                    for dst, src in ((gw[:, :], A["gwT"]), (gbias[:, :], A["L0_ffn_gate_bias"].partition_broadcast(P)),
                                     (self32[:, :, :], A["c_sel"])):
                        sp.dma_start(dst, src).then_inc(r_loaded.sem, 16)
                    for dst, src in ((w1[:, :], A["w1T"]), (w3[:, :], A["w3T"]), (w2[:, :, :], A["w2T"])):
                        sp.dma_start(dst, src).then_inc(moe_loaded.sem, 16)

                @block.gpsimd
                def _(pool):
                    c.ln_rstd(pool, Chain(pool, c.pool_step, 0), 0, G4)
                    pool.memset(gwins[:, :, :, :], 0.0)
                    pool.memset(part[:, :, :], 0.0)
                    pool.memset(wins[:, :, :, :], 0.0).then_inc(wins_zeroed.sem, 1)
                    def split_h(n):
                        for st in STREAMS:
                            pool.wait_ge(c.hT_ready.sem, c.hT_ready.at(2 * n + st + 1))
                            pool.tensor_tensor(pcarrier[:, st:st + 1], c.epsv[:, 0:1], c.epsv[:, 0:1], ALU.add)
                            tok = bass.ds(n * 2 * GT + st * GT, GT)
                            pool.tensor_tensor(h_lo[:, tok], c.hT[:, st, :], h_hi[:, tok], ALU.subtract).then_inc(h_split.sem, 1)

                    with pool.Fori(1, B) as n:
                        c.ln_rstd(pool, Chain(pool, c.pool_step, 2 * n), 2 * n, G4)
                        split_h(n - 1)
                    split_h(B - 1)
                    pool.wait_ge(moe_loaded.sem, 48)
                    chain = Chain(pool, c.pool_step, 2 * B)
                    for w, hi, lo in ((w1, w1_hi, w1_lo), (w3, w3_hi, w3_lo)):
                        chain(pool.tensor_copy(hi[:, :], w[:, :]))
                        pool.tensor_tensor(lo[:, :], w[:, :], hi[:, :], ALU.subtract)

                @block.tensor
                def _(pe):
                    def logits(n):
                        c.ln_transpose(pe, 2 * n, G4)
                        for st in STREAMS:
                            pe.wait_ge(c.hT_ready.sem, c.hT_ready.at(2 * n + st + 1))
                            for i in range(G4):
                                last = pe.matmul(bank(st, 1)[:, i * E:(i + 1) * E], c.hT[:, st, i * P:(i + 1) * P],
                                                 gw[:, :], start=True, stop=True)
                            last.then_inc(logit_ready.sem, 1)

                    def turn_parts(n):
                        pe.wait_ge(parts_ready.sem, parts_ready.at(n + 1))
                        if not isinstance(n, int) or n:
                            pe.wait_ge(partsT_read.sem, partsT_read.at(n))
                        for t in range(TB):
                            last = pe.transpose(PS[:, PBANK, :].bitcast(BF16)[:, t * P:(t + 1) * P], part[:, t, :], identb[:, :])
                        last.then_inc(partsT_ready.sem, 1)

                    pe.wait_ge(r_loaded.sem, 48)
                    logits(0)
                    logits(1)
                    turn_parts(0)
                    with pe.Fori(2, B) as n:
                        logits(n)
                        turn_parts(n - 1)
                    turn_parts(B - 1)

                @block.scalar
                def _(act):
                    def features(n):
                        c.mod_of_batch(act, n, 0, 3, [n, n], None if isinstance(n, int) and n == 0 else 2 * n)
                        for st in STREAMS:
                            if not (isinstance(n, int) and n == 0):
                                act.wait_ge(h_split.sem, h_split.at(2 * n + st - 1))
                            act.wait_ge(c.xnT_ready.sem, c.xnT_ready.at(2 * n + st + 1))
                            act.activation(c.hT[:, st, :], bank(st, 0), ACT.Identity,
                                           scale=c.modc[:, st, 1:2], bias=c.modc[:, st, 0:1])
                            act.activation(h_hi[:, bass.ds(n * 2 * GT + st * GT, GT)], bank(st, 0), ACT.Identity,
                                           scale=c.modc[:, st, 1:2], bias=c.modc[:, st, 0:1]).then_inc(c.hT_ready.sem, 1)
                        if not (isinstance(n, int) and n == 0):
                            act.wait_ge(exps_read.sem, exps_read.at(n))
                        for st in STREAMS:
                            act.wait_ge(logit_ready.sem, logit_ready.at(2 * n + st + 1))
                            last = act.activation(exps[:, G4 * st:G4 * (st + 1), :].rearrange("p t e -> p (t e)"),
                                                  bank(st, 1)[:, 0:G4 * E], ACT.Exp, scale=-1.0)
                        last.then_inc(exps_ready.sem, 1)

                    def take_parts(n):
                        act.wait_ge(partsT_ready.sem, partsT_ready.at(n + 1))
                        act.activation(acarrier[:, :], c.epsv[:, 0:1], ACT.Copy)
                        act.activation(combT[:, bass.ds(n * TB * P, TB * P)], PS[:, PBANK, :].bitcast(BF16)[0:3 * E, :],
                                       ACT.Copy).then_inc(partsT_read.sem, 1)

                    features(0)
                    features(1)
                    take_parts(0)
                    with act.Fori(2, B) as n:
                        features(n)
                        take_parts(n - 1)
                    take_parts(B - 1)

                @block.vector
                def _(dve):
                    steps = Steps(dve, c.dve_step)

                    def beats(won, value, n):
                        for i in range(n):
                            if i + 1 < n:
                                last = dve.tensor_tensor(won[:, i, :, i + 1:n], bc(value[:, :, i], 2, n - 1 - i),
                                                         value[:, :, i + 1:n], ALU.is_ge)
                            if i:
                                last = dve.tensor_tensor(won[:, i, :, 0:i], bc(value[:, :, i], 2, i),
                                                         value[:, :, 0:i], ALU.is_gt)
                        steps(last)
                        k = n // 2
                        steps(dve.tensor_tensor(beaten[:, 0:k, :, 0:n], won[:, 0:k, :, :], won[:, k:2 * k, :, :], ALU.add))
                        while k > 1:
                            k //= 2
                            steps(dve.tensor_tensor(beaten[:, 0:k, :, 0:n], beaten[:, 0:k, :, 0:n],
                                                    beaten[:, k:2 * k, :, 0:n], ALU.add))

                    def biases(n):
                        dve.wait_ge(exps_ready.sem, exps_ready.at(n + 1))
                        last = dve.tensor_scalar(score[:, :, :], exps[:, :, :], 1.0, None, ALU.add)
                        last.then_inc(exps_read.sem, 1)
                        dve.wait_ge(exps_read.sem, exps_read.at(n + 1))
                        steps(dve.reciprocal(score[:, :, :], score[:, :, :]))
                        steps(dve.tensor_tensor(biased[:, :, :], score[:, :, :], bc(gbias[:, :], 1, TB), ALU.add))
                        steps(dve.tensor_reduce(gmax[:, :, :], biased[:, :, :].rearrange("p t (g e) -> p t g e", e=EG),
                                                AX.X, ALU.max))

                    def ranks(n):
                        beats(gwins, gmax, NG)
                        steps(dve.tensor_scalar(keep[:, :, :], beaten[:, 0, :, 0:NG], float(TOPG), None, ALU.is_lt))
                        steps(dve.tensor_scalar(grank[:, :, :], keep[:, :, :], 1.0, -NEG, ALU.subtract, ALU.mult))
                        b4 = biased[:, :, :].rearrange("p t (g e) -> p (t g) e", e=EG)
                        steps(dve.tensor_tensor(b4, b4, bc(keep[:, :, :].rearrange("p t g -> p (t g)"), 2, EG), ALU.mult))
                        steps(dve.tensor_tensor(b4, b4, bc(grank[:, :, :].rearrange("p t g -> p (t g)"), 2, EG), ALU.add))
                        beats(wins, biased, E)
                        steps(dve.scalar_tensor_tensor(comb[:, :, :], beaten[:, 0, :, :], float(TOPK), score[:, :, :],
                                                       ALU.is_lt, ALU.mult))
                        if not isinstance(n, int) or n:
                            dve.wait_ge(partsT_ready.sem, partsT_ready.at(n))
                        steps(dve.tensor_copy(part[:, :, 0:E], comb[:, :, :]))
                        steps(dve.tensor_tensor(comb[:, :, :], comb[:, :, :], part[:, :, 0:E], ALU.subtract))
                        steps(dve.tensor_copy(part[:, :, E:2 * E], comb[:, :, :]))
                        steps(dve.tensor_tensor(comb[:, :, :], comb[:, :, :], part[:, :, E:2 * E], ALU.subtract))
                        dve.tensor_copy(part[:, :, 2 * E:3 * E], comb[:, :, :]).then_inc(parts_ready.sem, 1)

                    c.ln_stats(dve, steps, tiles(0))
                    c.ln_apply(dve, 0, tiles(0))
                    dve.wait_ge(r_loaded.sem, 48)
                    dve.tensor_copy(sel[:, :, :], self32[:, :, :])
                    dve.wait_ge(wins_zeroed.sem, 1)
                    first = steps.k
                    c.ln_stats(dve, steps, tiles(1))
                    biases(0)
                    c.ln_apply(dve, 2, tiles(1))
                    ranks(0)
                    each = steps.k - first
                    with dve.Fori(1, B - 1) as n:
                        steps.k = first + each * n
                        c.ln_stats(dve, steps, tiles(n + 1))
                        biases(n)
                        c.ln_apply(dve, 2 * n + 2, tiles(n + 1))
                        ranks(n)
                    steps.k = first + each * (B - 1)
                    biases(B - 1)
                    ranks(B - 1)
                    c.dve_step.base += steps.k
            c.ln_advance(8)
            c.act_step.base += 4
            c.pool_step.base += 8 + 2

        with ExitStack() as sc:
            def ssb(name, shape, dt=F32):
                return sc.enter_context(nc.sbuf_tensor(name, shape, dt))

            sg = ssb("sg", [P, 2, GT])
            uu = ssb("uu", [P, 2, GT])
            yT = ssb("yT", [P, GT])
            gcur = ssb("gcur", [P, 1])
            sgn = ssb("l1_sgn", [P, B, D])
            h_ready, silu_ready = signal("h_ready"), signal("silu_ready")
            u_ready = signal("u_ready", 1)
            acc_ready, yB_ready = signal("acc_ready"), signal("yB_ready")
            yT_ready = signal("yT_ready", 1)
            NU = NJ + 1
            YACC, YTOK = 6, 7

            with nc.Block() as block:

                @block.gpsimd
                def _(pool):
                    chain = Chain(pool, c.pool_step, 0)
                    one = c.rowB[:, c.L1CB, :, :]
                    chain(pool.tensor_scalar(one, one, 1.0, None, ALU.add))
                    for row in (c.L1GA, c.L1GB):
                        gate = c.rowB[:, row, :, :]
                        chain(pool.tensor_scalar(sgn[:, :, :], gate, 0.0, 2.0, ALU.is_ge, ALU.mult))
                        chain(pool.tensor_scalar(sgn[:, :, :], sgn[:, :, :], 1.0, None, ALU.subtract))
                        chain(pool.tensor_tensor(gate, gate, sgn[:, :, :], ALU.mult))
                        chain(pool.tensor_scalar(gate, gate, 0.25, None, ALU.max))
                        chain(pool.tensor_tensor(gate, gate, sgn[:, :, :], ALU.mult))

                @block.tensor
                def _(pe):
                    pe.wait_ge(moe_loaded.sem, 48)
                    def back(g):
                        pe.wait_ge(yT_ready.sem, yT_ready.at(g + 1))
                        for i in range(G4):
                            last = pe.transpose(PS[:, YTOK, i * P:(i + 1) * P], yT[:, i * P:(i + 1) * P], ident[:, :])
                        last.then_inc(yB_ready.sem, 1)

                    def group(g):
                        tok = bass.ds(g * GT, GT)

                        def down(j):
                            pe.wait_ge(u_ready.sem, u_ready.at(NU * g + j + 1))
                            return pe.matmul(PS[:, YACC, :], w2[:, j, :], uu[:, j % 2, :],
                                             start=(j == 0), stop=(j == NJ))

                        for j in range(NU):
                            p = j % 2
                            pe.wait_ge(u_ready.sem, u_ready.at(NU * g + max(j - 1, 0)))
                            cols = slice(j * P, (j + 1) * P)
                            for k, (hi, lo) in enumerate(((w1_hi, w1_lo), (w3_hi, w3_lo))):
                                pe.matmul(PS[:, 3 * p + k, :], hi[:, cols], h_hi[:, tok], start=True, stop=False)
                                pe.matmul(PS[:, 3 * p + k, :], hi[:, cols], h_lo[:, tok], start=False, stop=False)
                                last = pe.matmul(PS[:, 3 * p + k, :], lo[:, cols], h_hi[:, tok], start=False, stop=True)
                            if j < NJ:
                                last = pe.matmul(PS[:, 3 * p + 2, :], sel[:, j, :], combT[:, tok], start=True, stop=True)
                            last.then_inc(h_ready.sem, 1)
                            if j == 1 and not (isinstance(g, int) and g == 0):
                                back(g - 1)
                            if j:
                                down(j - 1)
                        down(NJ).then_inc(acc_ready.sem, 1)

                    group(0)
                    group(1)
                    with pe.Fori(1, B) as b:
                        group(2 * b)
                        group(2 * b + 1)
                    back(2 * B - 1)

                @block.scalar
                def _(act):
                    act.activation(gcur[:, :], c.gbT[:, 0:1], ACT.Copy).then_inc(yT_ready.sem, 1)
                    with act.Fori(0, B) as b:
                        act.wait_ge(yT_ready.sem, yT_ready.at(2 * b))
                        act.activation(gcur[:, :], c.gbT[:, bass.ds(b, 1)], ACT.Copy).then_inc(c.act_step.sem, 1)
                        act.wait_ge(c.act_step.sem, c.act_step.at(b + 1))
                        with act.Fori(0, 2) as half:
                            g = 2 * b + half
                            for j in range(NU):
                                p = j % 2
                                act.wait_ge(h_ready.sem, h_ready.at(NU * g + j + 1))
                                act.activation(sg[:, p, :], PS[:, 3 * p, :], ACT.Silu).then_inc(silu_ready.sem, 1)
                            act.wait_ge(acc_ready.sem, acc_ready.at(g + 1))
                            act.activation(yT[:, :], PS[:, YACC, :], ACT.Copy, scale=gcur[:, 0:1]).then_inc(yT_ready.sem, 1)

                @block.vector
                def _(dve):
                    dve.memset(c.carrier[:, :], 0.0).then_inc(u_ready.sem, 1)
                    def add(g):
                        dve.wait_ge(yB_ready.sem, yB_ready.at(g + 1))
                        xt = X[:, bass.ds(G4 * g, G4), :]
                        dve.tensor_tensor(xt, xt, PS[:, YTOK, :].rearrange("p (t d) -> p t d", d=D), ALU.add)

                    def group(g):
                        chain = Chain(dve, c.dve_step, NJ * g)
                        for j in range(NU):
                            p = j % 2
                            dve.wait_ge(silu_ready.sem, silu_ready.at(NU * g + j + 1))
                            last = dve.tensor_tensor(uu[:, p, :], sg[:, p, :], PS[:, 3 * p + 1, :], ALU.mult)
                            if j < NJ:
                                chain(last)
                                last = dve.tensor_tensor(uu[:, p, :], uu[:, p, :], PS[:, 3 * p + 2, :], ALU.mult)
                            last.then_inc(u_ready.sem, 1)
                            if j == 1 and not (isinstance(g, int) and g == 0):
                                add(g - 1)

                    group(0)
                    group(1)
                    with dve.Fori(1, B) as b:
                        group(2 * b)
                        group(2 * b + 1)
                    add(2 * B - 1)
            c.act_step.base += B
            c.pool_step.base += 11
            c.dve_step.base += NJ * 8

def windowed_attention(c, A, Z):
    nc, X, PS, ident, identb = c.nc, c.X, c.PS, c.ident, c.identb
    PASSES = H1 // 4
    VW = 32
    with ExitStack() as sc:
        def ssb(name, shape, dt=F32):
            return c.sb(name, shape, dt, sc)

        wqkv = ssb("d_wqkv", [P, 3 * D])
        wo = ssb("d_wo", [P, D])
        hmask = ssb("hmask", [P, 4])
        mask32 = ssb("mask32", [P, 2, KEYS1])
        mask = ssb("mask", [P, TB, KEYS1], BF16)
        kx_hi, kx_lo = ssb("kx_hi", [P, B, 4, KEYS1], F32R), ssb("kx_lo", [P, B, 4, KEYS1], F32R)
        kpre = ssb("kpre", [P, B, 4, PRE])
        kraw, k_hi, k_lo = ssb("kraw", [P, 2, P]), ssb("k_hi", [P, 2, P], F32R), ssb("k_lo", [P, 2, P])
        qraw, q_hi, q_lo = ssb("qraw", [P, 2, P]), ssb("q_hi", [P, 2, P], F32R), ssb("q_lo", [P, 2, P], F32R)
        va = ssb("va", [P, B, H1, VW])
        vb = ssb("vb", [KB1, B, H1, VW])
        pm = ssb("pm", [P, 2, 4, KEYS1])
        pa = ssb("pa", [P, 2, 4, P])
        pb = ssb("pb", [KB1, 2, 4, P])
        mx = ssb("d_mx", [P, 2, 4])
        kzero = ssb("kzero", [P, 4, W1])
        usum = ssb("usum", [P, 2, PASSES, P])
        rz = ssb("rz", [P, H1])
        on = ssb("on", [P, 2, H1, DH1])
        oT = ssb("oT", [P, 2, P])
        yg = ssb("yg", [P, 2, D])
        SBANK, TBANK, UBANK, YBANK, RBANK, FBANK = 0, 2, 4, 5, 6, 7
        signal = c.counter
        w_loaded = signal("d_loaded")
        pre_psum, kx_zeroed, v_init, v_filled = signal("pre_psum"), signal("kx_zeroed"), signal("v_init"), signal("v_filled")
        qkv_ready, qkv_evac, before_ready, kx_ready = signal("d_qkv"), signal("qkv_evac"), signal("before_ready"), signal("kx_ready")
        s_ready, p_shifted, p_exp, lo_ready = signal("s_ready"), signal("p_shifted"), signal("p_exp"), signal("lo_ready")
        pT_psum, pT_ready, u_psum, u_evac = signal("pT_psum"), signal("pT_ready"), signal("u_psum"), signal("u_evac")
        zsum6, zmeanvar, zvareps = ssb("zsum6", [P, 6]), ssb("zmeanvar", [P, 2]), ssb("zvareps", [P, 1])
        zrstd, zn = ssb("zrstd", [P, 1]), ssb("zn", [P, D])
        zstats_ready, zrstd_ready, z_ready, z_stored = (signal("zstats_ready"), signal("zrstd_ready"), signal("z_ready"),
                                                        signal("z0_stored"))
        uT_psum, o_ready, oT_psum, oT_ready, y_ready = (signal("uT_psum"), signal("o_ready"), signal("oT_psum"), signal("oT_ready"),
                                                        signal("d_y"))

        def first_tiles():
            return [[X[:, TB * (2 * st + i), :] for i in range(2)] for st in STREAMS]

        with nc.Block() as block:

            @block.sync
            def _(sp):
                for dst, src in ((wqkv[:, :], A["d_wqkvT"]), (wo[:, :], A["d_woutT"]), (hmask[:, :], A["c_hmask"]),
                                 (mask32[:, :, :], A["c_mask1"])):
                    sp.dma_start(dst, src).then_inc(w_loaded.sem, 16)

            @block.gpsimd
            def _(pool):
                c.ln_rstd(pool, Chain(pool, c.pool_step, 0), 0, 2)
                pool.memset(kzero[:, :, :], 0.0).then_inc(kx_zeroed.sem, 1)
                pool.wait_ge(kx_zeroed.sem, 1)
                for half in (kx_hi, kx_lo):
                    for b in range(B):
                        pool.tensor_tensor(half[:, b, :, 0:W1], kzero[:, :, :], kzero[:, :, :], ALU.add)

            @block.vector
            def _(dve):
                dve.memset(va[:, :, :, :], 0.0)
                dve.memset(vb[:, :, :, :], 0.0).then_inc(v_init.sem, 1)
                dve.wait_ge(v_init.sem, 1)
                dve.memset(va[:, :, :, DH1:DH1 + 1], 1.0)
                dve.memset(vb[:, :, :, DH1:DH1 + 1], 1.0).then_inc(v_filled.sem, 1)
                chain = Chain(dve, c.dve_step, 0)
                c.ln_stats(dve, chain, first_tiles())
                c.ln_apply(dve, 0, first_tiles())
                dve.wait_ge(w_loaded.sem, 64)
                dve.tensor_copy(mask[:, 0, :], mask32[:, 0, :])
                dve.tensor_copy(mask[:, 1:TB, :], bc(mask32[:, 1, :], 1, TB - 1))
                dve.wait_ge(pre_psum.sem, 1)
                for b in range(B):
                    k = c.bank(b // 2, 1)[:, (b % 2) * P:(b % 2) * P + PRE]
                    last = dve.tensor_tensor(kpre[:, b, :, :], bc(k, 1, 4), bc(hmask[:, :], 2, PRE), ALU.mult)
                chain(last)
                chain(dve.tensor_copy(kx_hi[:, :, :, W1:KB1], kpre[:, :, :, :]))
                dve.tensor_tensor(kx_lo[:, :, :, W1:KB1], kpre[:, :, :, :], kx_hi[:, :, :, W1:KB1], ALU.subtract)

            @block.scalar
            def _(act):
                for st in STREAMS:
                    act.wait_ge(c.xnT_ready.sem, c.xnT_ready.at(st + 1))
                    for i in range(2):
                        b = 2 * st + i
                        last = act.activation(c.hT[:, st, i * P:(i + 1) * P], c.bank(st, 0)[:, i * P:(i + 1) * P], ACT.Identity,
                                              scale=c.modT[:, 1, 1, b:b + 1], bias=c.modT[:, 1, 0, b:b + 1])
                    last.then_inc(c.hT_ready.sem, 1)
                act.wait_ge(v_filled.sem, 1)
                act.wait_ge(pre_psum.sem, 1)
                for b in range(B):
                    v = c.bank(b // 2, 2)[0:PRE, (b % 2) * P:(b % 2 + 1) * P].rearrange("p (h e) -> p h e", e=DH1)
                    act.activation(vb[W1:KB1, b, :, 0:DH1], v, ACT.Copy)

            @block.tensor
            def _(pe):
                pe.wait_ge(w_loaded.sem, 64)
                c.ln_transpose(pe, 0, 2)
                for st in STREAMS:
                    pe.wait_ge(c.hT_ready.sem, c.hT_ready.at(st + 1))
                    pe.matmul(c.bank(st, 1)[:, 0:2 * P], wqkv[:, D:2 * D], c.hT[:, st, 0:2 * P], start=True, stop=True)
                    for i in range(2):
                        last = pe.matmul(c.bank(st, 2)[0:PRE, i * P:(i + 1) * P], c.hT[:, st, i * P:i * P + PRE],
                                         wqkv[:, 2 * D:3 * D], start=True, stop=True)
                last.then_inc(pre_psum.sem, 1)
        c.ln_advance(2)
        c.pool_step.base += 2
        c.dve_step.base += 3

        def unit(t, b):
            return B * t + b

        def before(t, b, n=1):
            t, b = (t, b - n) if b >= n else (t - 1, b - n + B)
            return None if isinstance(t, int) and t < 0 else (t, b)

        def after(t, b, n=1):
            t, b = (t, b + n) if b + n < B else (t + 1, b + n - B)
            return None if isinstance(t, int) and t >= TB else (t, b)

        def turns(eng, turn, drain):
            turn(0)
            with eng.Fori(1, TB - 1) as t:
                turn(t)
            turn(TB - 1)
            drain()

        def slots(t):
            for b in range(B):
                for h in range(PASSES):
                    yield b, h, PASSES * unit(t, b) + h

        def some(k):
            return not isinstance(k, int) or k >= 0

        with nc.Block() as block:

            @block.sync
            def _(sp):
                with sp.Fori(0, TB) as t:
                    for b in range(B):
                        sp.wait_ge(z_ready.sem, z_ready.at(unit(t, b) + 1))
                        sp.dma_start(c.z_ffn[b, bass.ds(1 + P * t, P), :], Z[:, TB * b + t, :]).then_inc(z_stored.sem, 16)
                sp.wait_ge(z_stored.sem, 16 * B * TB)

            @block.gpsimd
            def _(pool):
                chain = Steps(pool, c.pool_step)

                def stream_rstd(t, b):
                    pool.wait_ge(zstats_ready.sem, zstats_ready.at(unit(t, b) + 1))
                    chain(pool.tensor_tensor(zvareps[:, :], zmeanvar[:, 1:2], c.epsv[:, 0:1], ALU.add))
                    pool.tensor_tensor(zrstd[:, :], zvareps[:, :], c.neghalf[:, 0:1], ALU.pow).then_inc(zrstd_ready.sem, 1)

                def front(t, b):
                    u, st = unit(t, b), b % 2
                    pool.wait_ge(c.stats_ready.sem, c.stats_ready.at(u + 1))
                    chain(pool.tensor_tensor(c.vareps[:, st, 0:1], c.meanvar[:, st, 0:1, 1], c.epsv[:, 0:1], ALU.add))
                    pool.tensor_tensor(c.rstd[:, st, 0:1], c.vareps[:, st, 0:1], c.neghalf[:, 0:1],
                                       ALU.pow).then_inc(c.rstd_ready.sem, 1)
                    if not (isinstance(t, int) and t == 0):
                        pool.wait_ge(s_ready.sem, s_ready.at(2 * PASSES * (u - B + 1)))
                        for half in (kx_hi, kx_lo):
                            last = pool.tensor_tensor(half[:, b, :, 0:W1], half[:, b, :, KEYS1 - W1:KEYS1], kzero[:, :, :], ALU.add)
                        last.then_inc(before_ready.sem, 1)

                def remainders(t, b):
                    u, par = unit(t, b), b % 2
                    pool.wait_ge(qkv_evac.sem, qkv_evac.at(u + 1))
                    pool.tensor_tensor(q_lo[:, par, :], qraw[:, par, :], q_hi[:, par, :], ALU.subtract)
                    chain(pool.tensor_tensor(k_lo[:, par, :], kraw[:, par, :], k_hi[:, par, :], ALU.subtract))
                    if not (isinstance(t, int) and t == 0):
                        pool.wait_ge(before_ready.sem, before_ready.at(u - B + 1))
                    pool.tensor_tensor(kx_lo[:, b, :, KB1:KEYS1], bc(k_lo[:, par, :], 1, 4), bc(hmask[:, :], 2, P),
                                       ALU.mult).then_inc(lo_ready.sem, 1)

                def turn(t):
                    for b in range(B):
                        if before(t, b, 3):
                            stream_rstd(*before(t, b, 3))
                        if after(t, b):
                            remainders(*after(t, b))
                        if after(t, b, 2):
                            front(*after(t, b, 2))

                front(0, 0)
                remainders(0, 0)
                front(0, 1)
                turn(0)
                first, each = chain.k, 3 * B
                with pool.Fori(1, TB - 1) as t:
                    chain.k = first + each * (t - 1)
                    turn(t)
                chain.k = first + each * (TB - 2)
                turn(TB - 1)
                for b in range(B - 3, B):
                    stream_rstd(TB - 1, b)
                assert chain.k == 3 * B * TB

            @block.vector
            def _(dve):
                chain = Steps(dve, c.dve_step)

                def stats(t, b):
                    st = b % 2
                    chain(dve.bn_stats(c.stat6[:, st, 0, :], X[:, TB * b + t, :]))
                    dve.memset(c.carrier[:, :], 0.0)
                    dve.bn_aggr(c.meanvar[:, st, 0, :], c.stat6[:, st, 0, :]).then_inc(c.stats_ready.sem, 1)

                def apply(t, b):
                    st = b % 2
                    dve.wait_ge(c.rstd_ready.sem, c.rstd_ready.at(unit(t, b) + 1))
                    dve.tensor_scalar(c.xn[:, st, 0, :], X[:, TB * b + t, :], c.meanvar[:, st, 0, 0:1], c.rstd[:, st, 0:1],
                                      ALU.subtract, ALU.mult).then_inc(c.xn_ready.sem, 1)

                def keys(t, b):
                    u = unit(t, b)
                    if not (isinstance(t, int) and t == 0):
                        dve.wait_ge(before_ready.sem, before_ready.at(u - B + 1))
                    dve.wait_ge(qkv_evac.sem, qkv_evac.at(u + 1))
                    par = b % 2
                    dve.tensor_tensor(kx_hi[:, b, :, KB1:KEYS1], bc(k_hi[:, par, :], 1, 4), bc(hmask[:, :], 2, P),
                                      ALU.mult).then_inc(kx_ready.sem, 1)

                def divide(t, b):
                    dve.wait_ge(uT_psum.sem, uT_psum.at(unit(t, b) + 1))
                    o = PS[:, RBANK, :].rearrange("p (h e) -> p h e", e=VW)
                    chain(dve.reciprocal(rz[:, :], o[:, :, DH1]))
                    dve.tensor_tensor(on[:, b % 2, :, :], o[:, :, 0:DH1], bc(rz[:, :], 2, DH1), ALU.mult).then_inc(o_ready.sem, 1)

                def resid(t, b):
                    dve.wait_ge(y_ready.sem, y_ready.at(unit(t, b) + 1))
                    chain(dve.tensor_tensor(yg[:, b % 2, :], PS[:, YBANK, 0:D], c.rowB[:, c.L1GA, b, :], ALU.mult))
                    xt = X[:, TB * b + t, :]
                    dve.tensor_tensor(xt, xt, yg[:, b % 2, :], ALU.add).then_inc(c.resid_done.sem, 1)
                    dve.wait_ge(c.resid_done.sem, c.resid_done.at(unit(t, b) + 1))
                    dve.memset(c.carrier[:, :], 0.0)
                    chain(dve.bn_stats(zsum6[:, :], xt))
                    dve.memset(c.carrier[:, :], 0.0)
                    dve.bn_aggr(zmeanvar[:, :], zsum6[:, :]).then_inc(zstats_ready.sem, 1)

                def stream(t, b):
                    dve.wait_ge(zrstd_ready.sem, zrstd_ready.at(unit(t, b) + 1))
                    z = Z[:, TB * b + t, :]
                    chain(dve.tensor_scalar(zn[:, :], X[:, TB * b + t, :], zmeanvar[:, 0:1], zrstd[:, 0:1],
                                            ALU.subtract, ALU.mult))
                    chain(dve.tensor_tensor(zn[:, :], zn[:, :], c.rowB[:, c.L1CB, b, :], ALU.mult))
                    dve.tensor_tensor(z, zn[:, :], c.rowB[:, c.L1SB, b, :], ALU.add).then_inc(z_ready.sem, 1)

                def turn(t):
                    for b, h, k in slots(t):
                        for i in range(2):
                            dve.wait_ge(s_ready.sem, s_ready.at(2 * k + i + 1))
                            s = PS[:, SBANK + i, 0:2 * KEYS1].rearrange("p (j k) -> p j k", k=KEYS1)
                            m = mx[:, h % 2, 2 * i:2 * i + 2]
                            chain(dve.tensor_reduce(m, s, AX.X, ALU.max))
                            if i == 0 and some(k - 2):
                                dve.wait_ge(pT_psum.sem, pT_psum.at(k - 1))
                            dve.tensor_tensor(pm[:, h % 2, 2 * i:2 * i + 2, :], s, bc(m, 2, KEYS1),
                                              ALU.subtract).then_inc(p_shifted.sem, 1)
                        if h == 0:
                            if after(t, b):
                                apply(*after(t, b))
                            if before(t, b, 3):
                                resid(*before(t, b, 3))
                        elif h == 1 and before(t, b, 2):
                            divide(*before(t, b, 2))
                        elif h == 2 and after(t, b):
                            keys(*after(t, b))
                        elif h == 3:
                            if after(t, b, 2):
                                stats(*after(t, b, 2))
                            if before(t, b, 3):
                                stream(*before(t, b, 3))

                stats(0, 0)
                apply(0, 0)
                keys(0, 0)
                stats(0, 1)
                turn(0)
                first, each = chain.k, B * (2 * PASSES + 6)
                with dve.Fori(1, TB - 1) as t:
                    chain.k = first + each * (t - 1)
                    turn(t)
                chain.k = first + each * (TB - 2)
                turn(TB - 1)
                resid(TB - 1, B - 3)
                stream(TB - 1, B - 3)
                for b in (B - 2, B - 1):
                    divide(TB - 1, b)
                    resid(TB - 1, b)
                    stream(TB - 1, b)
                c.dve_step.base += chain.k

            @block.scalar
            def _(act):
                def front_h(t, b):
                    u, st = unit(t, b), b % 2
                    act.wait_ge(c.xnT_ready.sem, c.xnT_ready.at(u + 1))
                    act.activation(c.hT[:, st, 0:P], PS[:, FBANK, 0:P], ACT.Identity,
                                   scale=c.modT[:, 1, 1, b:b + 1], bias=c.modT[:, 1, 0, b:b + 1]).then_inc(c.hT_ready.sem, 1)

                def front_qkv(t, b):
                    u = unit(t, b)
                    act.wait_ge(qkv_ready.sem, qkv_ready.at(u + 1))
                    if not (isinstance(t, int) and t == 0):
                        act.activation(vb[0:W1, b, :, 0:DH1], va[W1:P, b, :, 0:DH1], ACT.Copy).then_inc(c.act_step.sem, 1)
                    for k, q in ((kraw, qraw), (k_hi, q_hi)):
                        act.activation(k[:, b % 2, :], PS[:, FBANK, 2 * P:3 * P], ACT.Copy)
                        act.activation(q[:, b % 2, :], PS[:, FBANK, P:2 * P], ACT.Copy, scale=float(DH1) ** -0.5)
                    if not (isinstance(t, int) and t == 0):
                        act.wait_ge(c.act_step.sem, c.act_step.at(u - B + 1))
                    act.activation(va[:, b, :, 0:DH1], PS[:, FBANK, 3 * P:4 * P].rearrange("p (h e) -> p h e", e=DH1),
                                   ACT.Copy).then_inc(qkv_evac.sem, 1)

                def take_u(t, b):
                    act.wait_ge(u_psum.sem, u_psum.at(unit(t, b) + 1))
                    act.activation(usum[:, b % 2, :, :].rearrange("p h q -> p (h q)"), PS[:, UBANK, :],
                                   ACT.Copy).then_inc(u_evac.sem, 1)

                def take_o(t, b):
                    act.wait_ge(oT_psum.sem, oT_psum.at(unit(t, b) + 1))
                    act.activation(oT[:, b % 2, :], PS[:, YBANK, P:2 * P], ACT.Copy).then_inc(oT_ready.sem, 1)

                def take_p(k, par):
                    act.wait_ge(pT_psum.sem, pT_psum.at(k + 1))
                    act.activation(pa[:, par, :, :].rearrange("p j q -> p (j q)"), PS[:, TBANK, :], ACT.Copy)
                    act.activation(pb[:, par, :, :].rearrange("p j q -> p (j q)"), PS[0:KB1, TBANK + 1, :],
                                   ACT.Copy).then_inc(pT_ready.sem, 1)

                def turn(t):
                    for b, h, k in slots(t):
                        if h == 1 and after(t, b):
                            front_h(*after(t, b))
                        if h == 2:
                            if before(t, b):
                                take_u(*before(t, b))
                            if after(t, b):
                                front_qkv(*after(t, b))
                        if h == 3 and before(t, b, 2):
                            take_o(*before(t, b, 2))
                        if some(k - 1):
                            take_p(k - 1, (h - 1) % 2)
                        act.wait_ge(p_shifted.sem, p_shifted.at(2 * k + 2))
                        act.activation(pm[:, h % 2, :, :], pm[:, h % 2, :, :], ACT.Exp).then_inc(p_exp.sem, 1)

                def drain():
                    take_p(PASSES * B * TB - 1, 1)
                    take_o(TB - 1, B - 2)
                    take_u(TB - 1, B - 1)
                    take_o(TB - 1, B - 1)

                front_h(0, 0)
                front_qkv(0, 0)
                turns(act, turn, drain)

            @block.tensor
            def _(pe):
                def front_t(t, b):
                    u = unit(t, b)
                    if some(u - 1):
                        pe.wait_ge(qkv_evac.sem, qkv_evac.at(u))
                    pe.wait_ge(c.xn_ready.sem, c.xn_ready.at(u + 1))
                    pe.transpose(PS[:, FBANK, 0:P], c.xn[:, b % 2, 0, :], ident[:, :]).then_inc(c.xnT_ready.sem, 1)

                def front_qkv(t, b):
                    pe.wait_ge(c.hT_ready.sem, c.hT_ready.at(unit(t, b) + 1))
                    h = c.hT[:, b % 2, 0:P]
                    pe.matmul(PS[:, FBANK, P:2 * P], wqkv[:, 0:D], h, start=True, stop=True)
                    pe.matmul(PS[:, FBANK, 2 * P:3 * P], wqkv[:, D:2 * D], h, start=True, stop=True)
                    pe.matmul(PS[:, FBANK, 3 * P:4 * P], h, wqkv[:, 2 * D:3 * D], start=True, stop=True).then_inc(qkv_ready.sem, 1)

                def scores(t, b, h, k):
                    if h == 0:
                        pe.wait_ge(kx_ready.sem, kx_ready.at(unit(t, b) + 1))
                        pe.wait_ge(lo_ready.sem, lo_ready.at(unit(t, b) + 1))
                        pe.wait_ge(qkv_evac.sem, qkv_evac.at(unit(t, b) + 1))
                    rows = slice(32 * h, 32 * h + 32)
                    for i in range(2):
                        if some(k - 1):
                            pe.wait_ge(p_shifted.sem, p_shifted.at(2 * k - 1 + i))
                        s = PS[:, SBANK + i, 0:2 * KEYS1]
                        pe.matmul(s.rearrange("p (j k) -> p j k", k=KEYS1), identb[:, :], bc(mask[:, t, :], 1, 2),
                                  start=True, stop=False)
                        hi, lo = (k[rows, b, 2 * i:2 * i + 2, :].rearrange("p j k -> p (j k)") for k in (kx_hi, kx_lo))
                        pe.matmul(s, q_hi[rows, b % 2, :], hi, start=False, stop=False)
                        pe.matmul(s, q_hi[rows, b % 2, :], lo, start=False, stop=False)
                        pe.matmul(s, q_lo[rows, b % 2, :], hi, start=False, stop=True).then_inc(s_ready.sem, 1)

                def transpose_p(k, par):
                    pe.wait_ge(p_exp.sem, p_exp.at(k + 1))
                    if some(k - 1):
                        pe.wait_ge(pT_ready.sem, pT_ready.at(k))
                    for j in range(4):
                        pe.transpose(PS[:, TBANK, j * P:(j + 1) * P], pm[:, par, j, KB1:KEYS1], ident[:, :])
                        last = pe.transpose(PS[0:KB1, TBANK + 1, j * P:(j + 1) * P], pm[:, par, j, 0:KB1], ident[:, :])
                    last.then_inc(pT_psum.sem, 1)

                def weigh(t, b, h, k):
                    pe.wait_ge(pT_ready.sem, pT_ready.at(k + 1))
                    if h == 0 and before(t, b):
                        pe.wait_ge(u_evac.sem, u_evac.at(unit(*before(t, b)) + 1))
                    o = [PS[32 * j:32 * j + 32, UBANK, h * P:(h + 1) * P] for j in range(4)]
                    for j in range(4):
                        pe.matmul(o[j], va[:, b, 4 * h + j, :], pa[:, h % 2, j, :], start=True, stop=False)
                    for j in range(4):
                        last = pe.matmul(o[j], vb[:, b, 4 * h + j, :], pb[:, h % 2, j, :], start=False, stop=True)
                    if h == PASSES - 1:
                        last.then_inc(u_psum.sem, 1)

                def turn_u(t, b):
                    u = unit(t, b)
                    pe.wait_ge(u_evac.sem, u_evac.at(u + 1))
                    if some(u - 1):
                        pe.wait_ge(o_ready.sem, o_ready.at(u))
                    for h in range(PASSES):
                        last = pe.transpose(PS[:, RBANK, h * P:(h + 1) * P], usum[:, b % 2, h, :], ident[:, :])
                    last.then_inc(uT_psum.sem, 1)

                def turn_o(t, b):
                    u = unit(t, b)
                    pe.wait_ge(o_ready.sem, o_ready.at(u + 1))
                    if some(u - 1):
                        pe.wait_ge(c.resid_done.sem, c.resid_done.at(u))
                    pe.transpose(PS[:, YBANK, P:2 * P], on[:, b % 2, :, :].rearrange("p h e -> p (h e)"),
                                 ident[:, :]).then_inc(oT_psum.sem, 1)

                def project(t, b):
                    pe.wait_ge(oT_ready.sem, oT_ready.at(unit(t, b) + 1))
                    pe.matmul(PS[:, YBANK, 0:D], oT[:, b % 2, :], wo[:, :], start=True, stop=True).then_inc(y_ready.sem, 1)

                def turn(t):
                    for b, h, k in slots(t):
                        scores(t, b, h, k)
                        if h == 1:
                            if after(t, b):
                                front_t(*after(t, b))
                        elif h == 2:
                            if before(t, b, 2):
                                turn_o(*before(t, b, 2))
                            if after(t, b):
                                front_qkv(*after(t, b))
                        elif h == 3:
                            if before(t, b):
                                turn_u(*before(t, b))
                            if before(t, b, 2):
                                project(*before(t, b, 2))
                        if some(k - 1):
                            transpose_p(k - 1, (h - 1) % 2)
                        if some(k - 2):
                            where = (t, b) if h >= 2 else before(t, b)
                            weigh(*where, (h - 2) % PASSES, k - 2)

                def drain():
                    k, t, b = PASSES * B * TB, TB - 1, B - 1
                    transpose_p(k - 1, 1)
                    weigh(t, b, PASSES - 2, k - 2)
                    turn_o(t, b - 1)
                    weigh(t, b, PASSES - 1, k - 1)
                    project(t, b - 1)
                    turn_u(t, b)
                    turn_o(t, b)
                    project(t, b)

                front_t(0, 0)
                front_qkv(0, 0)
                turns(pe, turn, drain)
        c.ln_advance(B * TB)
        c.resid_done.base += B * TB
        c.act_step.base += B * (TB - 1)
        c.pool_step.base += 3 * B * TB


def local_transformer(c, A, Z):
    nc, bank, ident, identb, signal = c.nc, c.bank, c.ident, c.identb, c.counter
    resid = c.resid_done
    UA, UF = 2 * 2 * TB, 2 * B
    HALVES = H2 // 4
    with ExitStack() as sc:
        def ssb(name, shape, dt=F32):
            return c.sb(name, shape, dt, sc)

        wqkv = ssb("wqkv", [P, 3 * INNER])
        wo = ssb("e_wo", [P, INNER // P, D])
        w1 = ssb("f_w1", [P, 2 * HC, P])
        w2 = ssb("f_w2", [P, HC, D])
        b1 = ssb("f_b1", [P, 2 * HC])
        b2 = ssb("f_b2", [P, D])
        lnp = ssb("lnp", [P, 2])
        qks = ssb("qks", [P, 2, DH2])
        cos0 = ssb("cos0", [P, TB, 2, DH2])
        sin0 = ssb("sin0", [P, TB, 2, DH2])
        cosl = ssb("cosl", [P, TB, 2, DH2])
        sinl = ssb("sinl", [P, TB, 2, DH2])
        mask32 = ssb("e_mask32", [P, 2, KEYS2])
        mask = ssb("e_mask", [P, TB, KEYS2], BF16)
        zs = ssb("zs", [P, B, D])
        sq = ssb("sq", [P, 2, 2, INNER])
        ss = ssb("ss", [P, 2, 2 * H2])
        rn = ssb("rn", [P, 2, 2 * H2])
        tiny = ssb("tiny", [P, 2 * H2])
        qk = ssb("qk", [P, 2, 2, H2, DH2])
        rot = ssb("rot", [P, 2, 2, H2, DH2])
        qT = ssb("e_qT", [P, 2, 4, P])
        kT = ssb("e_kT", [P, B, 4, KEYS2])
        va = ssb("e_va", [P, B, H2, DH2 + 1])
        vb = ssb("e_vb", [P, B, HALVES, 2, 2, DH2 + 1])
        pm = ssb("e_pm", [P, 2, 4 * KEYS2])
        pa = ssb("e_pa", [P, 2, 4, P])
        pb = ssb("e_pb", [P, 2, 2, P])
        mx = ssb("e_mx", [P, 2, 4])
        rz = ssb("e_rz", [P, 2, 4])
        on = ssb("e_on", [P, 2, H2, DH2])
        oT = ssb("e_oT", [P, 2, 4, P])
        zg = ssb("zg", [P, 2, G4, D])
        gate = ssb("gate", [P, 2, GT])
        uu = ssb("f_uu", [P, 2, HC, GT])

        kzero = ssb("e_kzero", [P, 4, W2])
        carrier = ssb("p_carrier", [P, 2])
        stage_stored = signal("stage_stored")
        consts, cos_done, before_ready, qk_taken = signal("e_consts"), signal("cos_done"), signal("e_before"), signal("qk_taken")
        qkv_loaded, w_loaded, tables_ready = signal("e_qkv_loaded"), signal("e_loaded"), signal("tables_ready")
        zs_loaded = [signal(f"zs_loaded{b}") for b in range(B)]
        zs_stored = [signal(f"zs_stored{b}") for b in range(B)]
        zsT_psum, eh_ready, eqkv_ready, v_evac, sq_ready = (signal("zsT_psum"), signal("eh_ready"), signal("eqkv_ready"),
                                                            signal("ev_evac"), signal("sq_ready"))
        ss_ready, rn_ready, qk_normed, rot_ready = signal("ss_ready"), signal("rn_ready"), signal("qk_normed"), signal("rot_ready")
        qk_ready, qkT_psum, qkT_ready = signal("qk_ready"), signal("qkT_psum"), signal("qkT_ready")
        s_ready, p_shifted, p_exp = signal("e_s_ready"), signal("e_p_shifted"), signal("e_p_exp")
        pT_psum, pT_ready, o_psum = signal("e_pT_psum"), signal("e_pT_ready"), signal("e_o_psum")
        o_ready, oT_psum, oT_ready, y_ready = signal("e_o_ready"), signal("e_oT_psum"), signal("e_oT_ready"), signal("e_y")
        zg_loaded = [signal(f"zg_loaded{st}") for st in STREAMS]
        zg_stored = [signal(f"zg_stored{st}") for st in STREAMS]
        ag_ready, gelu_ready, u_ready, fy_ready = signal("ag_ready"), signal("gelu_ready"), signal("fu_ready"), signal("f_y")

        with nc.Block() as block:

            @block.sync
            def _(sp):
                for dst, src in ((mask32[:, :, :], A["c_mask2"]), (cos0[:, :, :, :], A["c_cos"]), (sin0[:, :, :, :], A["c_sin"])):
                    sp.dma_start(dst, src).then_inc(consts.sem, 16)
                sp.wait_ge(consts.sem, 48)

            @block.gpsimd
            def _(pool):
                pool.memset(kT[:, :, :, :], 0.0)
                pool.memset(vb[:, :, :, :, :, :], 0.0)
                pool.memset(tiny[:, :], 1e-24)
                pool.memset(kzero[:, :, :], 0.0)

            @block.vector
            def _(dve):
                dve.memset(va[:, :, :, :], 1.0)
                dve.wait_ge(consts.sem, 48)
                dve.tensor_copy(mask[:, 0, :], mask32[:, 0, :])
                dve.tensor_copy(mask[:, 1:TB, :], bc(mask32[:, 1, :], 1, TB - 1))

        KA = B * (1 + 2 * HALVES)
        KF = 1 + 2
        KDL = KA * TB + KF * B
        KPL = 2 * B
        with nc.Fori(0, DEPTH) as L:
            r0 = (UA + UF) * L
            def unit(t, b):
                return B * t + b

            def off(t, b, n):
                t, b = t + (b + n) // B, (b + n) % B
                return (t, b) if not isinstance(t, int) or 0 <= t < TB else None

            def off_half(t, b, h, n):
                at = off(t, b, (h + n) // HALVES)
                return at and at + ((h + n) % HALVES,)

            def first_tile(t):
                return isinstance(t, int) and t == 0

            def count(x):
                return UA * L + unit(*x) + 1 if len(x) == 2 else HALVES * (UA * L + unit(*x[:2])) + x[2] + 1

            def slots(t, units=range(B)):
                for b in units:
                    for h in range(HALVES):
                        yield t, b, h

            def turns(eng, slot):
                for where in slots(-1, range(1, B)):
                    slot(*where)
                for where in slots(0):
                    slot(*where)
                with eng.Fori(1, TB - 1) as t:
                    for where in slots(t):
                        slot(*where)
                for where in slots(TB - 1):
                    slot(*where)
                for where in slots(TB, range(3)):
                    slot(*where)

            SBANK, TBANK, OBANK, QBANK, VBANK = 0, 2, 4, 5, 7

            with nc.Block() as block:

                @block.sync
                def _(sp):
                    def load(t, b):
                        z, half = c.z_ffn[b], D // 2
                        sp.dma_start(zs[:, b, 0:half], z[bass.ds(1 + P * t, P), 0:half]).then_inc(zs_loaded[b].sem, 16)
                        sp.dma_start(zs[:, b, half:D], z[bass.ds(P * t, P), half:D]).then_inc(zs_loaded[b].sem, 16)

                    def store(t, b):
                        sp.wait_ge(resid.sem, resid.at(r0 + unit(t, b) + 1))
                        sp.dma_start(c.z_attn[b, bass.ds(1 + P * t, P), :], Z[:, TB * b + t, :]).then_inc(zs_stored[b].sem, 16)

                    def loads(t):
                        for b in range(B):
                            sp.wait_ge(zsT_psum.sem, zsT_psum.at(count((t - 1, b))))
                            load(t, b)

                    load(0, 0)
                    for dst, src in ((wqkv[:, :], A["e_wqkv"][L]), (qks[:, 0, :], A["e_qs"][L].partition_broadcast(P)),
                                     (qks[:, 1, :], A["e_ks"][L].partition_broadcast(P))):
                        sp.dma_start(dst, src).then_inc(qkv_loaded.sem, 16)
                    for b in range(1, B):
                        load(0, b)
                    for dst, src in ((wo[:, :, :], A["e_wo"][L]), (w1[:, :, :], A["e_w1"][L]), (w2[:, :, :], A["e_w2"][L]),
                                     (b1[:, :], A["e_b1"][L]), (b2[:, :], A["e_b2"][L].partition_broadcast(P)),
                                     (lnp[:, :], A["e_lnp"][L])):
                        sp.dma_start(dst, src).then_inc(w_loaded.sem, 16)
                    loads(1)
                    with sp.Fori(2, TB) as t:
                        loads(t)
                        for b in range(B):
                            store(t - 2, b)
                    for t in (TB - 2, TB - 1):
                        for b in range(B):
                            store(t, b)
                    for b in range(B):
                        sp.wait_ge(zs_stored[b].sem, 16 * TB * (L + 1))
                    sp.sem_inc(stage_stored.sem, 1)

                @block.gpsimd
                def _(pool):
                    def slot(t, b, h):
                        far = off(t, b, 2)
                        if h == 0 or not far:
                            return
                        u, par, half = count(far), far[1] % 2, DH2 // 2
                        pool.wait_ge(ss_ready.sem, ss_ready.at(u))
                        pool.tensor_tensor(rn[:, par, :], ss[:, par, :], c.neghalf[:, :], ALU.pow).then_inc(rn_ready.sem, 1)
                        if not first_tile(far[0]):
                            pool.wait_ge(s_ready.sem, s_ready.at(HALVES * (u - B)))
                            pool.tensor_tensor(kT[:, far[1], :, 0:W2], kT[:, far[1], :, P:KEYS2], kzero[:, :, :],
                                               ALU.add).then_inc(before_ready.sem, 1)
                        pool.wait_ge(qk_normed.sem, qk_normed.at(u))
                        pool.tensor_tensor(carrier[:, par:par + 1], tiny[:, 0:1], tiny[:, 0:1], ALU.add)
                        pool.tensor_tensor(rot[:, par, :, :, 0:half], qk[:, par, :, :, half:DH2],
                                           bc(sinl[:, far[0], :, 0:half], 2, H2), ALU.mult)
                        pool.tensor_tensor(rot[:, par, :, :, half:DH2], qk[:, par, :, :, 0:half],
                                           bc(sinl[:, far[0], :, half:DH2], 2, H2), ALU.mult).then_inc(rot_ready.sem, 1)

                    pool.wait_ge(tables_ready.sem, tables_ready.at(L + 1))
                    turns(pool, slot)

                @block.vector
                def _(dve):
                    steps = Steps(dve, c.dve_step, KDL * L)

                    def resid_sum(t, b):
                        dve.wait_ge(y_ready.sem, y_ready.at(count((t, b))))
                        z = Z[:, TB * b + t, :]
                        dve.tensor_tensor(z, z, c.PS[:, VBANK, 0:D], ALU.add).then_inc(resid.sem, 1)

                    def divide(t, b, h):
                        dve.wait_ge(o_psum.sem, o_psum.at(count((t, b, h))))
                        o = c.PS[:, OBANK, 0:4 * (DH2 + 1)].rearrange("p (r i e) -> p r i e", i=2, e=DH2 + 1)
                        steps(dve.reciprocal(rz[:, h, :].rearrange("p (r i) -> p r i", i=2), o[:, :, :, DH2]))
                        dve.tensor_tensor(on[:, b % 2, 4 * h:4 * h + 4, :].rearrange("p (i r) e -> p r i e", r=2),
                                          o[:, :, :, 0:DH2], bc(rz[:, h, :].rearrange("p (r i) -> p r i", i=2), 3, DH2),
                                          ALU.mult).then_inc(o_ready.sem, 1)

                    def shift(t, b, h):
                        k = count((t, b, h))
                        dve.wait_ge(s_ready.sem, s_ready.at(k))
                        s = c.PS[:, SBANK:SBANK + 2, 0:2 * KEYS2].rearrange("p b (j k) -> p b j k", k=KEYS2)
                        m = mx[:, h, :].rearrange("p (b j) -> p b j", j=2)
                        steps(dve.tensor_reduce(m, s, AX.X, ALU.max))
                        if off(t, b, -1):
                            dve.wait_ge(pT_psum.sem, pT_psum.at(k - HALVES))
                        for k0, k1 in ((0, W2), (W2, KEYS2)):
                            out = pm[:, h, 4 * k0:4 * k1].rearrange("p (b j k) -> p b j k", b=2, j=2)
                            last = dve.tensor_tensor(out, s[:, :, :, k0:k1], bc(m, 3, k1 - k0), ALU.subtract)
                        last.then_inc(p_shifted.sem, 1)

                    def square_sums(t, b):
                        par = b % 2
                        dve.wait_ge(sq_ready.sem, sq_ready.at(count((t, b))))
                        steps(dve.tensor_reduce(ss[:, par, :], sq[:, par, :, :].rearrange("p s (h e) -> p (s h) e", e=DH2),
                                                AX.X, ALU.add))
                        dve.tensor_tensor(ss[:, par, :], ss[:, par, :], tiny[:, :], ALU.max).then_inc(ss_ready.sem, 1)

                    def norm(t, b):
                        par = b % 2
                        dve.wait_ge(qk_taken.sem, qk_taken.at(count((t, b))))
                        dve.wait_ge(rn_ready.sem, rn_ready.at(count((t, b))))
                        x = qk[:, par, :, :, :].rearrange("p s h e -> p (s h) e")
                        dve.tensor_tensor(x, x, bc(rn[:, par, :], 2, DH2), ALU.mult).then_inc(qk_normed.sem, 1)

                    def by_cosine(t, b):
                        par = b % 2
                        dve.wait_ge(qk_normed.sem, qk_normed.at(count((t, b))))
                        dve.tensor_tensor(sq[:, par, :, :].rearrange("p s (h e) -> p s h e", e=DH2), qk[:, par, :, :, :],
                                          bc(cosl[:, t, :, :], 2, H2), ALU.mult).then_inc(cos_done.sem, 1)

                    def rotated(t, b):
                        u, par = count((t, b)), b % 2
                        dve.wait_ge(rot_ready.sem, rot_ready.at(u))
                        dve.wait_ge(cos_done.sem, cos_done.at(u))
                        dve.tensor_tensor(qk[:, par, :, :, :].rearrange("p s h e -> p (s h e)"),
                                          sq[:, par, :, :].rearrange("p s e -> p (s e)"),
                                          rot[:, par, :, :, :].rearrange("p s h e -> p (s h e)"), ALU.add)\
                           .then_inc(qk_ready.sem, 1)

                    def slot(t, b, h):
                        if h == 0 and off(t, b, -3):
                            resid_sum(*off(t, b, -3))
                        if off_half(t, b, h, -3):
                            divide(*off_half(t, b, h, -3))
                        if off(t, b, 0):
                            shift(t, b, h)
                        if h == 1 and off(t, b, 2):
                            norm(*off(t, b, 2))
                        if h == 0:
                            if off(t, b, 1):
                                rotated(*off(t, b, 1))
                            if off(t, b, 2):
                                square_sums(*off(t, b, 2))
                        elif off(t, b, 2):
                            by_cosine(*off(t, b, 2))

                    dve.wait_ge(qkv_loaded.sem, qkv_loaded.at(16 * 3 * (L + 1)))
                    half = DH2 // 2
                    dve.tensor_tensor(cosl[:, :, :, :], cos0[:, :, :, :], bc(qks[:, :, :], 1, TB), ALU.mult)
                    dve.tensor_tensor(sinl[:, :, :, 0:half], sin0[:, :, :, 0:half], bc(qks[:, :, half:], 1, TB), ALU.mult)
                    dve.tensor_tensor(sinl[:, :, :, half:], sin0[:, :, :, half:], bc(qks[:, :, 0:half], 1, TB),
                                      ALU.mult).then_inc(tables_ready.sem, 1)
                    dve.wait_ge(tables_ready.sem, tables_ready.at(L + 1))
                    for where in slots(-1, range(1, B)):
                        slot(*where)
                    for where in slots(0):
                        slot(*where)
                    first = steps.k
                    with dve.Fori(1, TB - 1) as t:
                        steps.k = first + KA * (t - 1)
                        for where in slots(t):
                            slot(*where)
                    steps.k = first + KA * (TB - 2)
                    for where in slots(TB - 1):
                        slot(*where)
                    for where in slots(TB, range(3)):
                        slot(*where)
                    assert steps.k == KA * TB

                @block.scalar
                def _(act):
                    def features(t, b):
                        u = count((t, b))
                        act.wait_ge(zsT_psum.sem, zsT_psum.at(u))
                        act.activation(c.hT[:, b % 2, 0:P], c.PS[:, QBANK, 0:P], ACT.Copy).then_inc(eh_ready.sem, 1)

                    def values_before(t, b):
                        if not first_tile(t):
                            act.wait_ge(o_psum.sem, o_psum.at(count(off(t, b, -B) + (HALVES - 1,))))
                            for i in range(2):
                                own = va[W2:P, b, :, :].rearrange("p (h i r) e -> p h r i e", i=2, r=2)[:, :, :, i, :]
                                last = act.activation(vb[W2 * i:W2 * i + W2, b, :, :, i, :], own, ACT.Copy)
                            last.then_inc(c.act_step.sem, 1)

                    def squares(t, b):
                        act.wait_ge(eqkv_ready.sem, eqkv_ready.at(count((t, b))))
                        act.activation(sq[:, b % 2, :, :], c.PS[:, QBANK:QBANK + 2, :], ACT.Square).then_inc(sq_ready.sem, 1)
                        act.activation(qk[:, b % 2, :, :, :].rearrange("p s h e -> p s (h e)"), c.PS[:, QBANK:QBANK + 2, :],
                                       ACT.Copy).then_inc(qk_taken.sem, 1)

                    def values(t, b):
                        if not first_tile(t):
                            act.wait_ge(c.act_step.sem, c.act_step.at((UA - B) * L + unit(t, b) - B + 1))
                        act.activation(va[:, b, :, 0:DH2], c.PS[:, VBANK, :].rearrange("p (h e) -> p h e", e=DH2),
                                       ACT.Copy).then_inc(v_evac.sem, 1)

                    def take_qk(t, b):
                        act.wait_ge(qkT_psum.sem, qkT_psum.at(count((t, b))))
                        act.activation(qT[:, b % 2, :, :].rearrange("p j q -> p (j q)"), c.PS[:, QBANK, :], ACT.Copy)
                        if not first_tile(t):
                            act.wait_ge(before_ready.sem, before_ready.at((UA - B) * L + unit(t, b) - B + 1))
                        act.activation(kT[:, b, :, W2:KEYS2], c.PS[:, QBANK + 1, :].rearrange("p (j q) -> p j q", q=P),
                                       ACT.Copy).then_inc(qkT_ready.sem, 1)

                    def take_o(t, b):
                        act.wait_ge(oT_psum.sem, oT_psum.at(count((t, b))))
                        act.activation(oT[:, b % 2, :, :].rearrange("p j q -> p (j q)"), c.PS[:, VBANK, :],
                                       ACT.Copy).then_inc(oT_ready.sem, 1)

                    def exponent(t, b, h):
                        act.wait_ge(p_shifted.sem, p_shifted.at(count((t, b, h))))
                        act.activation(pm[:, h, :], pm[:, h, :], ACT.Exp).then_inc(p_exp.sem, 1)

                    def take_p(t, b, h):
                        act.wait_ge(pT_psum.sem, pT_psum.at(count((t, b, h))))
                        act.activation(pa[:, h, :, :].rearrange("p j q -> p (j q)"), c.PS[:, TBANK, :], ACT.Copy)
                        act.activation(pb[:, h, :, :].rearrange("p r q -> p (r q)"), c.PS[:, TBANK + 1, 0:2 * P], ACT.Copy)\
                           .then_inc(pT_ready.sem, 1)

                    def slot(t, b, h):
                        ahead, back = off(t, b, 2), off_half(t, b, h, -1)
                        if h == 0:
                            if ahead:
                                features(*ahead)
                                values_before(*ahead)
                            if off(t, b, 0):
                                exponent(t, b, h)
                            if ahead:
                                squares(*ahead)
                        else:
                            if off(t, b, -2):
                                take_o(*off(t, b, -2))
                            if off(t, b, 1):
                                take_qk(*off(t, b, 1))
                            if off(t, b, 0):
                                exponent(t, b, h)
                        if h == 0 and ahead:
                            values(*ahead)
                        if back:
                            take_p(*back)

                    turns(act, slot)

                @block.tensor
                def _(pe):
                    def turn_z(t, b):
                        before = off(t, b, -2)
                        if before:
                            pe.wait_ge(qkT_ready.sem, qkT_ready.at(count(before)))
                        elif off(t, b, -1):
                            pe.wait_ge(qk_taken.sem, qk_taken.at(count(off(t, b, -1))))
                        pe.wait_ge(zs_loaded[b].sem, zs_loaded[b].at(32 * (TB * L + t) + 32))
                        pe.transpose(c.PS[:, QBANK, 0:P], zs[:, b, :], ident[:, :]).then_inc(zsT_psum.sem, 1)

                    def project(t, b):
                        pe.wait_ge(eh_ready.sem, eh_ready.at(count((t, b))))
                        if first_tile(t) and b == 0:
                            pe.wait_ge(qkv_loaded.sem, qkv_loaded.at(16 * 3 * (L + 1)))
                        for s in range(3):
                            if s == 2 and off(t, b, -5):
                                pe.wait_ge(resid.sem, resid.at(r0 + unit(*off(t, b, -5)) + 1))
                            last = pe.matmul(c.PS[:, QBANK + s, :], c.hT[:, b % 2, 0:P], wqkv[:, s * INNER:(s + 1) * INNER],
                                             start=True, stop=True)
                        last.then_inc(eqkv_ready.sem, 1)

                    def turn_qk(t, b):
                        pe.wait_ge(qk_ready.sem, qk_ready.at(count((t, b))))
                        if off(t, b, 1):
                            pe.wait_ge(qk_taken.sem, qk_taken.at(count(off(t, b, 1))))
                        for s in range(2):
                            for j in range(4):
                                last = pe.transpose(c.PS[:, QBANK + s, j * P:(j + 1) * P],
                                                    qk[:, b % 2, s, 2 * j:2 * j + 2, :].rearrange("p h e -> p (h e)"), ident[:, :])
                        last.then_inc(qkT_psum.sem, 1)

                    def scores(t, b, h):
                        back = off_half(t, b, h, -1)
                        if back:
                            pe.wait_ge(p_shifted.sem, p_shifted.at(count(back)))
                        if h == 0:
                            pe.wait_ge(qkT_ready.sem, qkT_ready.at(count((t, b))))
                        s = [c.PS[:, SBANK + r, 0:2 * KEYS2].rearrange("p (j k) -> p j k", k=KEYS2) for r in range(2)]
                        for r in range(2):
                            pe.matmul(s[r], identb[:, :], bc(mask[:, t, :], 1, 2), start=True, stop=False)
                        for j in range(2):
                            for r in range(2):
                                rows = slice(64 * r, 64 * r + 64)
                                last = pe.matmul(s[r][:, j, :], qT[rows, b % 2, 2 * h + j, :], kT[rows, b, 2 * h + j, :],
                                                 start=False, stop=(j == 1))
                        last.then_inc(s_ready.sem, 1)

                    def turn_p(t, b, h):
                        pe.wait_ge(p_exp.sem, p_exp.at(count((t, b, h))))
                        back = off_half(t, b, h, -1)
                        if back:
                            pe.wait_ge(pT_ready.sem, pT_ready.at(count(back)))
                        for j in range(4):
                            pe.transpose(c.PS[:, TBANK, j * P:(j + 1) * P], pm[:, h, 4 * W2 + j * P:4 * W2 + (j + 1) * P], ident[:, :])
                        for r in range(2):
                            last = pe.transpose(c.PS[:, TBANK + 1, r * P:(r + 1) * P], pm[:, h, r * P:(r + 1) * P], ident[:, :])
                        last.then_inc(pT_psum.sem, 1)

                    def weigh(t, b, h):
                        pe.wait_ge(pT_ready.sem, pT_ready.at(count((t, b, h))))
                        back = off_half(t, b, h, -1)
                        if back:
                            pe.wait_ge(o_ready.sem, o_ready.at(count(back)))
                        for r in range(2):
                            o = c.PS[:, OBANK, 2 * r * (DH2 + 1):2 * (r + 1) * (DH2 + 1)]
                            last = pe.matmul(o, pb[:, h, r, :], vb[:, b, h, r, :, :].rearrange("p i e -> p (i e)"),
                                             start=True, stop=False)
                            for i in range(2):
                                last = pe.matmul(o[:, i * (DH2 + 1):(i + 1) * (DH2 + 1)], pa[:, h, 2 * r + i, :],
                                                 va[:, b, 4 * h + 2 * i + r, :], start=False, stop=(i == 1))
                        last.then_inc(o_psum.sem, 1)

                    def turn_o(t, b):
                        pe.wait_ge(o_ready.sem, o_ready.at(count((t, b, HALVES - 1))))
                        if off(t, b, 4):
                            pe.wait_ge(v_evac.sem, v_evac.at(count(off(t, b, 4))))
                        if off(t, b, -1):
                            pe.wait_ge(resid.sem, resid.at(r0 + unit(*off(t, b, -1)) + 1))
                        for j in range(4):
                            last = pe.transpose(c.PS[:, VBANK, j * P:(j + 1) * P],
                                                on[:, b % 2, 2 * j:2 * j + 2, :].rearrange("p h e -> p (h e)"), ident[:, :])
                        last.then_inc(oT_psum.sem, 1)

                    def project_o(t, b):
                        pe.wait_ge(oT_ready.sem, oT_ready.at(count((t, b))))
                        if first_tile(t) and b == 0:
                            pe.wait_ge(w_loaded.sem, w_loaded.at(16 * 6 * (L + 1)))
                        for j in range(4):
                            last = pe.matmul(c.PS[:, VBANK, 0:D], oT[:, b % 2, j, :], wo[:, j, :], start=(j == 0), stop=(j == 3))
                        last.then_inc(y_ready.sem, 1)

                    def slot(t, b, h):
                        if off(t, b, 0):
                            scores(t, b, h)
                        if h == 0 and off(t, b, 2):
                            project(*off(t, b, 2))
                        if h == 1 and off(t, b, -2):
                            turn_o(*off(t, b, -2))
                        if h == 1 and off(t, b, 1):
                            turn_qk(*off(t, b, 1))
                        if off_half(t, b, h, -1):
                            turn_p(*off_half(t, b, h, -1))
                        if off_half(t, b, h, -2):
                            weigh(*off_half(t, b, h, -2))
                        if h == 1 and off(t, b, -2):
                            project_o(*off(t, b, -2))
                        if h == 1 and off(t, b, 3):
                            turn_z(*off(t, b, 3))

                    turns(pe, slot)

            with nc.Block() as block:

                @block.sync
                def _(sp):
                    def load(n, st):
                        z, half = c.z_attn[n], D // 2
                        for d0, before in ((0, 1), (half, 0)):
                            src = z[bass.ds(before + GT * st, GT), d0:d0 + half].rearrange("(t p) d -> p t d", p=P)
                            sp.dma_start(zg[:, st, :, d0:d0 + half], src).then_inc(zg_loaded[st].sem, 16)

                    def store(n, st):
                        sp.wait_ge(resid.sem, resid.at(r0 + UA + 2 * n + st + 1))
                        sp.dma_start(c.z_ffn[n, bass.ds(1 + GT * st, GT), :].rearrange("(t p) d -> p t d", p=P),
                                     Z[:, bass.ds(TB * n + G4 * st, G4), :]).then_inc(zg_stored[st].sem, 16)

                    def loads(n):
                        for st in STREAMS:
                            sp.wait_ge(c.xn_ready.sem, c.xn_ready.at(UF * L + 2 * n + st - 1))
                            load(n, st)

                    def stores(n):
                        for st in STREAMS:
                            store(n, st)

                    for st in STREAMS:
                        load(0, st)
                    loads(1)
                    with sp.Fori(2, B) as n:
                        loads(n)
                        stores(n - 2)
                    stores(B - 2)
                    stores(B - 1)
                    for st in STREAMS:
                        sp.wait_ge(zg_stored[st].sem, 16 * B * (L + 1))
                    sp.sem_inc(stage_stored.sem, 1)

                @block.gpsimd
                def _(pool):
                    with pool.Fori(0, B) as n:
                        c.ln_rstd(pool, Chain(pool, c.pool_step, KPL * L + 2 * n), UF * L + 2 * n, G4)

                @block.vector
                def _(dve):
                    steps = Steps(dve, c.dve_step, KDL * L + KA * TB)

                    def tiles(n):
                        return [[zg[:, st, i, :] for i in range(G4)] for st in STREAMS]

                    def stats(n):
                        for st in STREAMS:
                            dve.wait_ge(zg_loaded[st].sem, zg_loaded[st].at(32 * (B * L + n) + 32))
                        c.ln_stats(dve, steps, tiles(n))

                    def apply(n):
                        c.ln_apply(dve, UF * L + 2 * n, tiles(n))

                    def turn(n, last=False):
                        u = UF * L + 2 * n
                        for j in range(HC):
                            for st in STREAMS:
                                dve.wait_ge(gelu_ready.sem, gelu_ready.at(HC * u + 2 * j + st + 1))
                                dve.scalar_tensor_tensor(uu[:, st, j, :], bank(st, 1), b1[:, j:j + 1], gate[:, st, :],
                                                         ALU.add, ALU.mult).then_inc(u_ready.sem, 1)
                            if j == 0 and not last:
                                stats(n + 1)
                            elif j == 1 and not last:
                                apply(n + 1)
                        for st in STREAMS:
                            dve.wait_ge(fy_ready.sem, fy_ready.at(u + st + 1))
                            z = Z[:, bass.ds(TB * n + G4 * st, G4), :]
                            steps(dve.tensor_tensor(z, z, bank(st, 3).rearrange("p (t d) -> p t d", d=D), ALU.add))
                            dve.tensor_tensor(z, z, bc(b2[:, :], 1, G4), ALU.add).then_inc(resid.sem, 1)

                    stats(0)
                    apply(0)
                    first = steps.k
                    with dve.Fori(0, B - 1) as n:
                        steps.k = first + KF * n
                        turn(n)
                    steps.k = first + KF * (B - 1)
                    turn(B - 1, last=True)
                    assert steps.k == KF * B

                @block.scalar
                def _(act):
                    def features(n):
                        for st in STREAMS:
                            act.wait_ge(c.xnT_ready.sem, c.xnT_ready.at(UF * L + 2 * n + st + 1))
                            act.activation(c.hT[:, st, :], bank(st, 0), ACT.Identity, scale=lnp[:, 1:2],
                                           bias=lnp[:, 0:1]).then_inc(c.hT_ready.sem, 1)

                    def gates(n):
                        for j in range(HC):
                            for st in STREAMS:
                                act.wait_ge(ag_ready.sem, ag_ready.at(HC * (UF * L + 2 * n) + 2 * j + st + 1))
                                act.activation(gate[:, st, :], bank(st, 2), ACT.Gelu, bias=b1[:, HC + j:HC + j + 1])\
                                   .then_inc(gelu_ready.sem, 1)

                    features(0)
                    with act.Fori(0, B - 1) as n:
                        gates(n)
                        features(n + 1)
                    gates(B - 1)

                @block.tensor
                def _(pe):
                    def turn(n, last=False):
                        u = UF * L + 2 * n
                        for j in range(HC):
                            for st in STREAMS:
                                if j == 0:
                                    pe.wait_ge(c.hT_ready.sem, c.hT_ready.at(u + st + 1))
                                else:
                                    pe.wait_ge(u_ready.sem, u_ready.at(HC * u + 2 * (j - 1) + st + 1))
                                pe.matmul(bank(st, 1), w1[:, j, :], c.hT[:, st, :], start=True, stop=True)
                                pe.matmul(bank(st, 2), w1[:, HC + j, :], c.hT[:, st, :], start=True, stop=True)\
                                  .then_inc(ag_ready.sem, 1)
                            if j == 1 and not last:
                                c.ln_transpose(pe, u + 2, G4)
                        for st in STREAMS:
                            pe.wait_ge(u_ready.sem, u_ready.at(HC * u + 2 * (HC - 1) + st + 1))
                            if not isinstance(n, int) or n:
                                pe.wait_ge(resid.sem, resid.at(r0 + UA + 2 * n + st - 1))
                            for i in range(G4):
                                for j in range(HC):
                                    mm = pe.matmul(bank(st, 3)[:, i * P:(i + 1) * P], uu[:, st, j, i * P:(i + 1) * P], w2[:, j, :],
                                                   start=(j == 0), stop=(j == HC - 1))
                            mm.then_inc(fy_ready.sem, 1)

                    c.ln_transpose(pe, UF * L, G4)
                    turn(0)
                    with pe.Fori(1, B - 1) as n:
                        turn(n)
                    turn(B - 1, last=True)
        c.ln_advance(UF * DEPTH)
        resid.base += DEPTH * (UA + UF)


def finish(c, Z, out):
    nc, X = c.nc, c.X
    gated, summed, stored = c.counter("gated"), c.counter("summed"), c.counter("stored")

    def batch(t, b):
        return t[:, TB * b:TB * (b + 1), :]

    with nc.Block() as block:

        @block.vector
        def _(dve):
            for b in range(B):
                dve.tensor_tensor(batch(Z, b), batch(Z, b), bc(c.rowB[:, c.L1GB, b, :], 1, TB), ALU.mult).then_inc(gated.sem, 1)
                dve.wait_ge(gated.sem, b + 1)
                dve.tensor_tensor(batch(X, b), batch(X, b), batch(Z, b), ALU.add).then_inc(summed.sem, 1)

        @block.sync
        def _(sp):
            for b in range(B):
                sp.wait_ge(summed.sem, b + 1)
                sp.dma_start(out[b].rearrange("(t p) d -> p t d", p=P), batch(X, b)).then_inc(stored.sem, 16)
            sp.wait_ge(stored.sem, 16 * B)


def build(nc, A, out):
    with ExitStack() as ctx:
        c = Core(nc, ctx)
        setup(c, A)
        linear_attention(c, A)
        moe(c, A)
        Z = c.sb("Z", [P, NT, D])
        windowed_attention(c, A, Z)
        local_transformer(c, A, Z)
        finish(c, Z, out)


KDA = 26


def constants():
    c = {"c_ident": np.eye(P, dtype=np.float32)}
    h = np.arange(P) // DH0
    c["c_bmask"] = ((h[:, None] == h[None, :]) * S0).astype(np.float32)
    row, col = np.arange(3 * E) % E, np.arange(NJ * P) // INTER
    c["c_sel"] = (row[:, None] == col[None, :]).astype(np.float32).reshape(3 * E, NJ, P)
    c["c_hmask"] = (np.arange(P)[:, None] // DH1 % 4 == np.arange(4)[None, :]).astype(np.float32)
    q, k = np.arange(P)[:, None], np.arange(P)[None, :]
    before, pre = np.arange(W1)[None, :] - W1, np.arange(PRE)[None, :] + 0 * q
    own = (k <= q) & (q - k < W1)
    first = np.concatenate([before + 0 * q > 0, pre < 0, own | ((k <= q) & (k < PRE))], 1)
    other = np.concatenate([q - before < W1, pre >= 0, own], 1)
    own2 = (k <= q) & (q - k <= W2)
    before2 = np.arange(W2)[None, :] - W2
    first2, other2 = np.concatenate([before2 + 0 * q > 0, own2], 1), np.concatenate([q - before2 <= W2, own2], 1)
    c["c_mask2"] = np.where(np.stack([first2, other2], 1), 0.0, NEG).astype(np.float32)
    f = np.float32
    idx = np.arange(0, DH2, 2, dtype=f)
    inv_freq = f(1.0) / f(10000.0) ** (idx / f(DH2))
    pos = np.arange(S, dtype=f)
    freqs = pos[:, None] * inv_freq[None, :]
    base = (idx + f(0.4 * DH2)) / f(1.4 * DH2)
    xpos = base[None, :] ** ((pos - f(S // 2)) / f(W2 // 2))[:, None]
    cos, sin = np.cos(freqs), np.sin(freqs)
    cos, sin = np.concatenate([cos, cos], 1), np.concatenate([-sin, sin], 1)
    xpos = np.concatenate([xpos, xpos], 1)
    for name, tab in (("c_cos", cos), ("c_sin", sin)):
        both = np.stack([f(8.0) * tab * xpos, tab / xpos], 1).astype(f)
        c[name] = both.reshape(TB, P, 2, DH2).transpose(1, 0, 2, 3)
    c["c_mask1"] = np.where(np.stack([first, other], 1), 0.0, NEG).astype(np.float32)
    return c


def moe_layout(i):
    none = np.zeros((P - INTER, D), np.float32)
    up = lambda w, ws: np.concatenate([w.reshape(E * INTER, D), ws, none], 0).T
    down = np.concatenate([i["L0_ffn_w2"].transpose(0, 2, 1).reshape(E * INTER, D), i["L0_ffn_ws2"].T, none], 0)
    return {"gwT": i["L0_ffn_gate_w"].T, "L0_ffn_gate_bias": i["L0_ffn_gate_bias"],
            "w1T": up(i["L0_ffn_w1"], i["L0_ffn_ws1"]), "w3T": up(i["L0_ffn_w3"], i["L0_ffn_ws3"]),
            "w2T": down.reshape(NJ + 1, P, D).transpose(1, 0, 2)}


def local_layout(i):
    n = HC * P - HID

    def halves(w):
        w = w.reshape(w.shape[:-1] + (2, HID))
        w = np.pad(w, [(0, 0)] * (w.ndim - 1) + [(0, n)])
        return w.reshape(w.shape[:-2] + (2 * HC, P))

    w2 = np.pad(i["L1_ffn_w2"], [(0, 0), (0, n), (0, 0)])
    return {"e_wqkv": i["L1_ffn_wqkv"],
            "e_wo": i["L1_ffn_wo"].reshape(DEPTH, INNER // P, P, D).transpose(0, 2, 1, 3),
            "e_w1": halves(i["L1_ffn_w1"]), "e_b1": halves(i["L1_ffn_b1"]).transpose(0, 2, 1),
            "e_w2": w2.reshape(DEPTH, HC, P, D).transpose(0, 2, 1, 3), "e_b2": i["L1_ffn_b2"],
            "e_lnp": np.stack([i["L1_ffn_ln_b"], i["L1_ffn_ln_g"]], -1),
            "e_qs": i["L1_ffn_q_scale"], "e_ks": i["L1_ffn_k_scale"]}


def layout(i):
    a = {"L0_attn_x": i["L0_attn_x"], "L0_wmod": i["L0_wmod"], "L1_wmod": i["L1_wmod"],
         "L0_cT": i["L0_c"].T, "L1_cT": i["L1_c"].T,
         "a_wqv": np.concatenate([i["L0_attn_Wq"], i["L0_attn_Wv"]], 1),
         "a_bqv": np.concatenate([i["L0_attn_bq"], i["L0_attn_bv"]]),
         "L0_attn_Wo": i["L0_attn_Wo"], "L0_attn_bo": i["L0_attn_bo"]}
    a.update(moe_layout(i))
    a.update(local_layout(i))
    a.update({"d_wqkvT": i["L1_attn_w_qkv"].T, "d_woutT": i["L1_attn_w_out"].T})
    return a


def kernel(**inputs):
    import concourse.bacc as bacc
    from concourse.bass_utils import run_bass_kernel_spmd

    nc = bacc.Bacc("TRN2", target_bir_lowering=False, num_devices=1)
    arrays, args = {}, {}
    host = {k: np.asarray(v) for k, v in inputs.items()}
    for name, a in {**layout(host), **constants()}.items():
        arrays[f"in_{name}"] = a = np.ascontiguousarray(a)
        args[name] = nc.dram_tensor(f"in_{name}", a.shape, mybir.dt.from_np(a.dtype), kind="ExternalInput").ap()
    out = nc.dram_tensor("out_x", (B, S, D), F32, kind="ExternalOutput").ap()
    build(nc, args, out)
    r = run_bass_kernel_spmd(nc, [arrays], core_ids=[0])
    return r.results[0]["out_x"]
```
